# Optimizing a Trainium2 kernel written in Bass

```python
import numpy as np
import jax
import jax.numpy as jnp

def _softmax(x, axis=-1):
    return jax.nn.softmax(x, axis=axis)

def _gelu(x):
    return jax.nn.gelu(x, approximate=True)

def _silu(x):
    return jax.nn.silu(x)

def _sigmoid(x):
    return jax.nn.sigmoid(x)

def _layernorm(x, axis=-1, eps=1e-05):
    m = jnp.mean(x, axis=axis, keepdims=True)
    v = jnp.var(x, axis=axis, keepdims=True)
    return (x - m) / jnp.sqrt(v + eps)

def _scatter_add(tgt, idx, src, axis=0):
    return tgt.at[idx].add(src)

def _segment_sum(src, seg, n):
    return jax.ops.segment_sum(src, seg, n)
kernel_name = 'mk_perceiver_d2_seqx_r8_da69f1'

def setup_inputs(seed: int=0):
    np.random.seed(seed)
    _w = jnp.asarray

    def _rec_inputs():
        import jax
        import jax.numpy as jnp
        _rk = jax.random.key(seed)
        x = -0.0002928 + 1 * jax.random.normal(jax.random.fold_in(_rk, 1), (2, 128, 128), jnp.float32)
        _lenS = 128 - jax.random.randint(jax.random.fold_in(_rk, 7), (2,), 0, max(1, 128 // 4) + 1, jnp.int32)
        _lenS2 = 2048 - jax.random.randint(jax.random.fold_in(_rk, 8), (2,), 0, max(1, 2048 // 4) + 1, jnp.int32)
        _ctx_1024P = jax.random.normal(jax.random.fold_in(_rk, 11), (2, 16, 128), jnp.float32)
        _ctx_1024c = jax.random.dirichlet(jax.random.fold_in(_rk, 511), 0.3 * jnp.ones((16,), jnp.float32), (2, 2048))
        _ctx_1024t = jnp.einsum('bsk,bkd->bsd', _ctx_1024c, _ctx_1024P)
        _ctx_1024t = _ctx_1024t * jax.lax.rsqrt(jnp.mean(jnp.square(_ctx_1024t)) + 1e-12) * 0.953939
        ctx_1024 = -1.39393e-06 + 0.999914 * (_ctx_1024t + 0.3 * jax.random.normal(jax.random.fold_in(_rk, 611), (2, 2048, 128), jnp.float32))
        _validS = jnp.arange(128)[None, :] < _lenS[:, None]
        _validS2 = jnp.arange(2048)[None, :] < _lenS2[:, None]
        _causal = jnp.tril(jnp.ones((128, 128), dtype=bool))
        mask_Bx1xSxS2_ff0 = jnp.where(jnp.ones((2, 1, 128, 2048), dtype=bool), 0.0, -1000000000.0).astype(jnp.float32)
        return (x, ctx_1024, mask_Bx1xSxS2_ff0)
    x, ctx_1024, mask_Bx1xSxS2_ff0 = _rec_inputs()

    def _L0_xattn_setup():
        import jax, jax.numpy as jnp
        import numpy as np
        HIDDEN = 128
        NUM_HEADS = 16
        HEAD_DIM = HIDDEN // NUM_HEADS
        B, F, T = (2, 256, 256)
        key = jax.random.key(seed)
        ks = jax.random.split(key, 6)
        return {'query_input': jax.random.normal(ks[0], (B, F, HIDDEN), dtype=jnp.float32), 'source_input': jax.random.normal(ks[1], (B, T, HIDDEN), dtype=jnp.float32), 'bias': jnp.zeros((B, 1, F, T), dtype=jnp.float32), 'wq': jax.random.normal(ks[2], (HIDDEN, NUM_HEADS, HEAD_DIM), dtype=jnp.float32) * (1.0 / np.sqrt(HIDDEN)), 'wk': jax.random.normal(ks[3], (HIDDEN, NUM_HEADS, HEAD_DIM), dtype=jnp.float32) * (1.0 / np.sqrt(HIDDEN)), 'wv': jax.random.normal(ks[4], (HIDDEN, NUM_HEADS, HEAD_DIM), dtype=jnp.float32) * (1.0 / np.sqrt(HIDDEN)), 'wo': jax.random.normal(ks[5], (NUM_HEADS, HEAD_DIM, HIDDEN), dtype=jnp.float32) * (1.0 / np.sqrt(HIDDEN))}
    _L0_xattn_all = _L0_xattn_setup()
    _L0_xattn_in = {k: v for k, v in _L0_xattn_all.items() if k in ('wq', 'wk', 'wv', 'wo')}
    del _L0_xattn_all

    def _L0_attn_setup():
        import jax, jax.numpy as jnp
        import numpy as np
        from math import sqrt
        N_HEAD = 16
        W_SCALE = 0.02

        def _reference_tuple_inner(x, W_dq, W_uq, W_dkv, W_uk, W_uv, W_o):
            B, T, C = x.shape
            nh = N_HEAD
            hs = C // nh
            n_kvl = W_dkv.shape[0]
            k_eff = (W_dq.T @ W_uq.T @ W_uk).reshape(nh, hs, n_kvl)
            v_eff = jnp.transpose((W_uv.T @ W_o.T).reshape(n_kvl, nh, hs), (1, 0, 2))
            c_kv = x @ W_dkv.T
            q = x @ W_dq.T @ W_uq.T
            q = q.reshape(B, T, nh, hs)
            q_lat = jnp.einsum('bqhd,hdl->bhql', q, k_eff)
            attn = jnp.einsum('bhql,bkl->bhqk', q_lat, c_kv) / sqrt(hs)
            causal = jnp.tril(jnp.ones((T, T), dtype=bool))
            attn = jnp.where(causal[None, None], attn, -jnp.inf)
            attn = jax.nn.softmax(attn, axis=-1)
            y_lat = jnp.einsum('bhqk,bkl->bhql', attn, c_kv)
            y = jnp.einsum('bhql,hld->bqhd', y_lat, v_eff).reshape(B, T, C)
            return (y, c_kv)
        key = jax.random.key(seed)
        ks = jax.random.split(key, 7)
        B, T, C = (2, 256, 128)
        QL, KVL = (64, 64)
        return {'x': jax.random.normal(ks[0], (B, T, C), dtype=jnp.float32), 'W_dq': jax.random.normal(ks[1], (QL, C), dtype=jnp.float32) * W_SCALE, 'W_uq': jax.random.normal(ks[2], (C, QL), dtype=jnp.float32) * W_SCALE, 'W_dkv': jax.random.normal(ks[3], (KVL, C), dtype=jnp.float32) * W_SCALE, 'W_uk': jax.random.normal(ks[4], (C, KVL), dtype=jnp.float32) * W_SCALE, 'W_uv': jax.random.normal(ks[5], (C, KVL), dtype=jnp.float32) * W_SCALE, 'W_o': jax.random.normal(ks[6], (C, C), dtype=jnp.float32) * W_SCALE}
    _L0_attn_all = _L0_attn_setup()
    _L0_attn_in = {k: v for k, v in _L0_attn_all.items() if k in ('W_dq', 'W_uq', 'W_dkv', 'W_uk', 'W_uv', 'W_o')}
    del _L0_attn_all

    def _L0_ffn_setup():
        import jax, jax.numpy as jnp
        import numpy as np
        NUM_OPS, B, T, D = (8, 8, 64, 128)
        key = jax.random.key(seed)
        k1, k2, k3, k4 = jax.random.split(key, 4)
        x = jax.random.normal(k1, (B, T, D), dtype=jnp.float32)
        W = jax.random.normal(k2, (NUM_OPS, D, D), dtype=jnp.float32) * 0.02
        b = jnp.zeros((NUM_OPS, D), dtype=jnp.float32)
        logits = 0.001 * jax.random.normal(k3, (NUM_OPS,), dtype=jnp.float32)
        u = jax.random.uniform(k4, (NUM_OPS,), dtype=jnp.float32, minval=1e-06, maxval=1.0 - 1e-06)
        return {'x': x, 'W': W, 'b': b, 'logits': logits, 'u': u}
    _L0_ffn_all = _L0_ffn_setup()
    _L0_ffn_in = {k: v for k, v in _L0_ffn_all.items() if k in ('W', 'b', 'logits', 'u')}
    del _L0_ffn_all

    def _L1_xattn_setup():
        import jax, jax.numpy as jnp
        import numpy as np
        DIM = 128
        NUM_HEADS = 16
        HEAD_DIM = DIM // NUM_HEADS
        SCALE = HEAD_DIM ** (-0.5)
        key = jax.random.key(seed)
        ks = jax.random.split(key, 8)
        B, QL, KL = (2, 256, 256)
        s = DIM ** (-0.5)
        return {'q': jax.random.normal(ks[0], (B, QL, DIM), jnp.float32), 'k': jax.random.normal(ks[1], (B, KL, DIM), jnp.float32), 'v': jax.random.normal(ks[2], (B, KL, DIM), jnp.float32), 'Wq': jax.random.normal(ks[3], (DIM, DIM), jnp.float32) * s, 'Wk': jax.random.normal(ks[4], (DIM, DIM), jnp.float32) * s, 'Wv': jax.random.normal(ks[5], (DIM, DIM), jnp.float32) * s, 'Wo': jax.random.normal(ks[6], (DIM, DIM), jnp.float32) * s, 'bo': jax.random.normal(ks[7], (DIM,), jnp.float32) * 0.02}
    _L1_xattn_all = _L1_xattn_setup()
    _L1_xattn_in = {k: v for k, v in _L1_xattn_all.items() if k in ('Wq', 'Wk', 'Wv', 'Wo', 'bo')}
    del _L1_xattn_all

    def _L1_attn_setup():
        import jax, jax.numpy as jnp
        import numpy as np
        import math
        HIDDEN = 128
        HEADS = 16
        HEAD = HIDDEN // HEADS
        B, N = (2, 256)
        NEG_INF = -10000.0
        key = jax.random.key(seed)
        k1, k2, k3, k4, k5 = jax.random.split(key, 5)
        s = 1.0 / math.sqrt(HIDDEN)
        return {'encodings': jax.random.normal(k1, (B, N, HIDDEN), dtype=jnp.float32), 'attn_w': jax.random.uniform(k2, (3 * HIDDEN, HIDDEN), minval=-s, maxval=s, dtype=jnp.float32), 'attn_b': jax.random.uniform(k3, (3 * HIDDEN,), minval=-s, maxval=s, dtype=jnp.float32), 'out_w': jax.random.uniform(k4, (HIDDEN, HIDDEN), minval=-s, maxval=s, dtype=jnp.float32), 'out_b': jax.random.uniform(k5, (HIDDEN,), minval=-s, maxval=s, dtype=jnp.float32)}
    _L1_attn_all = _L1_attn_setup()
    _L1_attn_in = {k: v for k, v in _L1_attn_all.items() if k in ('attn_w', 'attn_b', 'out_w', 'out_b')}
    del _L1_attn_all

    def _L1_ffn_setup():
        import jax, jax.numpy as jnp
        import numpy as np
        B, S, H = (1, 256, 128)
        E, K = (16, 4)
        G, TG = (4, 2)
        I_MOE = 64
        N_SH = 2
        SCALE = 2.5

        def _mlp(x, gw, uw, dw):
            return jax.nn.silu(x @ gw.T) * (x @ uw.T) @ dw.T

        def _route(x2d, router_weight, e_bias):
            T = x2d.shape[0]
            scores = jax.nn.sigmoid(x2d @ router_weight.T)
            sc = scores + e_bias[None, :]
            group_scores = jnp.sum(jax.lax.top_k(sc.reshape(T, G, E // G), 2)[0], axis=-1)
            _, gidx = jax.lax.top_k(group_scores, TG)
            gmask = jnp.zeros((T, G), sc.dtype).at[jnp.arange(T)[:, None], gidx].set(1.0)
            smask = jnp.repeat(gmask, E // G, axis=1)
            masked = jnp.where(smask > 0, sc, 0.0)
            _, tidx = jax.lax.top_k(masked, K)
            tw = jnp.take_along_axis(scores, tidx, axis=1)
            tw = tw / (jnp.sum(tw, axis=-1, keepdims=True) + 1e-20)
            tw = tw * SCALE
            return (tidx, tw)

        def _moe_forward(hidden_states, router_weight, e_bias, gate_w, up_w, down_w, sh_gate_w, sh_up_w, sh_down_w):
            orig_shape = hidden_states.shape
            x = hidden_states.reshape(-1, H)
            T = x.shape[0]
            tidx, tw = _route(x, router_weight, e_bias)
            g = jnp.einsum('th,eih->tei', x, gate_w)
            u = jnp.einsum('th,eih->tei', x, up_w)
            h = jax.nn.silu(g) * u
            yo = jnp.einsum('tei,ehi->teh', h, down_w)
            combine = jnp.zeros((T, E), tw.dtype).at[jnp.arange(T)[:, None], tidx].add(tw)
            routed = jnp.einsum('te,teh->th', combine, yo)
            shared = _mlp(hidden_states.reshape(-1, H), sh_gate_w, sh_up_w, sh_down_w)
            return (routed + shared).reshape(orig_shape)
        key = jax.random.key(seed)
        ks = jax.random.split(key, 9)
        s = 0.02
        return {'hidden_states': jax.random.normal(ks[0], (B, S, H), jnp.float32), 'router_weight': jax.random.normal(ks[1], (E, H), jnp.float32) * s, 'e_bias': jnp.zeros((E,), jnp.float32), 'gate_w': jax.random.normal(ks[2], (E, I_MOE, H), jnp.float32) * s, 'up_w': jax.random.normal(ks[3], (E, I_MOE, H), jnp.float32) * s, 'down_w': jax.random.normal(ks[4], (E, H, I_MOE), jnp.float32) * s, 'sh_gate_w': jax.random.normal(ks[5], (N_SH * I_MOE, H), jnp.float32) * s, 'sh_up_w': jax.random.normal(ks[6], (N_SH * I_MOE, H), jnp.float32) * s, 'sh_down_w': jax.random.normal(ks[7], (H, N_SH * I_MOE), jnp.float32) * s}
    _L1_ffn_all = _L1_ffn_setup()
    _L1_ffn_in = {k: v for k, v in _L1_ffn_all.items() if k in ('router_weight', 'e_bias', 'gate_w', 'up_w', 'down_w', 'sh_gate_w', 'sh_up_w', 'sh_down_w')}
    del _L1_ffn_all
    return {'x': x, 'ctx_1024': ctx_1024, 'mask_Bx1xSxS2_ff0': mask_Bx1xSxS2_ff0, 'L0_xattn_wq': _L0_xattn_in['wq'], 'L0_xattn_wk': _L0_xattn_in['wk'], 'L0_xattn_wv': _L0_xattn_in['wv'], 'L0_xattn_wo': _L0_xattn_in['wo'], 'L0_attn_W_dq': _L0_attn_in['W_dq'], 'L0_attn_W_uq': _L0_attn_in['W_uq'], 'L0_attn_W_dkv': _L0_attn_in['W_dkv'], 'L0_attn_W_uk': _L0_attn_in['W_uk'], 'L0_attn_W_uv': _L0_attn_in['W_uv'], 'L0_attn_W_o': _L0_attn_in['W_o'], 'L0_ffn_W': _L0_ffn_in['W'], 'L0_ffn_b': _L0_ffn_in['b'], 'L0_ffn_logits': _L0_ffn_in['logits'], 'L0_ffn_u': _L0_ffn_in['u'], 'L1_xattn_Wq': _L1_xattn_in['Wq'], 'L1_xattn_Wk': _L1_xattn_in['Wk'], 'L1_xattn_Wv': _L1_xattn_in['Wv'], 'L1_xattn_Wo': _L1_xattn_in['Wo'], 'L1_xattn_bo': _L1_xattn_in['bo'], 'L1_attn_attn_w': _L1_attn_in['attn_w'], 'L1_attn_attn_b': _L1_attn_in['attn_b'], 'L1_attn_out_w': _L1_attn_in['out_w'], 'L1_attn_out_b': _L1_attn_in['out_b'], 'L1_ffn_router_weight': _L1_ffn_in['router_weight'], 'L1_ffn_e_bias': _L1_ffn_in['e_bias'], 'L1_ffn_gate_w': _L1_ffn_in['gate_w'], 'L1_ffn_up_w': _L1_ffn_in['up_w'], 'L1_ffn_down_w': _L1_ffn_in['down_w'], 'L1_ffn_sh_gate_w': _L1_ffn_in['sh_gate_w'], 'L1_ffn_sh_up_w': _L1_ffn_in['sh_up_w'], 'L1_ffn_sh_down_w': _L1_ffn_in['sh_down_w']}

def reference(x, ctx_1024, mask_Bx1xSxS2_ff0, L0_xattn_wq, L0_xattn_wk, L0_xattn_wv, L0_xattn_wo, L0_attn_W_dq, L0_attn_W_uq, L0_attn_W_dkv, L0_attn_W_uk, L0_attn_W_uv, L0_attn_W_o, L0_ffn_W, L0_ffn_b, L0_ffn_logits, L0_ffn_u, L1_xattn_Wq, L1_xattn_Wk, L1_xattn_Wv, L1_xattn_Wo, L1_xattn_bo, L1_attn_attn_w, L1_attn_attn_b, L1_attn_out_w, L1_attn_out_b, L1_ffn_router_weight, L1_ffn_e_bias, L1_ffn_gate_w, L1_ffn_up_w, L1_ffn_down_w, L1_ffn_sh_gate_w, L1_ffn_sh_up_w, L1_ffn_sh_down_w):
    import jax
    import jax.numpy as jnp

    def _L0_xattn_ref(query_input, source_input, bias, wq, wk, wv, wo):
        import jax, jax.numpy as jnp
        import numpy as np
        HIDDEN = 128
        NUM_HEADS = 16
        HEAD_DIM = HIDDEN // NUM_HEADS
        B, F, T = (2, 256, 256)
        q = jnp.einsum('bfd,dnh->bfnh', query_input, wq)
        k = jnp.einsum('btd,dnh->btnh', source_input, wk)
        v = jnp.einsum('btd,dnh->btnh', source_input, wv)
        q = q * HEAD_DIM ** (-0.5)
        logits = jnp.einsum('btnh,bfnh->bnft', k, q) + bias
        weights = jax.nn.softmax(logits, axis=-1)
        attn = jnp.einsum('bnft,btnh->bfnh', weights, v)
        return jnp.einsum('bfnh,nhd->bfd', attn, wo)

    def _L0_attn_ref(x, W_dq, W_uq, W_dkv, W_uk, W_uv, W_o):
        import jax, jax.numpy as jnp
        import numpy as np
        from math import sqrt
        N_HEAD = 16
        W_SCALE = 0.02

        def _reference_tuple_inner(x, W_dq, W_uq, W_dkv, W_uk, W_uv, W_o):
            B, T, C = x.shape
            nh = N_HEAD
            hs = C // nh
            n_kvl = W_dkv.shape[0]
            k_eff = (W_dq.T @ W_uq.T @ W_uk).reshape(nh, hs, n_kvl)
            v_eff = jnp.transpose((W_uv.T @ W_o.T).reshape(n_kvl, nh, hs), (1, 0, 2))
            c_kv = x @ W_dkv.T
            q = x @ W_dq.T @ W_uq.T
            q = q.reshape(B, T, nh, hs)
            q_lat = jnp.einsum('bqhd,hdl->bhql', q, k_eff)
            attn = jnp.einsum('bhql,bkl->bhqk', q_lat, c_kv) / sqrt(hs)
            causal = jnp.tril(jnp.ones((T, T), dtype=bool))
            attn = jnp.where(causal[None, None], attn, -jnp.inf)
            attn = jax.nn.softmax(attn, axis=-1)
            y_lat = jnp.einsum('bhqk,bkl->bhql', attn, c_kv)
            y = jnp.einsum('bhql,hld->bqhd', y_lat, v_eff).reshape(B, T, C)
            return (y, c_kv)
        return _reference_tuple_inner(x, W_dq, W_uq, W_dkv, W_uk, W_uv, W_o)[0]

    def _L0_ffn_ref(x, W, b, logits, u):
        import jax, jax.numpy as jnp
        import numpy as np
        NUM_OPS, B, T, D = (8, 8, 64, 128)
        gumbel = -jnp.log(-jnp.log(u))
        idx = jnp.argmax(jax.nn.log_softmax(logits) + gumbel)
        out = jnp.einsum('btd,de->bte', x, W[idx]) + b[idx]
        return out

    def _L1_xattn_ref(q, k, v, Wq, Wk, Wv, Wo, bo):
        import jax, jax.numpy as jnp
        import numpy as np
        DIM = 128
        NUM_HEADS = 16
        HEAD_DIM = DIM // NUM_HEADS
        SCALE = HEAD_DIM ** (-0.5)
        B, QL, _ = q.shape
        KL = k.shape[1]
        qh = (q @ Wq.T).reshape(B, QL, NUM_HEADS, HEAD_DIM)
        kh = (k @ Wk.T).reshape(B, KL, NUM_HEADS, HEAD_DIM)
        vh = (v @ Wv.T).reshape(B, KL, NUM_HEADS, HEAD_DIM)
        attn = jnp.einsum('bnhc,bmhc->bhnm', qh, kh) * SCALE
        attn = jax.nn.softmax(attn, axis=-1)
        out = jnp.einsum('bhnm,bmhc->bnhc', attn, vh).reshape(B, QL, DIM)
        return out @ Wo.T + bo

    def _L1_attn_ref(encodings, attn_w, attn_b, out_w, out_b):
        import jax, jax.numpy as jnp
        import numpy as np
        import math
        HIDDEN = 128
        HEADS = 16
        HEAD = HIDDEN // HEADS
        B, N = (2, 256)
        NEG_INF = -10000.0
        b, n, _ = encodings.shape
        qkv = encodings @ attn_w.T + attn_b
        qkv = qkv.reshape(b, n, HEADS, 3 * HEAD).transpose(0, 2, 1, 3)
        q, k, v = jnp.split(qkv, 3, axis=-1)
        mask = jnp.arange(n)[:, None] <= jnp.arange(n)[None, :]
        scores = jnp.einsum('bhki,bhqi->bhkq', k, q) / math.sqrt(HEAD)
        scores = jnp.where(mask, scores, NEG_INF)
        probs = jax.nn.softmax(scores, axis=2)
        combined = jnp.einsum('bhkq,bhkl->bhql', probs, v)
        out = combined.transpose(0, 2, 1, 3).reshape(b, n, HIDDEN)
        return out @ out_w.T + out_b

    def _L1_ffn_ref(hidden_states, router_weight, e_bias, gate_w, up_w, down_w, sh_gate_w, sh_up_w, sh_down_w):
        import jax, jax.numpy as jnp
        import numpy as np
        B, S, H = (1, 256, 128)
        E, K = (16, 4)
        G, TG = (4, 2)
        I_MOE = 64
        N_SH = 2
        SCALE = 2.5

        def _mlp(x, gw, uw, dw):
            return jax.nn.silu(x @ gw.T) * (x @ uw.T) @ dw.T

        def _route(x2d, router_weight, e_bias):
            T = x2d.shape[0]
            scores = jax.nn.sigmoid(x2d @ router_weight.T)
            sc = scores + e_bias[None, :]
            group_scores = jnp.sum(jax.lax.top_k(sc.reshape(T, G, E // G), 2)[0], axis=-1)
            _, gidx = jax.lax.top_k(group_scores, TG)
            gmask = jnp.zeros((T, G), sc.dtype).at[jnp.arange(T)[:, None], gidx].set(1.0)
            smask = jnp.repeat(gmask, E // G, axis=1)
            masked = jnp.where(smask > 0, sc, 0.0)
            _, tidx = jax.lax.top_k(masked, K)
            tw = jnp.take_along_axis(scores, tidx, axis=1)
            tw = tw / (jnp.sum(tw, axis=-1, keepdims=True) + 1e-20)
            tw = tw * SCALE
            return (tidx, tw)

        def _moe_forward(hidden_states, router_weight, e_bias, gate_w, up_w, down_w, sh_gate_w, sh_up_w, sh_down_w):
            orig_shape = hidden_states.shape
            x = hidden_states.reshape(-1, H)
            T = x.shape[0]
            tidx, tw = _route(x, router_weight, e_bias)
            g = jnp.einsum('th,eih->tei', x, gate_w)
            u = jnp.einsum('th,eih->tei', x, up_w)
            h = jax.nn.silu(g) * u
            yo = jnp.einsum('tei,ehi->teh', h, down_w)
            combine = jnp.zeros((T, E), tw.dtype).at[jnp.arange(T)[:, None], tidx].add(tw)
            routed = jnp.einsum('te,teh->th', combine, yo)
            shared = _mlp(hidden_states.reshape(-1, H), sh_gate_w, sh_up_w, sh_down_w)
            return (routed + shared).reshape(orig_shape)
        return _moe_forward(hidden_states, router_weight, e_bias, gate_w, up_w, down_w, sh_gate_w, sh_up_w, sh_down_w)
    x = x + _L0_xattn_ref(_layernorm(x, axis=-1), ctx_1024, mask_Bx1xSxS2_ff0, L0_xattn_wq, L0_xattn_wk, L0_xattn_wv, L0_xattn_wo)
    x = x + _L0_attn_ref(_layernorm(x, axis=-1), L0_attn_W_dq, L0_attn_W_uq, L0_attn_W_dkv, L0_attn_W_uk, L0_attn_W_uv, L0_attn_W_o)
    x = x + _L0_ffn_ref(_layernorm(x, axis=-1), L0_ffn_W, L0_ffn_b, L0_ffn_logits, L0_ffn_u)
    x = x + _L1_xattn_ref(_layernorm(x, axis=-1), ctx_1024, ctx_1024, L1_xattn_Wq, L1_xattn_Wk, L1_xattn_Wv, L1_xattn_Wo, L1_xattn_bo)
    x = x + _L1_attn_ref(_layernorm(x, axis=-1), L1_attn_attn_w, L1_attn_attn_b, L1_attn_out_w, L1_attn_out_b)
    x = x + _L1_ffn_ref(_layernorm(x, axis=-1), L1_ffn_router_weight, L1_ffn_e_bias, L1_ffn_gate_w, L1_ffn_up_w, L1_ffn_down_w, L1_ffn_sh_gate_w, L1_ffn_sh_up_w, L1_ffn_sh_down_w)
    return x

_drawn_inputs = setup_inputs


def setup_inputs(seed=0):
    import zlib

    import numpy as np

    out = dict(_drawn_inputs(seed))
    spreads = {'L0_ffn_b': (0.0, 0.1), 'L1_ffn_e_bias': (0.0, 0.8)}
    factors = {'L0_attn_W_dq': 8.0,
     'L0_attn_W_uq': 8.0,
     'L0_attn_W_dkv': 8.0,
     'L0_attn_W_uk': 8.0,
     'L0_attn_W_uv': 8.0,
     'L0_attn_W_o': 8.0,
     'L1_xattn_bo': 3.263,
     'L1_attn_attn_b': 2.868,
     'L1_ffn_router_weight': 8.0,
     'L1_ffn_gate_w': 8.0,
     'L1_ffn_up_w': 8.0,
     'L1_ffn_down_w': 8.0,
     'L1_ffn_sh_gate_w': 8.0,
     'L1_ffn_sh_up_w': 8.0,
     'L1_ffn_sh_down_w': 8.0}
    for name, (base, spread) in spreads.items():
        noise = np.random.default_rng([zlib.crc32(name.encode()), seed]).standard_normal(out[name].shape)
        drawn = base * np.exp(spread * noise) if base else spread * noise
        out[name] = jnp.asarray(drawn.astype(out[name].dtype))
    for name, factor in factors.items():
        out[name] = (out[name] * factor).astype(out[name].dtype)
    return out
```

```python
from contextlib import ExitStack

import numpy as np

import concourse.bass as bass
from concourse import mybir

F32 = mybir.dt.float32
BF16 = mybir.dt.bfloat16
U16 = mybir.dt.uint16
U32 = mybir.dt.uint32
I32 = mybir.dt.int32
ALU = mybir.AluOpType
ACT = mybir.ActivationFunctionType
AX = mybir.AxisListType

P = 128
B = 2
H = 16
HD = P // H
SK = 2048
NP = H // 2
NN = NP * B
KB = SK // P
PARTS = 3
SLOTS = [(0, 0), (0, 1), (0, 2), (1, 0), (1, 1), (2, 0)]
K_TIMES = [sum(kp == part for kp, _ in SLOTS) for part in range(PARTS)]
HR = len(SLOTS) * HD
HOFF = 64
VW = 17
VP = 32
U = 4
E = 16
FB = E * 64 // P
FB1 = FB + 1
GROUPS = 4
SCALE = float(HD) ** -0.5
BIG = 3.0e38
BIGHALF = 2.0e38
EPS = 1e-5
ROUTED_SCALE = 2.5

PK_A = dict(x=0, wq0=256, wk0=384, wv0=512, wo0=640, ident=768)
PK_A_W = 896
PK_B = dict(wk1=0, wv1=128, wq1=256, wo1=384, w_oT=512, w_uv=640, w_uk=704, aq=768, ak=896, av=1024,
            aoT=1152, router=1280, hmask=1296, sel_o=1312, bq=1330, bk=1331)
PK_B_W = 1332
PK_C = dict(w_dq=0, w_uqT=128, w_dkv=256)
PK_C_W = 384
PK_R = dict(u=0, logits=8, bo1=16, bv=144, bout=272, ebias=400, ones=416)
PK_R_W = 544
PK_M = dict(gate=0, up=1152, down=2304)
PK_M_W = 3456

C_EXP = 4
C_PV = 16
C_DIV = 1


def perceiver_kernel(nc, packA, packB, packC, packR, packM, ffnW, ffnb, mask, ctxT, selq_d, krows_d, rep_d, out):
    with ExitStack() as ctx:
        def sb(name, shape, dt=F32):
            return ctx.enter_context(nc.sbuf_tensor(name, shape, dt))

        sems = {}

        def S(name):
            if name not in sems:
                sems[name] = ctx.enter_context(nc.semaphore(name))
            return sems[name]

        bank = ctx.enter_context(nc.psum_tensor("bank", [P, 8, 512], F32))
        kscr = nc.dram_tensor("k_scratch", (2, B, PARTS, H, HD, SK), BF16, kind="Internal").ap()

        wA = sb("wA", [P, PK_A_W])
        wB = sb("wB", [P, PK_B_W])
        wC = sb("wC", [64, PK_C_W])
        wR = sb("wR", [1, PK_R_W])
        wM = sb("wM", [P, PK_M_W])
        ctxT_s = sb("ctxT_s", [P, B * SK])
        mask_s = sb("mask_s", [P, B, SK])
        selq = sb("selq", [P, PARTS * NP * P], BF16)
        rep = sb("rep", [E, FB * P])
        ident_b = sb("ident_b", [P, P], BF16)
        two_ident = sb("two_ident", [P, 2, P])

        kparts = sb("kparts", [P, PARTS, B * SK], BF16)
        k_rest = [sb(f"k_rest{i}", [P, 512]) for i in range(2)]
        v_all = [sb(f"v_all{l}", [P, NP, B, KB, VW]) for l in range(2)]

        kpair = [sb(f"kpair{i}", [P, SK], BF16) for i in range(U)]
        vpair = [sb(f"vpair{i}", [P, KB, VP]) for i in range(2)]
        q_f = sb("q_f", [P, B * P])
        q_rest = sb("q_rest", [P, B * P])
        q_parts = sb("q_parts", [P, PARTS, B * P], BF16)
        q_max = [sb(f"q_max{i}", [P, 2 * P], BF16) for i in range(2)]
        q_exp = [sb(f"q_exp{i}", [P, 2 * P], BF16) for i in range(2)]
        mx = [sb(f"mx{i}", [P, 2, 2]) for i in range(2)]
        negm = sb("negm", [P, 2])
        m_rows = [sb(f"m_rows{i}", [P, P], BF16) for i in range(2)]
        probs = sb("probs", [P, 4, 512])
        o_sb = [sb(f"o_sb{i}", [P, 2 * P]) for i in range(2)]
        o_rec = sb("o_rec", [P, 2])
        onorm = sb("onorm", [P, B, HD * 2 + P])
        oT = sb("oT", [P, B * P])

        x = wA[:, 0:B * P].rearrange("p (b d) -> p b d", b=B)
        st = sb("st", [P, B, 6])
        mv = sb("mv", [P, B, 2])
        ve = sb("ve", [P, B])
        lnv = sb("lnv", [P, B])
        y0 = sb("y0", [P, B])
        yt = sb("yt", [P, B])
        rstd = sb("rstd", [P, B])
        xn = sb("xn", [P, B, P])
        xnT = sb("xnT", [P, B * P])

        qT = sb("qT", [P, B * P])
        kT = sb("kT", [P, B * P])
        kflat = v_all[0][:, :, :, :, :].rearrange("p a b k w -> p (a b k w)")[:, 0:B * H * P]
        kexp = kflat.rearrange("p (b h k) -> p b h k", b=B, h=H)
        s_sb = sb("s_sb", [P, 2 * 4, 512])
        pT = mask_s[:, :, :].rearrange("p b (w n) -> p (b w) n", n=512)
        v9 = sb("v9", [P, B, H, HD + 1])
        s_mx = sb("s_mx", [P, 8, 4])
        s_rec = sb("s_rec", [P, B, H])
        att = sb("att", [P, B, P])
        attT = sb("attT", [P, B * P])
        w_g = sb("w_g", [P, P])
        w_gT = sb("w_gT", [P, P])
        k_effT = sb("k_effT", [64, P])
        v_eff = sb("v_eff", [64, P])
        wk_eff = sb("wk_eff", [P, P])
        wv_eff = sb("wv_eff", [P, P])

        gum = sb("gum", [1, 64])
        gidx = sb("gidx", [1, 8], U32)
        wsel = sb("wsel", [P, P])
        bsel = sb("bsel", [1, P])
        flag_f = sb("flag_f", [P, 2])
        flag_i = sb("flag_i", [1, 1], I32)
        ones_col = sb("ones_col", [P, 1])

        r_e = sb("r_e", [P, B, E])
        r_sc = sb("r_sc", [P, B, E])
        r_scb = sb("r_scb", [P, B, E])
        r_six = sb("r_six", [P, B * GROUPS, 6])
        r_gs = sb("r_gs", [P, B, 8])
        r_v8 = sb("r_v8", [P, B, 8])
        r_top = sb("r_top", [P, B, 8])
        r_top4 = sb("r_top4", [P, B, 8])
        r_mr = sb("r_mr", [P, B, 8])
        r_gm = sb("r_gm", [P, B, 8])
        r_msk = sb("r_msk", [P, B, E])
        r_mr2 = sb("r_mr2", [P, B, E])
        r_sum = sb("r_sum", [P, B])
        comb = sb("comb", [P, B, E])
        combT = sb("combT", [E, B * P])
        f_t = s_sb[:, :, :].rearrange("p w n -> p (w n)")[:, 0:FB1 * 256].rearrange("p (f t) -> p f t", t=256)
        f_h = kflat[:, 0:FB1 * 256].rearrange("p (f t) -> p f t", t=256)
        f_a = kpair[0][:, :].bitcast(F32)[:, 0:512].rearrange("p (i t) -> p i t", i=2)
        f_c = pT[:, 0:4, :].rearrange("p w (i t) -> p (w i) t", t=256)

        def A_(k, w=P):
            return wA[:, PK_A[k]:PK_A[k] + w]

        def B_(k, w=P):
            return wB[:, PK_B[k]:PK_B[k] + w]

        def C_(k):
            return wC[:, PK_C[k]:PK_C[k] + P]

        def R_(k, w=P):
            return wR[0:1, PK_R[k]:PK_R[k] + w]

        ident = A_("ident")
        ones_row = R_("ones")
        sel_o = B_("sel_o", 18).rearrange("p (a c) -> p a c", a=2)
        WK = [A_("wk0"), B_("wk1")]
        WV = [A_("wv0"), B_("wv1")]
        WQ = [A_("wq0"), B_("wq1")]
        WO = [A_("wo0"), B_("wo1")]

        block = ctx.enter_context(nc.Block())

        @block.sync
        def _(sp):
            sp.dma_start(wA[:, :], packA).then_inc(S("in_A"), 16)
            for c in range(4):
                sp.dma_start(ctxT_s[:, c * 1024:(c + 1) * 1024], ctxT[:, c * 1024:(c + 1) * 1024]) \
                    .then_inc(S(f"in_ctx{c}"), 16)
            sp.dma_start(wR[:, :], packR).then_inc(S("in_R"), 16)
            for b in range(B):
                sp.dma_start(mask_s[:, b, :], mask[b, 0, :, :]).then_inc(S("in_mask"), 16)
            sp.dma_start(wM[:, :], packM).then_inc(S("in_M"), 16)
            sp.dma_start(rep[:, :], rep_d).then_inc(S("in_M"), 16)

            def store_k(l):
                for b in range(B):
                    sp.wait_ge(S("k_low"), 8 * l + 4 * b + 4)
                    for kp in range(PARTS):
                        sp.dma_start(kscr[l, b, kp, :, :, :],
                                     kparts[:, kp, b * SK:(b + 1) * SK]).then_inc(S(f"k_stored{b}"), 16)

            def load_k(l, p, b, u):
                for a in range(2):
                    row = a * HOFF
                    for kp in range(PARTS):
                        times = K_TIMES[kp]
                        src = kscr[l, b, kp, bass.ds(p * 2 + a, 1), :, :].rearrange("h d t -> (h d) t")
                        src = src.unsqueeze(0).to_broadcast([times, HD, SK])
                        sp.dma_start(kpair[u][row:row + times * HD, :], src).then_inc(S(f"k_loaded{u}"), 16)
                        row += times * HD

            def cross_k(l):
                for b in range(B):
                    sp.wait_ge(S(f"k_stored{b}"), 16 * PARTS * (l + 1))
                for n in range(3):
                    if l:
                        sp.wait_ge(S("b_done"), 8 * (NN * l + n - 3))
                    load_k(l, n // B, n % B, n)
                with sp.Fori(0, 3) as i:
                    for u in range(U):
                        sp.wait_ge(S("b_done"), i * 32 + (8 * (NN * l + u) + 1))
                        load_k(l, i * 2 + (u + 3) // 2, (u + 3) % B, (u + 3) % U)
                sp.wait_ge(S("b_done"), 8 * (NN * l + 12))
                load_k(l, NP - 1, 1, 3)

            sp.wait_ge(S("krows_in"), 16 * 2 * U)
            store_k(0)
            cross_k(0)
            store_k(1)
            sp.wait_ge(S("idx"), 1)
            idx = sp.value_load(gidx[0:1, 0:1], min_val=0, max_val=7)
            sp.dma_start(wsel[:, :], ffnW[bass.ds(idx, 1), :, :]).then_inc(S("in_sel"), 16)
            sp.dma_start(bsel[:, :], ffnb[bass.ds(idx, 1), :]).then_inc(S("in_sel"), 16)
            cross_k(1)
            sp.wait_ge(S("y_ready"), 2)
            sp.dma_start(out.rearrange("b t d -> t b d"), x).then_inc(S("out_done"), 16)
            sp.wait_ge(S("out_done"), 16)

        @block.gpsimd
        def _(pool):
            for i in range(2):
                pool.memset(vpair[i][:, :, :], 0.0).then_inc(S("v_zero"), 1)

            def cross_v(l):
                pool.wait_ge(S("v_copied"), 8 * (l + 1))
                if l == 0:
                    pool.wait_ge(S("v_zero"), 4)

                def one(n, pp, u):
                    pool.wait_ge(S("pv_done"), n * 4 + (C_PV + 4 * NN * l - 4))
                    pool.tensor_copy(vpair[u % 2][:, :, 0:VW], pp).then_inc(S("v_pair"), 1)

                vl = v_all[l][:, :, :, :, :].rearrange("p a b k w -> p (a b k w)")
                with pool.Fori(0, 4) as i:
                    for u in range(U):
                        W = KB * VW
                        src = vl[:, bass.ds(i * (U * W) + u * W, W)].rearrange("p (k w) -> p k w", w=VW)
                        one(i * U + u, src, u)

            def causal(l):
                for w in range(8):
                    pool.wait_ge(S("s_copied"), 8 * l + w + 1)
                    v = s_sb[:, w, :].rearrange("p (h k) -> p h k", h=4)
                    pool.affine_select(out=v, in_=v, compare_op=ALU.is_ge, fill=(-BIG if l == 0 else -10000.0),
                                       base=0, pattern=[[0, 4], [-1, P]], channel_multiplier=1) \
                        .then_inc(S("s_masked"), 1)

            cross_v(0)
            causal(0)
            cross_v(1)
            causal(1)
            for f in range(FB):
                pool.wait_ge(S("f_inner"), f + 1)
                pool.wait_ge(S("f_weight"), f // 2 + 1)
                pool.tensor_tensor(f_h[:, f, :], f_h[:, f, :], f_c[:, f, :], ALU.mult).then_inc(S("f_scaled"), 1)

        @block.scalar
        def _(act):
            act.dma_start(wC[:, :], packC).then_inc(S("in_C"), 16)
            act.dma_start(wB[:, :], packB).then_inc(S("in_B"), 16)
            act.dma_start(selq[:, :].bitcast(U16), selq_d).then_inc(S("in_selq"), 16)
            act.wait_ge(S("k_zero"), U)
            for i in range(U):
                for a in range(2):
                    act.dma_start(kpair[i][a * HOFF + HR:(a + 1) * HOFF, :].bitcast(U16), krows_d) \
                        .then_inc(S("krows_in"), 16)
            chain = [0]

            def link(ins):
                chain[0] += 1
                ins.then_inc(S("act_link"), 1)
                act.wait_ge(S("act_link"), chain[0])

            def copy(dst, src, scale=1.0):
                return act.activation(dst, src, ACT.Copy, scale=scale)

            def prep(l, c):
                k = 8 * l + c
                act.wait_ge(S("k_proj"), k + 1)
                if l and c % 4 == 0:
                    act.wait_ge(S(f"k_stored{c // 4}"), 16 * PARTS)
                copy(kparts[:, 0, c * 512:(c + 1) * 512], bank[:, 6, :]).then_inc(S("k_high"), 1)
                act.wait_ge(S("k_rest1"), k + 1)
                copy(kparts[:, 1, c * 512:(c + 1) * 512], k_rest[c % 2][:, :]).then_inc(S("k_mid"), 1)
                act.wait_ge(S("v_proj"), k + 1)
                b, kb = c // 4, (c % 4) * 4
                for i in range(4):
                    last = copy(v_all[l][:, :, b, kb + i, 0:16],
                                bank[:, 7, i * P:(i + 1) * P].rearrange("p (a w) -> p a w", a=NP))
                last.then_inc(S("v_copied"), 1)

            def norm(ph):
                act.wait_ge(S(f"{ph}_var"), 1)
                link(act.activation(lnv[:, :], ve[:, :], ACT.Ln))
                act.activation(y0[:, :], lnv[:, :], ACT.Exp, scale=-0.5).then_inc(S(f"{ph}_y0"), 1)
                act.wait_ge(S(f"{ph}_xnTp"), 1)
                copy(xnT[:, :], bank[:, 0, 0:256]).then_inc(S(f"{ph}_xnT"), 1)

            def query(l):
                act.wait_ge(S("q_proj"), l + 1)
                copy(q_f[:, :], bank[:, 1, 0:256], SCALE).then_inc(S("q_f"), 1)
                act.wait_ge(S("q_f"), l + 1)
                copy(q_parts[:, 0, :], q_f[:, :]).then_inc(S("q_high"), 1)

            def cross(l):
                g0 = NN * l

                def put_q(dst):
                    copy(dst[0:64, 0:P], bank[0:64, 6, 0:P])
                    return copy(dst[64:P, P:2 * P], bank[64:P, 6, 0:P])

                def put_qm(n, u):
                    act.wait_ge(S("qm_rows"), n + (g0 + 1))
                    put_q(q_max[u % 2]).then_inc(S("qm_put"), 1)

                def put_qe(n, u):
                    act.wait_ge(S("qe_rows"), n + (g0 + 1))
                    put_q(q_exp[u % 2]).then_inc(S("qe_put"), 1)

                def take_o(n, u):
                    act.wait_ge(S("pv_done"), n * 4 + (C_PV + 4 * g0))
                    copy(o_sb[(u + 1) % 2][:, :], bank[:, 7, 0:256]).then_inc(S("o_taken"), 1)

                def body(n, u, qm, qe):
                    take_o(n, u)
                    for j in range(8):
                        act.wait_ge(S("b_done"), n * 8 + (8 * g0 + j + 1))
                        if j % 2 == 0:
                            act.wait_ge(S("pv_done"), n * 4 + (C_PV + 4 * g0 + j // 2 - 1))
                        act.activation(probs[:, j % 4, :], bank[:, 4 + j % 2, :], ACT.Exp) \
                            .then_inc(S("exp_done"), 1)
                        if j == 1 and qm:
                            put_qm(n + 3, u + 3)
                        if j == 3 and qe:
                            put_qe(n + 1, u + 1)

                act.wait_ge(S("q_zero"), 4)
                act.wait_ge(S("o_zero"), 1)
                for n in range(3):
                    if n == 2:
                        act.wait_ge(S("a_done"), 4 * (g0 + 1))
                    put_qm(n, n)
                put_qe(0, 0)
                with act.Fori(0, 3) as i:
                    for u in range(U):
                        body(i * U + u, u, True, True)
                for u in range(U):
                    n = 12 + u
                    body(n, u, n + 3 < NN, n + 1 < NN)
                take_o(NN, 0)
                act.wait_ge(S("oT_p"), l + 1)
                copy(oT[:, :], bank[:, 0, 0:256]).then_inc(S("oT"), 1)

            def self_attention(l):
                act.wait_ge(S("v_self"), l + 1)
                copy(v9[:, :, :, 0:HD], bank[:, 3, 0:256].rearrange("p (b h d) -> p b h d", b=B, d=HD)) \
                    .then_inc(S("v9"), 1)

                def s_copy(w):
                    act.wait_ge(S("s_done"), 8 * l + w + 1)
                    copy(s_sb[:, w, :], bank[:, 4 + w % 2, :]).then_inc(S("s_copied"), 1)

                def s_exp(w):
                    act.wait_ge(S("s_max"), 8 * l + w + 1)
                    for h in range(4):
                        last = act.activation(s_sb[:, w, h * P:(h + 1) * P], s_sb[:, w, h * P:(h + 1) * P],
                                              ACT.Exp, bias=s_mx[:, w, h:h + 1])
                    last.then_inc(S("s_exp"), 1)

                for w in range(8 + 3):
                    if w < 8:
                        s_copy(w)
                    if w >= 3:
                        s_exp(w - 3)
                    if l == 0:
                        if w < 8:
                            prep(1, w)
                if l:
                    act.wait_ge(S("attT_p"), 1)
                    copy(attT[:, :], bank[:, 3, 0:256]).then_inc(S("attT"), 1)

            act.wait_ge(S("in_A"), 16)
            copy(ident_b[:, :], ident)
            copy(two_ident[:, 0, :], ident)
            copy(two_ident[:, 1, :], ident).then_inc(S("idents"), 1)
            norm("n0")
            query(0)
            for c in range(8):
                prep(0, c)
            act.wait_ge(S("in_R"), 16)
            link(act.activation(gum[:, 0:8], R_("u", 8), ACT.Ln))
            act.activation(gum[:, 8:16], gum[:, 0:8], ACT.Ln, scale=-1.0).then_inc(S("gum_ln"), 1)
            act.wait_ge(S("gum_shift"), 1)
            act.activation(gum[:, 24:32], gum[:, 16:24], ACT.Exp).then_inc(S("gum_exp"), 1)
            act.wait_ge(S("gum_sum"), 1)
            act.activation(gum[:, 33:34], gum[:, 32:33], ACT.Ln).then_inc(S("gum_lse"), 1)
            cross(0)
            norm("n1")
            self_attention(0)
            norm("n2")
            norm("n3")
            query(1)
            cross(1)
            norm("n4")
            self_attention(1)
            norm("n5")
            act.wait_ge(S("r_logits"), 1)
            act.activation(r_e[:, :, :], bank[:, 1, 0:2 * E].rearrange("p (b e) -> p b e", b=B),
                           ACT.Exp, scale=-1.0).then_inc(S("r_exp"), 1)
            for f in range(FB1):
                act.wait_ge(S("f_done"), f + 1)
                act.activation(f_t[:, f, :], bank[:, 3 + f % 3, 0:256], ACT.Tanh, scale=0.5) \
                    .then_inc(S("f_tanh"), 1)
            act.wait_ge(S("combT_p"), 1)
            copy(combT[:, :], bank[0:E, 2, 0:256]).then_inc(S("combT"), 1)
            for f in range(FB // 2):
                act.wait_ge(S("rep_done"), f + 1)
                copy(f_c[:, 2 * f:2 * f + 2, :], bank[:, 6 + f % 2, :].rearrange("p (i t) -> p i t", i=2)) \
                    .then_inc(S("f_weight"), 1)

        @block.vector
        def _(dve):
            chain = [0]

            def link(ins):
                chain[0] += 1
                ins.then_inc(S("dve_link"), 1)
                dve.wait_ge(S("dve_link"), chain[0])

            V = nc.vector
            for i in range(U):
                V.memset(kpair[i][:, :].bitcast(U32), 0).then_inc(S("k_zero"), 1)
            for i in range(2):
                V.memset(q_max[i][:, :], 0.0).then_inc(S("q_zero"), 1)
                V.memset(q_exp[i][:, :], 0.0).then_inc(S("q_zero"), 1)
                V.memset(m_rows[i][:, :], 0.0).then_inc(S("m_zero"), 1)
                V.memset(v_all[i][:, :, :, :, VW - 1:VW], 1.0).then_inc(S("v_zero"), 1)
            V.memset(o_sb[0][:, :], 1.0)
            V.memset(bank[:, 7, 0:256], 1.0).then_inc(S("o_zero"), 1)
            V.memset(onorm[:, :, :], 0.0).then_inc(S("o_div"), C_DIV)
            V.memset(v9[:, :, :, HD:HD + 1], 1.0).then_inc(S("v9_ones"), 1)
            V.memset(ones_col[:, :], 1.0).then_inc(S("exp_done"), C_EXP)
            V.memset(r_gs[:, :, :], -BIG)
            V.memset(r_top[:, :, :], BIG)
            V.memset(r_top4[:, :, :], BIG).then_inc(S("pv_done"), C_PV)
            dve.wait_ge(S("pv_done"), C_PV)

            def norm(ph):
                for b in range(B):
                    last = V.bn_stats(st[:, b, :], x[:, b, :])
                link(last)
                for b in range(B):
                    last = V.bn_aggr(mv[:, b, :], st[:, b, :])
                link(last)
                V.tensor_scalar(ve[:, :], mv[:, :, 1], EPS, None, ALU.add).then_inc(S(f"{ph}_var"), 1)
                dve.wait_ge(S(f"{ph}_y0"), 1)
                link(V.tensor_tensor(yt[:, :], y0[:, :], y0[:, :], ALU.mult))
                link(V.tensor_tensor(yt[:, :], yt[:, :], ve[:, :], ALU.mult))
                link(V.tensor_scalar(yt[:, :], yt[:, :], -0.5, 1.5, ALU.mult, ALU.add))
                link(V.tensor_tensor(rstd[:, :], yt[:, :], y0[:, :], ALU.mult))
                for b in range(B):
                    V.tensor_scalar(xn[:, b, :], x[:, b, :], mv[:, b, 0:1], rstd[:, b:b + 1],
                                    ALU.subtract, ALU.mult).then_inc(S(f"{ph}_xn"), 1)

            def prep(l, c):
                k = 8 * l + c
                cols = slice(c * 512, (c + 1) * 512)
                dve.wait_ge(S("k_high"), k + 1)
                if k >= 2:
                    dve.wait_ge(S("k_low"), k - 1)
                V.tensor_tensor(k_rest[c % 2][:, :], bank[:, 6, :], kparts[:, 0, cols], ALU.subtract) \
                    .then_inc(S("k_rest1"), 1)
                dve.wait_ge(S("k_mid"), k + 1)
                V.tensor_tensor(kparts[:, 2, cols], k_rest[c % 2][:, :], kparts[:, 1, cols], ALU.subtract) \
                    .then_inc(S("k_low"), 1)

            def query(l):
                dve.wait_ge(S("q_high"), l + 1)
                link(V.tensor_tensor(q_rest[:, :], q_f[:, :], q_parts[:, 0, :], ALU.subtract))
                link(V.tensor_copy(q_parts[:, 1, :], q_rest[:, :]))
                V.tensor_tensor(q_parts[:, 2, :], q_rest[:, :], q_parts[:, 1, :], ALU.subtract) \
                    .then_inc(S("q_split"), 1)

            def cross(l):
                g0 = NN * l

                def maxima(n, u, w):
                    dve.wait_ge(S("a_done"), n * 4 + (4 * g0 + w + 1))
                    V.tensor_reduce(mx[u % 2][:, w // 2, w % 2:w % 2 + 1],
                                    bank[:, 2 * (w % 2):2 * (w % 2) + 2, :], AX.XY, ALU.max) \
                        .then_inc(S("max_done"), 1)

                def rows(n, u):
                    m3 = m_rows[u % 2][:, :].rearrange("q (a r) -> q a r", a=2)
                    dve.wait_ge(S("max_done"), n * 4 + (4 * g0 + 4))
                    V.tensor_reduce(negm[:, :], mx[u % 2][:, :, :], AX.X, ALU.max, negate=True) \
                        .then_inc(S("neg_done"), 1)
                    dve.wait_ge(S("neg_done"), n + (g0 + 1))
                    V.tensor_copy(m3[:, :, HR], negm[:, :]).then_inc(S("m_high"), 1)
                    dve.wait_ge(S("m_high"), n + (g0 + 1))
                    V.tensor_tensor(m3[:, :, HR + 1], negm[:, :], m3[:, :, HR], ALU.subtract) \
                        .then_inc(S("m_rows"), 1)

                def divide(n, u, off, b):
                    ps = bank[:, 6, 256:256 + 18].rearrange("p (a c) -> p a c", a=2)
                    dve.wait_ge(S("o_heads"), n + (17 * l + 1))
                    V.reciprocal(o_rec[:, :], ps[:, :, HD]).then_inc(S("o_rec"), 1)
                    dve.wait_ge(S("o_rec"), n + (17 * l + 1))
                    dst = onorm[:, b, bass.ds(off, 16)].rearrange("p (a d) -> p a d", a=2)
                    V.tensor_tensor(dst, ps[:, :, 0:HD], o_rec[:, :].unsqueeze(2).to_broadcast([P, 2, HD]), ALU.mult) \
                        .then_inc(S("o_div"), 1)

                def body(n, u, i, ahead, more):
                    if more:
                        rows(n + 1, u + 1)
                    for w in range(4):
                        if ahead:
                            maxima(n + 2, u, w)
                        if w == 2:
                            divide(n, u, i * 32 + 16 * ((u + 1) // 2), (u + 1) % 2)

                for n in range(2):
                    for w in range(4):
                        maxima(n, n, w)
                    if n == 0:
                        rows(0, 0)
                with dve.Fori(0, 3) as i:
                    for u in range(U):
                        body(i * U + u, u, i, True, True)
                for u in range(U):
                    n = 12 + u
                    body(n, u, 3, n + 2 < NN, n + 1 < NN)
                divide(NN, 0, 32 * 4, 1)
                for b in range(B):
                    dve.wait_ge(S("o_out"), 2 * l + b + 1)
                    last = V.tensor_tensor(x[:, b, :], bank[:, 1 + b, 0:P], x[:, b, :], ALU.add)
                link(last)

            def self_attention(l):
                qs, ks = (("bq", "bk") if l else (None, None))
                dve.wait_ge(S("q_self"), l + 1)
                if l:
                    V.tensor_scalar(qT[:, :], bank[:, 1, 0:256], B_("bq", 1), SCALE, ALU.add, ALU.mult) \
                        .then_inc(S("qT"), 1)
                    dve.wait_ge(S("k_self"), l + 1)
                    V.tensor_scalar(kT[:, :], bank[:, 2, 0:256], B_("bk", 1), None, ALU.add).then_inc(S("kT"), 1)
                else:
                    V.tensor_scalar(qT[:, :], bank[:, 1, 0:256], SCALE, None, ALU.mult).then_inc(S("qT"), 1)
                    dve.wait_ge(S("k_self"), l + 1)
                    V.tensor_copy(kT[:, :], bank[:, 2, 0:256]).then_inc(S("kT"), 1)
                dve.wait_ge(S("kT"), l + 1)
                for b in range(B):
                    V.tensor_tensor(kexp[:, b, :, :],
                                    kT[:, b * P:(b + 1) * P].unsqueeze(1).to_broadcast([P, H, P]),
                                    B_("hmask", H).unsqueeze(2).to_broadcast([P, H, P]), ALU.mult) \
                        .then_inc(S("kexp"), 1)

                def s_max(w):
                    dve.wait_ge(S("s_masked"), 8 * l + w + 1)
                    V.tensor_reduce(s_mx[:, w, :], s_sb[:, w, :].rearrange("p (h k) -> p h k", h=4), AX.X, ALU.max,
                                    negate=True).then_inc(S("s_max"), 1)

                def p_copy(w):
                    dve.wait_ge(S("p_trans"), 8 * l + w + 1)
                    V.tensor_copy(pT[:, w, :], bank[:, w % 2, :]).then_inc(S("p_copied"), 1)

                for w in range(8 + 4):
                    if w < 8:
                        s_max(w)
                    if w >= 4:
                        p_copy(w - 4)
                    if l == 0 and w < 8:
                        prep(1, w)
                dve.wait_ge(S("pv_self"), 8 * l + 8)
                o9 = bank[:, 2, 0:B * H * 9].rearrange("p (b h c) -> p b h c", b=B, c=HD + 1)
                link(V.reciprocal(s_rec[:, :, :], o9[:, :, :, HD]))
                for b in range(B):
                    last = V.tensor_tensor(att[:, b, :].rearrange("p (h d) -> p h d", h=H), o9[:, b, :, 0:HD],
                                           s_rec[:, b, :].unsqueeze(2).to_broadcast([P, H, HD]), ALU.mult)
                last.then_inc(S("att"), 1)
                dve.wait_ge(S("att"), l + 1)
                if l == 0:
                    link(V.tensor_tensor(x[:, :, :], att[:, :, :], x[:, :, :], ALU.add))
                else:
                    dve.wait_ge(S("att_out"), 1)
                    link(V.tensor_tensor(x[:, :, :], bank[:, 4, 0:256].rearrange("p (b d) -> p b d", b=B), x[:, :, :],
                                         ALU.add))

            dve.wait_ge(S("in_A"), 16)
            norm("n0")
            query(0)
            for c in range(8):
                prep(0, c)
            dve.wait_ge(S("fold1"), 1)
            V.tensor_copy(w_g[:, :], bank[:, 2, 0:P])
            V.tensor_copy(w_gT[:, :], bank[:, 2, P:2 * P])
            V.tensor_copy(v_eff[:, :], bank[0:64, 2, 2 * P:3 * P]).then_inc(S("fold1_c"), 1)
            dve.wait_ge(S("fold2"), 1)
            V.tensor_copy(wv_eff[:, :], bank[:, 3, 0:P])
            V.tensor_copy(k_effT[:, :], bank[0:64, 3, P:2 * P]).then_inc(S("fold2_c"), 1)
            dve.wait_ge(S("fold3"), 1)
            V.tensor_copy(wk_eff[:, :], bank[:, 2, 0:P]).then_inc(S("fold3_c"), 1)
            dve.wait_ge(S("in_mask"), 32)
            mflat = mask_s[:, :, :].rearrange("p b t -> p (b t)")
            V.tensor_scalar(v_scratch(s_sb), mflat, 0.0, None, ALU.not_equal, ALU.add, accum_out=flag_f[:, 0:1]) \
                .then_inc(S("flag_rows"), 1)
            dve.wait_ge(S("flag_sum"), 1)
            V.tensor_copy(flag_i[:, :], bank[0:1, 3, 0:1]).then_inc(S("flag"), 1)
            dve.wait_ge(S("in_R"), 16)
            link(V.tensor_reduce(gum[:, 34:35], R_("logits", 8), AX.X, ALU.max))
            V.tensor_scalar(gum[:, 16:24], R_("logits", 8), gum[:, 34:35], None, ALU.subtract) \
                .then_inc(S("gum_shift"), 1)
            dve.wait_ge(S("gum_exp"), 1)
            V.tensor_reduce(gum[:, 32:33], gum[:, 24:32], AX.X, ALU.add).then_inc(S("gum_sum"), 1)
            dve.wait_ge(S("gum_lse"), 1)
            link(V.tensor_scalar(gum[:, 36:44], gum[:, 16:24], gum[:, 33:34], None, ALU.subtract))
            dve.wait_ge(S("gum_ln"), 1)
            link(V.tensor_tensor(gum[:, 44:52], gum[:, 36:44], gum[:, 8:16], ALU.subtract))
            link(V.max(gum[:, 52:60], gum[:, 44:52]))
            V.max_index(gidx[:, :], gum[:, 52:60], gum[:, 44:52]).then_inc(S("idx"), 1)

            cross(0)
            norm("n1")
            self_attention(0)
            norm("n2")
            dve.wait_ge(S("ff_out"), 1)
            link(V.tensor_tensor(x[:, :, :], bank[:, 1, 0:256].rearrange("p (b d) -> p b d", b=B), x[:, :, :], ALU.add))
            norm("n3")
            query(1)
            cross(1)
            norm("n4")
            self_attention(1)
            norm("n5")
            dve.wait_ge(S("r_exp"), 1)
            link(V.tensor_scalar(r_e[:, :, :], r_e[:, :, :], 1.0, None, ALU.add))
            link(V.reciprocal(r_sc[:, :, :], r_e[:, :, :]))
            link(V.tensor_tensor(r_scb[:, :, :], r_sc[:, :, :],
                                 bank[:, 1, 64:64 + E].unsqueeze(1).to_broadcast([P, B, E]), ALU.add))
            g4 = r_scb[:, :, :].rearrange("p b (g k) -> p (b g) k", k=4)
            V.tensor_tensor(r_six[:, :, 0:3], g4[:, :, 0:3], g4[:, :, 1:4], ALU.add)
            V.tensor_tensor(r_six[:, :, 3:5], g4[:, :, 0:2], g4[:, :, 2:4], ALU.add)
            link(V.tensor_tensor(r_six[:, :, 5:6], g4[:, :, 0:1], g4[:, :, 3:4], ALU.add))
            link(V.tensor_reduce(r_gs[:, :, 0:4], r_six[:, :, :].rearrange("p (b g) s -> p b g s", b=B), AX.X, ALU.max))
            for b in range(B):
                last = V.max(r_v8[:, b, :], r_gs[:, b, :])
            link(last)
            link(V.tensor_copy(r_top[:, :, 0:2], r_v8[:, :, 0:2]))
            for b in range(B):
                last = V.match_replace(r_mr[:, b, :], r_top[:, b, :], r_gs[:, b, :], BIG)
            link(last)
            link(V.tensor_scalar(r_gm[:, :, :], r_mr[:, :, :], BIGHALF, None, ALU.is_ge))
            link(V.tensor_tensor(r_msk[:, :, :].rearrange("p b (g k) -> p b g k", k=4),
                                 r_scb[:, :, :].rearrange("p b (g k) -> p b g k", k=4),
                                 r_gm[:, :, 0:4].unsqueeze(3).to_broadcast([P, B, GROUPS, 4]), ALU.mult))
            link(V.tensor_scalar(r_msk[:, :, :], r_msk[:, :, :], 0.0, None, ALU.add))
            for b in range(B):
                last = V.max(r_v8[:, b, :], r_msk[:, b, :])
            link(last)
            link(V.tensor_copy(r_top4[:, :, 0:4], r_v8[:, :, 0:4]))
            for b in range(B):
                last = V.match_replace(r_mr2[:, b, :], r_top4[:, b, :], r_msk[:, b, :], BIG)
            link(last)
            link(V.tensor_scalar(r_mr2[:, :, :], r_mr2[:, :, :], BIGHALF, None, ALU.is_ge))
            link(V.tensor_tensor(r_mr2[:, :, :], r_mr2[:, :, :], r_sc[:, :, :], ALU.mult))
            link(V.tensor_reduce(r_sum[:, :], r_mr2[:, :, :], AX.X, ALU.add))
            link(V.tensor_scalar(r_sum[:, :], r_sum[:, :], 1e-20, None, ALU.add))
            link(V.reciprocal(r_sum[:, :], r_sum[:, :]))
            link(V.tensor_scalar(r_sum[:, :], r_sum[:, :], ROUTED_SCALE, None, ALU.mult))
            V.tensor_tensor(comb[:, :, :], r_mr2[:, :, :], r_sum[:, :].unsqueeze(2).to_broadcast([P, B, E]),
                            ALU.mult).then_inc(S("comb"), 1)
            for f in range(FB1):
                dve.wait_ge(S("f_tanh"), f + 1)
                gb = bank[:, 3 + f % 3, :]
                link(V.scalar_tensor_tensor(f_a[:, f % 2, :], f_t[:, f, :], 1.0, gb[:, 0:256], ALU.add, ALU.mult))
                V.scalar_tensor_tensor(f_h[:, f, :], f_a[:, f % 2, :], 0.5, gb[:, 256:512], ALU.mult, ALU.mult) \
                    .then_inc(S("f_inner"), 1)
            for b in range(B):
                dve.wait_ge(S("down_done"), 1)
                V.tensor_tensor(x[:, b, :], bank[:, b, 0:P], x[:, b, :], ALU.add).then_inc(S("y_ready"), 1)

        @block.tensor
        def _(pe):
            T = nc.tensor

            def mm(out_, lhsT, rhs, start=True, stop=True, **kw):
                return T.matmul(out_, lhsT=lhsT, rhs=rhs, start=start, stop=stop, **kw)

            def prep(l, c):
                k = 8 * l + c
                if l == 0:
                    pe.wait_ge(S(f"in_ctx{c // 2}"), 16)
                else:
                    pe.wait_ge(S("in_B"), 16)
                if k:
                    pe.wait_ge(S("k_rest1"), k)
                mm(bank[:, 6, :], WK[l], ctxT_s[:, c * 512:(c + 1) * 512]).then_inc(S("k_proj"), 1)
                if k:
                    pe.wait_ge(S("v_copied"), k)
                for i in range(4):
                    last = mm(bank[:, 7, i * P:(i + 1) * P], ctxT_s[:, c * 512 + i * P:c * 512 + (i + 1) * P], WV[l])
                last.then_inc(S("v_proj"), 1)

            def norm(ph):
                for b in range(B):
                    pe.wait_ge(S(f"{ph}_xn"), b + 1)
                    last = T.transpose(bank[:, 0, b * P:(b + 1) * P], xn[:, b, :], ident)
                last.then_inc(S(f"{ph}_xnTp"), 1)
                pe.wait_ge(S(f"{ph}_xnT"), 1)

            def query(l):
                mm(bank[:, 1, 0:256], WQ[l], xnT[:, :]).then_inc(S("q_proj"), 1)

            def cross(l, masked):
                g0 = NN * l

                def put(p_off, b, done, extra=None):
                    for s in range(PARTS):
                        last = mm(bank[:, 6, 0:P], selq[:, bass.ds(p_off + s * NP * P, P)],
                                  q_parts[:, s, b * P:(b + 1) * P], start=(s == 0),
                                  stop=(s == PARTS - 1 and extra is None))
                    if extra is not None:
                        last = mm(bank[:, 6, 0:P], extra, ident_b[:, :], start=False, stop=True)
                    last.then_inc(S(done), 1)

                def put_max(n, p_off, b):
                    put(p_off, b, "qm_rows")

                def put_exp(n, p_off, u):
                    pe.wait_ge(S("m_rows"), n + (g0 + 1))
                    put(p_off, u % 2, "qe_rows", m_rows[u % 2][:, :])

                def a_unit(n, u, w):
                    if w == 0:
                        pe.wait_ge(S("qm_put"), n + (g0 + 1))
                        pe.wait_ge(S(f"k_loaded{u % U}"), (n - u % U) * 24 + 96 * (g0 // U + 1))
                    if not (isinstance(n, int) and 4 * (n + g0) + w - 1 <= 0):
                        pe.wait_ge(S("max_done"), n * 4 + (4 * g0 + w - 1))
                    for h in range(2):
                        keys = slice((w % 2) * 1024 + h * 512, (w % 2) * 1024 + (h + 1) * 512)
                        o = bank[:, 2 * (w % 2) + h, :]
                        a = w // 2
                        last = mm(o, q_max[u % 2][:, a * P:(a + 1) * P], kpair[u % U][:, keys], stop=not masked)
                        if masked:
                            last = mm(o, ident, mask_s[:, u % 2, keys], start=False)
                    last.then_inc(S("a_done"), 1)

                def b_unit(n, u, j):
                    if j == 0:
                        pe.wait_ge(S("qe_put"), n + (g0 + 1))
                    pe.wait_ge(S("exp_done"), n * 8 + (C_EXP + 8 * g0 + j - 1))
                    for i in range(2):
                        c = 2 * j + i
                        o = bank[:, 4 + j % 2, i * 256:(i + 1) * 256]
                        last = mm(o, kpair[u % U][:, c * P:(c + 1) * P], q_exp[u % 2][:, :], stop=not masked)
                        if masked:
                            last = mm(o, mask_s[:, u % 2, c * P:(c + 1) * P],
                                      two_ident[:, :, :].rearrange("p a q -> p (a q)"), start=False)
                    last.then_inc(S("b_done"), 1)

                def pv_group(n, u, k):
                    if k == 0:
                        pe.wait_ge(S("v_pair"), n + (g0 + 1))
                        pe.wait_ge(S("o_taken"), n + (17 * l + 1))
                    pe.wait_ge(S("exp_done"), n * 8 + (C_EXP + 8 * g0 + 2 * k + 2))
                    for t in range(4):
                        c = 4 * k + t
                        last = mm(bank[t * 32:(t + 1) * 32, 7, 0:256], vpair[u % 2][:, c, :],
                                  probs[:, (c // 2) % 4, (c % 2) * 256:(c % 2 + 1) * 256],
                                  start=(k == 0), stop=(k == KB // 4 - 1))
                    last.then_inc(S("pv_done"), 1)

                def heads(n, u):
                    pe.wait_ge(S("o_taken"), n + (17 * l + 1))
                    pe.wait_ge(S("o_div"), n + (17 * l + C_DIV))
                    for a in range(2):
                        last = mm(bank[:, 6, 256 + 9 * a:256 + 9 * (a + 1)], o_sb[(u + 1) % 2][:, a * P:(a + 1) * P],
                                  sel_o[:, a, :])
                    last.then_inc(S("o_heads"), 1)

                def p_of(i, k):
                    return i * (2 * P) + (k // 2) * P

                def body(n, u, i, ahead, qm, qe):
                    for k in range(4):
                        b_unit(n, u, 2 * k)
                        b_unit(n, u, 2 * k + 1)
                        if ahead:
                            a_unit(n + 2, u + 2, k)
                        if k == 0 and qm:
                            pe.wait_ge(S("o_div"), n + (17 * l + C_DIV))
                            put_max(n + 3, p_of(i, u + 3), (u + 3) % 2)
                        if k:
                            pv_group(n, u, k - 1)
                        if k == 1 and qe:
                            pe.wait_ge(S("qm_put"), (n + (g0 + 4)) if qm else g0 + NN)
                            pe.wait_ge(S("o_div"), n + (17 * l + C_DIV))
                            put_exp(n + 1, p_of(i, u + 1), u + 1)
                        if k == 2:
                            pe.wait_ge(S("qe_put"), (n + (g0 + 2)) if qe else g0 + NN)
                            heads(n, u)
                    pv_group(n, u, 3)

                for n in range(3):
                    if n:
                        pe.wait_ge(S("qm_put"), g0 + n)
                    put_max(n, p_of(0, n), n % 2)
                    if n:
                        for w in range(4):
                            a_unit(n - 1, n - 1, w)
                pe.wait_ge(S("qm_put"), g0 + 3)
                put_exp(0, p_of(0, 0), 0)
                with pe.Fori(0, 3) as i:
                    for u in range(U):
                        body(i * U + u, u, i, True, True, True)
                for u in range(U):
                    n = 12 + u
                    body(n, u, 3, n + 2 < NN, n + 3 < NN, n + 1 < NN)
                heads(NN, 0)

            def cross_out(l):
                pe.wait_ge(S("o_div"), 17 * (l + 1) + C_DIV)
                pe.wait_ge(S("max_done"), 4 * NN * (l + 1))
                for b in range(B):
                    last = T.transpose(bank[:, 0, b * P:(b + 1) * P], onorm[:, b, 16:16 + P], ident)
                last.then_inc(S("oT_p"), 1)
                pe.wait_ge(S("oT"), l + 1)
                for b in range(B):
                    last = mm(bank[:, 1 + b, 0:P], oT[:, b * P:(b + 1) * P], WO[l], stop=(l == 0))
                    if l:
                        last = mm(bank[:, 1 + b, 0:P], ones_row, R_("bo1"), start=False)
                    last.then_inc(S("o_out"), 1)

            def self_attention(l):
                wq, wk, wv = (B_("aq"), B_("ak"), B_("av")) if l else (w_g[:, :], wk_eff[:, :], wv_eff[:, :])
                mm(bank[:, 1, 0:256], wq, xnT[:, :]).then_inc(S("q_self"), 1)
                mm(bank[:, 2, 0:256], wk, xnT[:, :]).then_inc(S("k_self"), 1)
                for b in range(B):
                    last = mm(bank[:, 3, b * P:(b + 1) * P], xnT[:, b * P:(b + 1) * P], wv, stop=(l == 0))
                    if l:
                        last = mm(bank[:, 3, b * P:(b + 1) * P], ones_row, R_("bv"), start=False)
                last.then_inc(S("v_self"), 1)
                pe.wait_ge(S("qT"), l + 1)

                def scores(w):
                    b, g = w // 4, w % 4
                    pe.wait_ge(S("kexp"), 2 * l + b + 1)
                    if w >= 2:
                        pe.wait_ge(S("s_copied"), 8 * l + w - 1)
                    mm(bank[:, 4 + w % 2, :], qT[:, b * P:(b + 1) * P],
                       kexp[:, b, 4 * g:4 * g + 4, :].rearrange("p h k -> p (h k)")).then_inc(S("s_done"), 1)

                def transposes(w):
                    pe.wait_ge(S("s_exp"), 8 * l + w + 1)
                    if w >= 2:
                        pe.wait_ge(S("p_copied"), 8 * l + w - 1)
                    for h in range(4):
                        last = T.transpose(bank[:, w % 2, h * P:(h + 1) * P], s_sb[:, w, h * P:(h + 1) * P], ident)
                    last.then_inc(S("p_trans"), 1)

                def values(w):
                    b, g = w // 4, w % 4
                    pe.wait_ge(S("p_copied"), 8 * l + w + 1)
                    for h in range(4):
                        hh = 4 * g + h
                        c = (b * H + hh) * (HD + 1)
                        last = mm(bank[:, 2, c:c + HD + 1], pT[:, w, h * P:(h + 1) * P], v9[:, b, hh, :])
                    last.then_inc(S("pv_self"), 1)

                for w in range(8 + 4):
                    if w < 8:
                        scores(w)
                        if l == 0:
                            prep(1, w)
                    if w >= 4:
                        if w == 4:
                            pe.wait_ge(S("kT"), l + 1)
                            pe.wait_ge(S("v9"), l + 1)
                        transposes(w - 4)
                        if w >= 5:
                            values(w - 5)
                values(7)
                if l:
                    pe.wait_ge(S("att"), 2)
                    for b in range(B):
                        last = T.transpose(bank[:, 3, b * P:(b + 1) * P], att[:, b, :], ident)
                    last.then_inc(S("attT_p"), 1)
                    pe.wait_ge(S("attT"), 1)
                    for b in range(B):
                        mm(bank[:, 4, b * P:(b + 1) * P], attT[:, b * P:(b + 1) * P], B_("aoT"), stop=False)
                        last = mm(bank[:, 4, b * P:(b + 1) * P], ones_row, R_("bout"), start=False)
                    last.then_inc(S("att_out"), 1)

            pe.wait_ge(S("in_A"), 16)
            pe.wait_ge(S("idents"), 1)
            norm("n0")
            query(0)
            pe.wait_ge(S("o_zero"), 1)
            for c in range(8):
                prep(0, c)
            pe.wait_ge(S("in_B"), 16)
            pe.wait_ge(S("in_C"), 16)
            mm(bank[:, 2, 0:P], C_("w_dq"), C_("w_uqT"))
            mm(bank[:, 2, P:2 * P], C_("w_uqT"), C_("w_dq"))
            mm(bank[0:64, 2, 2 * P:3 * P], B_("w_uv", 64), B_("w_oT")).then_inc(S("fold1"), 1)
            pe.wait_ge(S("fold1_c"), 1)
            mm(bank[:, 3, 0:P], C_("w_dkv"), v_eff[:, :])
            mm(bank[0:64, 3, P:2 * P], B_("w_uk", 64), w_gT[:, :]).then_inc(S("fold2"), 1)
            pe.wait_ge(S("fold2_c"), 1)
            mm(bank[:, 2, 0:P], C_("w_dkv"), k_effT[:, :]).then_inc(S("fold3"), 1)
            pe.wait_ge(S("fold3_c"), 1)
            pe.wait_ge(S("flag_rows"), 1)
            mm(bank[0:1, 3, 0:1], flag_f[:, 0:1], ones_col[:, :]).then_inc(S("flag_sum"), 1)
            pe.wait_ge(S("flag"), 1)
            pe.wait_ge(S("q_split"), 1)
            pe.wait_ge(S("in_selq"), 16)
            pe.wait_ge(S("m_zero"), 2)
            pe.wait_ge(S("v_copied"), 8)
            entries = pe.value_load(flag_i[0:1, 0:1], min_val=0, max_val=P * B * SK)
            with pe.If(entries > 0):
                cross(0, True)
            with pe.Else():
                cross(0, False)
            cross_out(0)
            norm("n1")
            self_attention(0)
            norm("n2")
            pe.wait_ge(S("in_sel"), 32)
            for b in range(B):
                mm(bank[:, 1, b * P:(b + 1) * P], xnT[:, b * P:(b + 1) * P], wsel[:, :], stop=False)
                last = mm(bank[:, 1, b * P:(b + 1) * P], ones_row, bsel[:, :], start=False)
            last.then_inc(S("ff_out"), 1)
            norm("n3")
            query(1)
            pe.wait_ge(S("q_split"), 2)
            pe.wait_ge(S("v_copied"), 16)
            cross(1, False)
            cross_out(1)
            norm("n4")
            self_attention(1)
            norm("n5")
            for b in range(B):
                mm(bank[:, 1, b * E:(b + 1) * E], xnT[:, b * P:(b + 1) * P], B_("router", E))
            mm(bank[:, 1, 64:64 + E], ones_row, R_("ebias", E)).then_inc(S("r_logits"), 1)
            pe.wait_ge(S("in_M"), 32)

            def inner(f):
                if f >= 3:
                    pe.wait_ge(S("f_inner"), f - 2)
                o = bank[:, 3 + f % 3, :]
                for k, c in (("gate", 0), ("up", 256)):
                    w = wM[:, PK_M[k] + f * P:PK_M[k] + (f + 1) * P]
                    last = mm(o[:, c:c + 256], w, xnT[:, :])
                last.then_inc(S("f_done"), 1)

            for f in range(3):
                inner(f)
            pe.wait_ge(S("comb"), 1)
            for b in range(B):
                last = T.transpose(bank[0:E, 2, b * P:(b + 1) * P], comb[:, b, :], ident)
            last.then_inc(S("combT_p"), 1)
            for f in range(3, FB1):
                inner(f)
            pe.wait_ge(S("combT"), 1)
            for f in range(FB // 2):
                if f >= 2:
                    pe.wait_ge(S("f_weight"), f - 1)
                for i in range(2):
                    last = mm(bank[:, 6 + f % 2, i * 256:(i + 1) * 256], rep[:, (2 * f + i) * P:(2 * f + i + 1) * P],
                              combT[:, :])
                last.then_inc(S("rep_done"), 1)
            pe.wait_ge(S("f_inner"), FB1)
            order = [FB] + list(range(FB))
            for k, f in enumerate(order):
                if f < FB:
                    pe.wait_ge(S("f_scaled"), f + 1)
                for b in range(B):
                    last = mm(bank[:, b, 0:P], f_h[:, f, b * P:(b + 1) * P],
                              wM[:, PK_M["down"] + f * P:PK_M["down"] + (f + 1) * P],
                              start=(k == 0), stop=(k == FB1 - 1))
            last.then_inc(S("down_done"), 1)


def v_scratch(t):
    return t[:, :, :].rearrange("p w n -> p (w n)")


def constants():
    one = np.uint16(0x3F80)
    selq = np.zeros((P, PARTS, NP, P), np.uint16)
    for h in range(H):
        for s, (_, qp) in enumerate(SLOTS):
            for d in range(HD):
                selq[h * HD + d, qp, h // 2, (h % 2) * HOFF + s * HD + d] = one
    krows = np.zeros((HOFF - HR, SK), np.uint16)
    krows[0:2] = one
    sel_o = np.zeros((P, 2, 9), np.float32)
    for t in range(4):
        for a in range(2):
            for d in range(HD):
                sel_o[t * 32 + a * HD + d, a, d] = 1.0
            sel_o[t * 32 + 2 * HD, a, HD] = 1.0
    hmask = np.zeros((P, H), np.float32)
    for h in range(H):
        hmask[h * HD:(h + 1) * HD, h] = 1.0
    rep = np.zeros((E, FB * P), np.float32)
    for e in range(E):
        rep[e, e * 64:(e + 1) * 64] = 1.0
    return selq.reshape(P, PARTS * NP * P), krows, sel_o.reshape(P, 18), hmask, rep


def kernel(**inp):
    import concourse.bacc as bacc
    from concourse.bass_utils import run_bass_kernel_spmd

    f = {k: np.ascontiguousarray(v) for k, v in inp.items()}
    selq, krows, sel_o, hmask, rep = constants()
    x = f["x"]
    ident = np.eye(P, dtype=np.float32)
    packA = np.concatenate([x[0], x[1], f["L0_xattn_wq"].reshape(P, P), f["L0_xattn_wk"].reshape(P, P),
                            f["L0_xattn_wv"].reshape(P, P), f["L0_xattn_wo"].reshape(P, P), ident], axis=1)
    aw = f["L1_attn_attn_w"].reshape(H, 3, HD, P)
    ab = f["L1_attn_attn_b"].reshape(H, 3, HD)
    aq, ak, av = (aw[:, i].reshape(P, P).T for i in range(3))
    bq, bk, bv = (ab[:, i].reshape(P) for i in range(3))
    packB = np.concatenate([f["L1_xattn_Wk"].T, f["L1_xattn_Wv"].T, f["L1_xattn_Wq"].T, f["L1_xattn_Wo"].T,
                            f["L0_attn_W_o"].T, f["L0_attn_W_uv"], f["L0_attn_W_uk"], aq, ak, av,
                            f["L1_attn_out_w"].T, f["L1_ffn_router_weight"].T, hmask, sel_o,
                            bq[:, None], bk[:, None]], axis=1)
    packC = np.concatenate([f["L0_attn_W_dq"], f["L0_attn_W_uq"].T, f["L0_attn_W_dkv"]], axis=1)
    packR = np.concatenate([f["L0_ffn_u"], f["L0_ffn_logits"], f["L1_xattn_bo"], bv, f["L1_attn_out_b"],
                            f["L1_ffn_e_bias"], np.ones(P, np.float32)])[None, :]
    down = np.concatenate([f["L1_ffn_down_w"].transpose(0, 2, 1).reshape(E * 64, P), f["L1_ffn_sh_down_w"].T], axis=0)
    packM = np.concatenate([f["L1_ffn_gate_w"].reshape(E * 64, P).T, f["L1_ffn_sh_gate_w"].T,
                            f["L1_ffn_up_w"].reshape(E * 64, P).T, f["L1_ffn_sh_up_w"].T,
                            down.reshape(FB1, P, P).transpose(1, 0, 2).reshape(P, FB1 * P)], axis=1)
    ctxT = f["ctx_1024"].reshape(B * SK, P).T
    ins = dict(packA=packA, packB=packB, packC=packC, packR=packR, packM=packM, ffnW=f["L0_ffn_W"], ffnb=f["L0_ffn_b"],
               mask=f["mask_Bx1xSxS2_ff0"], ctxT=ctxT, selq_d=selq, krows_d=krows, rep_d=rep)
    nc = bacc.Bacc("TRN2", target_bir_lowering=False, num_devices=1)
    arrays, args = {}, []
    for name, a in ins.items():
        a = np.ascontiguousarray(a)
        arrays["in_" + name] = a
        args.append(nc.dram_tensor("in_" + name, a.shape, mybir.dt.from_np(a.dtype), kind="ExternalInput").ap())
    out = nc.dram_tensor("out_0", (B, P, P), F32, kind="ExternalOutput").ap()
    perceiver_kernel(nc, *args, out)
    r = run_bass_kernel_spmd(nc, [arrays], core_ids=[0])
    return r.results[0]["out_0"]
```

```python
from contextlib import ExitStack

import numpy as np

import concourse.bass as bass
from concourse import mybir

F32 = mybir.dt.float32
BF16 = mybir.dt.bfloat16
U16 = mybir.dt.uint16
U32 = mybir.dt.uint32
I32 = mybir.dt.int32
ALU = mybir.AluOpType
ACT = mybir.ActivationFunctionType
AX = mybir.AxisListType

P = 128
B = 2
H = 16
HD = P // H
SK = 2048
NP = H // 2
NN = NP * B
KB = SK // P
PARTS = 3
SLOTS = [(0, 0), (0, 1), (0, 2), (1, 0), (1, 1), (2, 0)]
K_TIMES = [sum(kp == part for kp, _ in SLOTS) for part in range(PARTS)]
HR = len(SLOTS) * HD
HOFF = 64
VW = 17
VP = 32
U = 4
E = 16
FB = E * 64 // P
FB1 = FB + 1
GROUPS = 4
SCALE = float(HD) ** -0.5
BIG = 3.0e38
BIGHALF = 2.0e38
EPS = 1e-5
ROUTED_SCALE = 2.5

PK_A = dict(x=0, wq0=256, wk0=384, wv0=512, wo0=640, ident=768)
PK_A_W = 896
PK_B = dict(wk1=0, wv1=128, wq1=256, wo1=384, w_oT=512, w_uv=640, w_uk=704, aq=768, ak=896, av=1024,
            aoT=1152, router=1280, hsel=1296, sel_o=1300, bq=1318, bk=1319)
PK_B_W = 1320
PK_C = dict(w_dq=0, w_uqT=128, w_dkv=256)
PK_C_W = 384
PK_R = dict(u=0, logits=8, bo1=16, bv=144, bout=272, ebias=400, ones=416)
PK_R_W = 544
PK_M = dict(gate=0, up=1152, down=2304)
PK_M_W = 3456

K1_BANK = (0, 1, 2, 3, 4, 5, 4, 3)
K1_UNIT = 2

C_EXP = 4
C_PV = 16
C_DIV = 2


def perceiver_kernel(nc, packA, packB, packC, packR, packM, ffnW, ffnb, mask, ctxT, selq_d, rep_d, out):
    with ExitStack() as ctx:
        def sb(name, shape, dt=F32):
            return ctx.enter_context(nc.sbuf_tensor(name, shape, dt))

        sems = {}

        def S(name):
            if name not in sems:
                sems[name] = ctx.enter_context(nc.semaphore(name))
            return sems[name]

        bank = ctx.enter_context(nc.psum_tensor("bank", [P, 8, 512], F32))
        kscr = nc.dram_tensor("k_scratch", (2, B, PARTS, H, HD, SK), BF16, kind="Internal").ap()

        wA = sb("wA", [P, PK_A_W])
        wB = sb("wB", [P, PK_B_W])
        wC = sb("wC", [64, PK_C_W])
        wR = sb("wR", [1, PK_R_W])
        wM = sb("wM", [P, PK_M_W])
        ctxT_s = sb("ctxT_s", [P, B * SK])
        mask_s = sb("mask_s", [P, B, SK])
        selq = sb("selq", [P, PARTS * NP * P], BF16)
        rep = sb("rep", [E, FB * P])
        ident_b = sb("ident_b", [P, P], BF16)
        two_ident = sb("two_ident", [P, 2, P])

        kparts = sb("kparts", [P, PARTS, B * SK], BF16)
        k_rest = [sb(f"k_rest{i}", [P, 512]) for i in range(2)]
        v_all = [sb(f"v_all{l}", [P, NP, B, KB, VW]) for l in range(2)]

        kpair = [sb(f"kpair{i}", [P, SK], BF16) for i in range(U)]
        vpair = [sb(f"vpair{i}", [P, KB, VP]) for i in range(2)]
        q_f = sb("q_f", [P, B * P])
        q_rest = sb("q_rest", [P, B * P])
        q_parts = sb("q_parts", [P, PARTS, B * P], BF16)
        q_max = [sb(f"q_max{i}", [P, 2 * P], BF16) for i in range(2)]
        q_exp = [sb(f"q_exp{i}", [P, 2 * P], BF16) for i in range(2)]
        mx = [sb(f"mx{i}", [P, 2, 2]) for i in range(2)]
        negm = sb("negm", [P, 2])
        m_rows = [sb(f"m_rows{i}", [P, P], BF16) for i in range(2)]
        probs = sb("probs", [P, 4, 512])
        o_sb = [sb(f"o_sb{i}", [P, 2 * P]) for i in range(2)]
        o_rec = sb("o_rec", [P, 2])
        onorm = sb("onorm", [P, B, P])
        oT = sb("oT", [P, B * P])

        x = wA[:, 0:B * P].rearrange("p (b d) -> p b d", b=B)
        st = sb("st", [P, B, 6])
        mv = sb("mv", [P, B, 2])
        ve = sb("ve", [P, B])
        mhalf = sb("mhalf", [P, B])
        y0 = sb("y0", [P, B])
        yt = sb("yt", [P, B])
        rstd = sb("rstd", [P, B])
        xn = sb("xn", [P, B, P])
        xnT = sb("xnT", [P, B * P])

        qT = sb("qT", [P, B * P])
        kT = sb("kT", [P, B * P])
        dead_v = v_all[0][:, :, :, :, :].rearrange("p a b k w -> p (a b k w)")
        kexp = dead_v[:, 0:B * 4 * P].rearrange("p (b j k) -> p b j k", b=B, j=4)
        v32 = dead_v[:, B * 4 * P:B * 4 * P + B * H * VP].rearrange("p (b h w) -> p b h w", b=B, h=H)
        s_sb = sb("s_sb", [P, 2 * 4, 512])
        pT = mask_s[:, :, :].rearrange("p b (w n) -> p (b w) n", n=512)
        o_flat = sb("o_flat", [P, B, 512])
        s_mx = sb("s_mx", [P, 8, 4])
        s_rec = sb("s_rec", [P, B, H])
        att = sb("att", [P, B, P])
        attT = sb("attT", [P, B * P])
        w_g = sb("w_g", [P, P])
        w_gT = sb("w_gT", [P, P])
        k_effT = sb("k_effT", [64, P])
        v_eff = sb("v_eff", [64, P])
        wk_eff = sb("wk_eff", [P, P])
        wv_eff = sb("wv_eff", [P, P])

        gum = sb("gum", [1, 64])
        gidx = sb("gidx", [1, 8], U32)
        wsel = sb("wsel", [P, P])
        bsel = sb("bsel", [1, P])
        flag_f = sb("flag_f", [P, 2])
        flag_i = sb("flag_i", [1, 1], I32)
        ones_col = sb("ones_col", [P, 1])

        r_e = sb("r_e", [P, B, E])
        r_sc = sb("r_sc", [P, B, E])
        r_scb = sb("r_scb", [P, B, E])
        r_six = sb("r_six", [P, B * GROUPS, 6])
        r_gs = sb("r_gs", [P, B, 8])
        r_v8 = sb("r_v8", [P, B, 8])
        r_top = sb("r_top", [P, B, 8])
        r_top4 = sb("r_top4", [P, B, 8])
        r_mr = sb("r_mr", [P, B, 8])
        r_gm = sb("r_gm", [P, B, 8])
        r_msk = sb("r_msk", [P, B, E])
        r_mr2 = sb("r_mr2", [P, B, E])
        r_sum = sb("r_sum", [P, B])
        comb = sb("comb", [P, B, E])
        combT = sb("combT", [E, B * P])
        f_t = s_sb[:, :, :].rearrange("p w n -> p (w n)")[:, 0:FB1 * 256].rearrange("p (f t) -> p f t", t=256)
        f_h = dead_v[:, 0:FB1 * 256].rearrange("p (f t) -> p f t", t=256)
        f_a = kpair[0][:, :].bitcast(F32)[:, 0:512].rearrange("p (i t) -> p i t", i=2)
        f_c = pT[:, 0:4, :].rearrange("p w (i t) -> p (w i) t", t=256)

        def A_(k, w=P):
            return wA[:, PK_A[k]:PK_A[k] + w]

        def B_(k, w=P):
            return wB[:, PK_B[k]:PK_B[k] + w]

        def C_(k):
            return wC[:, PK_C[k]:PK_C[k] + P]

        def R_(k, w=P):
            return wR[0:1, PK_R[k]:PK_R[k] + w]

        ident = A_("ident")
        ones_row = R_("ones")
        sel_o = B_("sel_o", 18).rearrange("p (a c) -> p a c", a=2)
        WK = [A_("wk0"), B_("wk1")]
        WV = [A_("wv0"), B_("wv1")]
        WQ = [A_("wq0"), B_("wq1")]
        WO = [A_("wo0"), B_("wo1")]

        def r_bank(k):
            return 2 if k % 2 else 7

        def k_bank(l, c):
            return K1_BANK[c] if l else 6 + c % 2

        def v_bank(l, c):
            return 7 if l else 4 + c % 2

        block = ctx.enter_context(nc.Block())

        @block.sync
        def _(sp):
            sp.dma_start(wA[:, :], packA).then_inc(S("in_A"), 16)
            for c in range(4):
                sp.dma_start(ctxT_s[:, c * 1024:(c + 1) * 1024], ctxT[:, c * 1024:(c + 1) * 1024]) \
                    .then_inc(S(f"in_ctx{c}"), 16)
            sp.dma_start(selq[:, :].bitcast(U16), selq_d).then_inc(S("in_selq"), 16)
            sp.dma_start(wB[:, :], packB).then_inc(S("in_B"), 16)
            sp.dma_start(wC[:, :], packC).then_inc(S("in_C"), 16)
            for b in range(B):
                sp.dma_start(mask_s[:, b, :], mask[b, 0, :, :]).then_inc(S("in_mask"), 16)

            def store_k(l):
                for b in range(B):
                    sp.wait_ge(S("k_low"), 8 * l + 4 * b + 4)
                    for kp in range(PARTS):
                        sp.dma_start(kscr[l, b, kp, :, :, :],
                                     kparts[:, kp, b * SK:(b + 1) * SK]).then_inc(S(f"k_stored{b}"), 16)

            def load_k(l, p, b, u):
                for a in range(2):
                    row = a * HOFF
                    for kp in range(PARTS):
                        times = K_TIMES[kp]
                        src = kscr[l, b, kp, bass.ds(p * 2 + a, 1), :, :].rearrange("h d t -> (h d) t")
                        src = src.unsqueeze(0).to_broadcast([times, HD, SK])
                        sp.dma_start(kpair[u][row:row + times * HD, :], src).then_inc(S(f"k_loaded{u}"), 16)
                        row += times * HD

            def cross_k(l):
                for b in range(B):
                    sp.wait_ge(S(f"k_stored{b}"), 16 * PARTS * (l + 1))
                for n in range(3):
                    if l:
                        sp.wait_ge(S("b_done"), 8 * (NN * l + n - 3))
                    load_k(l, n // B, n % B, n)
                with sp.Fori(0, 3) as i:
                    for u in range(U):
                        sp.wait_ge(S("b_done"), i * 32 + (8 * (NN * l + u) + 1))
                        load_k(l, i * 2 + (u + 3) // 2, (u + 3) % B, (u + 3) % U)
                sp.wait_ge(S("b_done"), 8 * (NN * l + 12))
                load_k(l, NP - 1, 1, 3)

            store_k(0)
            sp.wait_ge(S("k_ones"), U)
            cross_k(0)
            sp.dma_start(wM[:, :], packM).then_inc(S("in_M"), 16)
            sp.dma_start(rep[:, :], rep_d).then_inc(S("in_M"), 16)
            store_k(1)
            sp.wait_ge(S("idx"), 1)
            idx = sp.value_load(gidx[0:1, 0:1], min_val=0, max_val=7)
            sp.dma_start(wsel[:, :], ffnW[bass.ds(idx, 1), :, :]).then_inc(S("in_sel"), 16)
            sp.dma_start(bsel[:, :], ffnb[bass.ds(idx, 1), :]).then_inc(S("in_sel"), 16)
            cross_k(1)
            sp.wait_ge(S("y_ready"), 2)
            sp.dma_start(out.rearrange("b t d -> t b d"), x).then_inc(S("out_done"), 16)
            sp.wait_ge(S("out_done"), 16)

        @block.gpsimd
        def _(pool):
            pool.memset(mhalf[:, :], -0.5).then_inc(S("mhalf"), 1)
            for i in range(2):
                pool.memset(vpair[i][:, :, :], 0.0).then_inc(S("v_zero"), 1)
            for i in range(U):
                pool.memset(kpair[i][:, :], 1.0).then_inc(S("k_ones"), 1)
            pool.wait_ge(S("in_A"), 16)
            pool.tensor_copy(ident_b[:, :], ident)
            for a in range(2):
                last = pool.tensor_copy(two_ident[:, a, :], ident)
            last.then_inc(S("idents"), 1)

            def norm(ph):
                pool.wait_ge(S(f"{ph}_var"), 1)
                pool.tensor_tensor(y0[:, :], ve[:, :], mhalf[:, :], ALU.pow).then_inc(S(f"{ph}_y0"), 1)

            def prep_k(l, c):
                pool.wait_ge(S("k_mid"), 8 * l + c + 1)
                cols = slice(c * 512, (c + 1) * 512)
                pool.tensor_tensor(kparts[:, 2, cols], k_rest[c % 2][:, :], kparts[:, 1, cols], ALU.subtract) \
                    .then_inc(S("k_low"), 1)

            def cross_v(l):
                pool.wait_ge(S("v_copied"), 8 * (l + 1))
                if l == 0:
                    pool.wait_ge(S("v_zero"), 4)

                def one(n, pp, u):
                    pool.wait_ge(S("pv_done"), n * 4 + (C_PV + 4 * NN * l - 4))
                    pool.tensor_copy(vpair[u % 2][:, :, 0:VW], pp).then_inc(S("v_pair"), 1)

                vl = v_all[l][:, :, :, :, :].rearrange("p a b k w -> p (a b k w)")
                with pool.Fori(0, 4) as i:
                    for u in range(U):
                        W = KB * VW
                        src = vl[:, bass.ds(i * (U * W) + u * W, W)].rearrange("p (k w) -> p k w", w=VW)
                        one(i * U + u, src, u)

            def causal(l):
                for w in range(8):
                    pool.wait_ge(S("s_copied"), 8 * l + w + 1)
                    v = s_sb[:, w, :].rearrange("p (h k) -> p h k", h=4)
                    pool.affine_select(out=v, in_=v, compare_op=ALU.is_ge, fill=(-BIG if l == 0 else -10000.0),
                                       base=0, pattern=[[0, 4], [-1, P]], channel_multiplier=1) \
                        .then_inc(S("s_masked"), 1)
                    if l == 0 and w == K1_UNIT:
                        prep_k(1, 7)

            pool.wait_ge(S("mhalf"), 1)
            norm("n0")
            for c in range(8):
                prep_k(0, c)
            cross_v(0)
            for c in range(4):
                prep_k(1, c)
            pool.wait_ge(S("v_pair"), NN)
            pool.memset(v32, 0.0).then_inc(S("v32_zero"), 1)
            pool.wait_ge(S("v32_zero"), 1)
            pool.memset(v32[:, :, :, HD:HD + 1], 1.0).then_inc(S("v32_ones"), 1)
            for c in range(4, 6):
                prep_k(1, c)
            norm("n1")
            prep_k(1, 6)
            causal(0)
            norm("n2")
            norm("n3")
            cross_v(1)
            norm("n4")
            causal(1)
            norm("n5")
            for f in range(FB):
                pool.wait_ge(S("f_inner"), f + 1)
                pool.wait_ge(S("f_weight"), f // 2 + 1)
                pool.tensor_tensor(f_h[:, f, :], f_h[:, f, :], f_c[:, f, :], ALU.mult).then_inc(S("f_scaled"), 1)

        @block.scalar
        def _(act):
            act.dma_start(wR[:, :], packR).then_inc(S("in_R"), 16)
            chain = [0]

            def link(ins):
                chain[0] += 1
                ins.then_inc(S("act_link"), 1)
                act.wait_ge(S("act_link"), chain[0])

            def copy(dst, src, scale=1.0):
                return act.activation(dst, src, ACT.Copy, scale=scale)

            def prep_k(l, c):
                k = 8 * l + c
                act.wait_ge(S("k_proj"), k + 1)
                if l and c % 4 == 0:
                    act.wait_ge(S(f"k_stored{c // 4}"), 16 * PARTS)
                copy(kparts[:, 0, c * 512:(c + 1) * 512], bank[:, k_bank(l, c), :]).then_inc(S("k_high"), 1)

            def prep_v(l, c):
                act.wait_ge(S("v_proj"), 8 * l + c + 1)
                b, kb = c // 4, (c % 4) * 4
                copy(v_all[l][:, :, b, kb:kb + 4, 0:16].rearrange("p a k w -> p k a w"),
                     bank[:, v_bank(l, c), :].rearrange("p (k a w) -> p k a w", k=4, a=NP)).then_inc(S("v_copied"), 1)

            def norm(ph):
                act.wait_ge(S(f"{ph}_xnTp"), 1)
                copy(xnT[:, :], bank[:, 0, 0:256]).then_inc(S(f"{ph}_xnT"), 1)

            def query(l):
                act.wait_ge(S("q_proj"), l + 1)
                copy(q_f[:, :], bank[:, 1, 0:256], SCALE).then_inc(S("q_f"), 1)
                act.wait_ge(S("q_f"), l + 1)
                copy(q_parts[:, 0, :], q_f[:, :]).then_inc(S("q_high"), 1)

            def cross(l):
                g0 = NN * l

                def put_q(dst):
                    copy(dst[0:64, 0:P], bank[0:64, 6, 0:P])
                    return copy(dst[64:P, P:2 * P], bank[64:P, 6, 0:P])

                def put_qm(n, u):
                    act.wait_ge(S("qm_rows"), n + (g0 + 1))
                    put_q(q_max[u % 2]).then_inc(S("qm_put"), 1)

                def put_qe(n, u):
                    act.wait_ge(S("qe_rows"), n + (g0 + 1))
                    put_q(q_exp[u % 2]).then_inc(S("qe_put"), 1)

                def take_o(n, u):
                    act.wait_ge(S("pv_done"), n * 4 + (C_PV + 4 * g0))
                    copy(o_sb[(u + 1) % 2][:, :], bank[:, 7, 0:256]).then_inc(S("o_taken"), 1)

                def exp_unit(n, j):
                    act.wait_ge(S("b_done"), n * 8 + (8 * g0 + j + 1))
                    if j % 2 == 0:
                        act.wait_ge(S("pv_done"), n * 4 + (C_PV + 4 * g0 + j // 2 - 1))
                    act.activation(probs[:, j % 4, :], bank[:, 4 + j % 2, :], ACT.Exp).then_inc(S("exp_done"), 1)

                def body(n, v, qm, qe, n_tail=None):
                    for j in range(8):
                        exp_unit(n, j)
                        if j == 1:
                            if qm:
                                put_qm(n + 3, v + 3)
                            take_o(n, v)
                        if j == 3 and qe:
                            put_qe(n + 1, v + 1)
                        if l == 0 and n_tail is not None and j in (2, 6):
                            prep_k(1, 2 * n_tail + j // 4)

                act.wait_ge(S("q_zero"), 4)
                for n in range(3):
                    if n == 2:
                        act.wait_ge(S("a_done"), 4 * (g0 + 1))
                    put_qm(n, n)
                put_qe(0, 0)
                for j in range(8):
                    exp_unit(0, j)
                    if j == 5:
                        put_qm(3, 3)
                put_qe(1, 1)
                with act.Fori(0, 3) as i:
                    for v in range(1, U + 1):
                        body(i * U + v, v, True, True)
                for v in range(1, U):
                    n = 12 + v
                    body(n, v, n + 3 < NN, n + 1 < NN, n - 14 if n >= 14 else None)
                take_o(NN, 0)
                act.wait_ge(S("oT_p"), l + 1)
                copy(oT[:, :], bank[:, 0, 0:256]).then_inc(S("oT"), 1)
                if l == 0:
                    for c in range(4, 7):
                        prep_k(1, c)

            def self_attention(l):
                act.wait_ge(S("v_self"), l + 1)
                act.wait_ge(S("v32_ones"), 1)
                copy(v32[:, :, :, 0:HD], bank[:, 3, 0:256].rearrange("p (b h d) -> p b h d", b=B, d=HD)) \
                    .then_inc(S("v32"), 1)

                def s_copy(w):
                    act.wait_ge(S("s_done"), 8 * l + w + 1)
                    copy(s_sb[:, w, :], bank[:, 4 + w % 4, :]).then_inc(S("s_copied"), 1)

                def s_exp(w):
                    act.wait_ge(S("s_sub"), 8 * l + w + 1)
                    act.activation(s_sb[:, w, :], s_sb[:, w, :], ACT.Exp).then_inc(S("s_exp"), 1)

                def p_copy(w):
                    act.wait_ge(S("p_trans"), 8 * l + w + 1)
                    copy(pT[:, w, :], bank[:, w % 2, :]).then_inc(S("p_copied1"), 1)

                for w in range(8 + 6):
                    if w < 8:
                        s_copy(w)
                    if l == 0 and w == K1_UNIT:
                        prep_k(1, 7)
                    if 3 <= w < 11:
                        s_exp(w - 3)
                    if w >= 6 and w % 2 == 0:
                        p_copy(w - 5)
                    if w in (10, 13):
                        b = w // 13
                        act.wait_ge(S("pv_self"), 8 * l + 4 * b + 4)
                        copy(o_flat[:, b, :], bank[:, 2 + 2 * b, :]).then_inc(S("o_flat"), 1)
                if l:
                    act.wait_ge(S("attT_p"), 1)
                    copy(attT[:, :], bank[:, 3, 0:256]).then_inc(S("attT"), 1)

            act.wait_ge(S("in_R"), 16)
            link(act.activation(gum[:, 0:8], R_("u", 8), ACT.Ln))
            act.activation(gum[:, 8:16], gum[:, 0:8], ACT.Ln, scale=-1.0).then_inc(S("gum_ln"), 1)
            act.wait_ge(S("gum_shift"), 1)
            act.activation(gum[:, 24:32], gum[:, 16:24], ACT.Exp).then_inc(S("gum_exp"), 1)
            act.wait_ge(S("gum_sum"), 1)
            act.activation(gum[:, 33:34], gum[:, 32:33], ACT.Ln).then_inc(S("gum_lse"), 1)
            for c in range(2):
                prep_k(0, c)
            norm("n0")
            query(0)
            for c in range(2, 8):
                prep_k(0, c)
            for c in range(8):
                prep_v(0, c)
            cross(0)
            norm("n1")
            self_attention(0)
            for c in range(3):
                prep_v(1, c)
            norm("n2")
            for c in range(3, 6):
                prep_v(1, c)
            norm("n3")
            for c in range(6, 8):
                prep_v(1, c)
            query(1)
            cross(1)
            norm("n4")
            self_attention(1)
            norm("n5")
            act.wait_ge(S("r_logits"), 1)
            act.activation(r_e[:, :, :], bank[:, 1, 0:2 * E].rearrange("p (b e) -> p b e", b=B),
                           ACT.Exp, scale=-1.0).then_inc(S("r_exp"), 1)
            def tanh(f):
                act.wait_ge(S("f_done"), f + 1)
                act.activation(f_t[:, f, :], bank[:, 3 + f % 4, 0:256], ACT.Tanh, scale=0.5) \
                    .then_inc(S("f_tanh"), 1)

            for f in range(4):
                tanh(f)
            act.wait_ge(S("combT_p"), 1)
            copy(combT[:, :], bank[0:E, 2, 0:256]).then_inc(S("combT"), 1)
            for f in range(4, FB1):
                tanh(f)
                if f - 4 < FB // 2:
                    act.wait_ge(S("rep_done"), f - 3)
                    copy(f_c[:, 2 * f - 8:2 * f - 6, :], bank[:, r_bank(f - 4), :].rearrange("p (i t) -> p i t", i=2)) \
                        .then_inc(S("f_weight"), 1)

        @block.vector
        def _(dve):
            chain = [0]

            def link(ins):
                chain[0] += 1
                ins.then_inc(S("dve_link"), 1)
                dve.wait_ge(S("dve_link"), chain[0])

            V = nc.vector
            for i in range(2):
                V.memset(q_max[i][:, :], 0.0).then_inc(S("q_zero"), 1)
                V.memset(q_exp[i][:, :], 0.0).then_inc(S("q_zero"), 1)
                V.memset(m_rows[i][:, :], 0.0).then_inc(S("m_zero"), 1)
                V.memset(v_all[i][:, :, :, :, VW - 1:VW], 1.0).then_inc(S("v_zero"), 1)
            V.memset(ones_col[:, :], 1.0).then_inc(S("exp_done"), C_EXP)
            V.memset(r_gs[:, :, :], -BIG).then_inc(S("o_div"), C_DIV)
            V.memset(r_top[:, :, :], BIG)
            V.memset(r_top4[:, :, :], BIG).then_inc(S("pv_done"), C_PV)
            dve.wait_ge(S("pv_done"), C_PV)

            def norm(ph, between=()):
                for b in range(B):
                    last = V.bn_stats(st[:, b, :], x[:, b, :])
                link(last)
                for b in range(B):
                    last = V.bn_aggr(mv[:, b, :], st[:, b, :])
                link(last)
                V.tensor_scalar(ve[:, :], mv[:, :, 1], EPS, None, ALU.add).then_inc(S(f"{ph}_var"), 1)
                for c in between:
                    prep_k(1, c)
                dve.wait_ge(S(f"{ph}_y0"), 1)
                link(V.tensor_tensor(yt[:, :], y0[:, :], y0[:, :], ALU.mult))
                link(V.tensor_tensor(yt[:, :], yt[:, :], ve[:, :], ALU.mult))
                link(V.tensor_scalar(yt[:, :], yt[:, :], -0.5, 1.5, ALU.mult, ALU.add))
                link(V.tensor_tensor(rstd[:, :], yt[:, :], y0[:, :], ALU.mult))
                for b in range(B):
                    V.tensor_scalar(xn[:, b, :], x[:, b, :], mv[:, b, 0:1], rstd[:, b:b + 1],
                                    ALU.subtract, ALU.mult).then_inc(S(f"{ph}_xn"), 1)

            def prep_k(l, c):
                k = 8 * l + c
                cols = slice(c * 512, (c + 1) * 512)
                dve.wait_ge(S("k_high"), k + 1)
                if k >= 2:
                    dve.wait_ge(S("k_low"), k - 1)
                V.tensor_tensor(k_rest[c % 2][:, :], bank[:, k_bank(l, c), :], kparts[:, 0, cols], ALU.subtract) \
                    .then_inc(S("k_rest1"), 1)
                dve.wait_ge(S("k_rest1"), k + 1)
                V.tensor_copy(kparts[:, 1, cols], k_rest[c % 2][:, :]).then_inc(S("k_mid"), 1)

            def query(l):
                dve.wait_ge(S("q_high"), l + 1)
                link(V.tensor_tensor(q_rest[:, :], q_f[:, :], q_parts[:, 0, :], ALU.subtract))
                link(V.tensor_copy(q_parts[:, 1, :], q_rest[:, :]))
                V.tensor_tensor(q_parts[:, 2, :], q_rest[:, :], q_parts[:, 1, :], ALU.subtract) \
                    .then_inc(S("q_split"), 1)

            def cross(l):
                g0 = NN * l

                def maxima(n, u, w):
                    dve.wait_ge(S("a_done"), n * 4 + (4 * g0 + w + 1))
                    V.tensor_reduce(mx[u % 2][:, w // 2, w % 2:w % 2 + 1],
                                    bank[:, 2 * (w % 2):2 * (w % 2) + 2, :], AX.XY, ALU.max) \
                        .then_inc(S("max_done"), 1)

                def rows(n, u):
                    m3 = m_rows[u % 2][:, :].rearrange("q (a r) -> q a r", a=2)
                    dve.wait_ge(S("max_done"), n * 4 + (4 * g0 + 4))
                    V.tensor_reduce(negm[:, :], mx[u % 2][:, :, :], AX.X, ALU.max, negate=True) \
                        .then_inc(S("neg_done"), 1)
                    dve.wait_ge(S("neg_done"), n + (g0 + 1))
                    V.tensor_copy(m3[:, :, HR], negm[:, :]).then_inc(S("m_high"), 1)
                    dve.wait_ge(S("m_high"), n + (g0 + 1))
                    V.tensor_tensor(m3[:, :, HR + 1], negm[:, :], m3[:, :, HR], ALU.subtract) \
                        .then_inc(S("m_rows"), 1)

                def divide(n, off, b):
                    ps = bank[:, 6, 256:256 + 18].rearrange("p (a c) -> p a c", a=2)
                    dve.wait_ge(S("o_heads"), n + 16 * l)
                    V.reciprocal(o_rec[:, :], ps[:, :, HD]).then_inc(S("o_rec"), 1)
                    dve.wait_ge(S("o_rec"), n + 16 * l)
                    dst = onorm[:, b, bass.ds(off, 16)].rearrange("p (a d) -> p a d", a=2)
                    V.tensor_tensor(dst, ps[:, :, 0:HD], o_rec[:, :].unsqueeze(2).to_broadcast([P, 2, HD]), ALU.mult) \
                        .then_inc(S("o_div"), 1)

                def body(n, v, i, ahead, more, n_tail=None):
                    if more:
                        rows(n + 1, v + 1)
                    for w in range(4):
                        if l == 0 and n_tail is not None and w % 2:
                            prep_k(1, 2 * n_tail + w // 2)
                        if ahead:
                            maxima(n + 2, v, w)
                        if w == 2:
                            divide(n, i * 32 + 16 * ((v - 1) // 2), (v - 1) % 2)

                for n in range(3):
                    for w in range(4):
                        maxima(n, n, w)
                    if n < 2:
                        rows(n, n)
                with dve.Fori(0, 3) as i:
                    for v in range(1, U + 1):
                        body(i * U + v, v, i, True, True)
                for v in range(1, U):
                    n = 12 + v
                    body(n, v, 3, n + 2 < NN, n + 1 < NN, n - 14 if n >= 14 else None)
                divide(NN, 16 * (NP - 1), 1)
                if l == 0:
                    for c in range(4, 6):
                        prep_k(1, c)
                for b in range(B):
                    dve.wait_ge(S("o_out"), 2 * l + b + 1)
                    last = V.tensor_tensor(x[:, b, :], bank[:, 1 + b, 0:P], x[:, b, :], ALU.add)
                link(last)

            def self_attention(l):
                bk, bq = (B_("bk", 1), B_("bq", 1)) if l else (0.0, 0.0)
                for b in range(B):
                    dve.wait_ge(S("k_self"), l + 1)
                    V.scalar_tensor_tensor(kexp[:, b, :, :],
                                           bank[:, 2, b * P:(b + 1) * P].unsqueeze(1).to_broadcast([P, 4, P]), bk,
                                           B_("hsel", 4).unsqueeze(2).to_broadcast([P, 4, P]), ALU.add, ALU.mult) \
                        .then_inc(S("kexp"), 1)
                    if b == 0:
                        dve.wait_ge(S("q_self"), l + 1)
                        V.tensor_scalar(qT[:, :], bank[:, 1, 0:256], bq, SCALE, ALU.add, ALU.mult) \
                            .then_inc(S("qT"), 1)

                def s_max(w):
                    dve.wait_ge(S("s_masked"), 8 * l + w + 1)
                    V.tensor_reduce(s_mx[:, w, :], s_sb[:, w, :].rearrange("p (h k) -> p h k", h=4), AX.X, ALU.max) \
                        .then_inc(S("s_max"), 1)

                def s_sub(w):
                    dve.wait_ge(S("s_max"), 8 * l + w + 1)
                    v = s_sb[:, w, :].rearrange("p (h k) -> p h k", h=4)
                    V.tensor_tensor(v, v, s_mx[:, w, :].unsqueeze(2).to_broadcast([P, 4, P]), ALU.subtract) \
                        .then_inc(S("s_sub"), 1)

                def p_copy(w):
                    dve.wait_ge(S("p_trans"), 8 * l + w + 1)
                    V.tensor_copy(pT[:, w, :], bank[:, w % 2, :]).then_inc(S("p_copied0"), 1)

                for w in range(8 + 4):
                    if w < 8:
                        s_max(w)
                        s_sub(w)
                    if l == 0 and w == K1_UNIT:
                        prep_k(1, 7)
                    if w >= 4 and w % 2 == 0:
                        p_copy(w - 4)
                for b in range(B):
                    dve.wait_ge(S("o_back"), 2 * l + b + 1)
                    o = bank[:, 5 + b, :].rearrange("p (h w) -> p h w", w=VP)
                    link(V.reciprocal(s_rec[:, b, :], o[:, :, HD]))
                    V.tensor_tensor(att[:, b, :].rearrange("p (h d) -> p h d", h=H), o[:, :, 0:HD],
                                    s_rec[:, b, :].unsqueeze(2).to_broadcast([P, H, HD]), ALU.mult) \
                        .then_inc(S("att"), 1)
                dve.wait_ge(S("att"), 2 * l + 2)
                if l == 0:
                    link(V.tensor_tensor(x[:, :, :], att[:, :, :], x[:, :, :], ALU.add))
                else:
                    dve.wait_ge(S("att_out"), 1)
                    link(V.tensor_tensor(x[:, :, :], bank[:, 4, 0:256].rearrange("p (b d) -> p b d", b=B), x[:, :, :],
                                         ALU.add))

            dve.wait_ge(S("in_R"), 16)
            link(V.tensor_reduce(gum[:, 34:35], R_("logits", 8), AX.X, ALU.max))
            V.tensor_scalar(gum[:, 16:24], R_("logits", 8), gum[:, 34:35], None, ALU.subtract) \
                .then_inc(S("gum_shift"), 1)
            dve.wait_ge(S("gum_exp"), 1)
            V.tensor_reduce(gum[:, 32:33], gum[:, 24:32], AX.X, ALU.add).then_inc(S("gum_sum"), 1)
            dve.wait_ge(S("gum_lse"), 1)
            link(V.tensor_scalar(gum[:, 36:44], gum[:, 16:24], gum[:, 33:34], None, ALU.subtract))
            dve.wait_ge(S("gum_ln"), 1)
            link(V.tensor_tensor(gum[:, 44:52], gum[:, 36:44], gum[:, 8:16], ALU.subtract))
            link(V.max(gum[:, 52:60], gum[:, 44:52]))
            V.max_index(gidx[:, :], gum[:, 52:60], gum[:, 44:52]).then_inc(S("idx"), 1)

            dve.wait_ge(S("in_A"), 16)
            norm("n0")
            for c in range(2):
                prep_k(0, c)
            query(0)
            for c in range(2, 8):
                prep_k(0, c)
            dve.wait_ge(S("in_mask"), 32)
            mflat = mask_s[:, :, :].rearrange("p b t -> p (b t)")
            V.tensor_scalar(v_scratch(s_sb), mflat, 0.0, None, ALU.not_equal, ALU.add, accum_out=flag_f[:, 0:1]) \
                .then_inc(S("flag_rows"), 1)
            dve.wait_ge(S("fold1"), 1)
            V.tensor_copy(w_g[:, :], bank[:, 2, 0:P])
            V.tensor_copy(w_gT[:, :], bank[:, 2, P:2 * P])
            V.tensor_copy(v_eff[:, :], bank[0:64, 2, 2 * P:3 * P]).then_inc(S("fold1_c"), 1)
            dve.wait_ge(S("fold2"), 1)
            V.tensor_copy(wv_eff[:, :], bank[:, 3, 0:P])
            V.tensor_copy(k_effT[:, :], bank[0:64, 3, P:2 * P]).then_inc(S("fold2_c"), 1)
            dve.wait_ge(S("fold3"), 1)
            V.tensor_copy(wk_eff[:, :], bank[:, 2, 0:P]).then_inc(S("fold3_c"), 1)
            dve.wait_ge(S("flag_sum"), 1)
            V.tensor_copy(flag_i[:, :], bank[0:1, 3, 0:1]).then_inc(S("flag"), 1)
            cross(0)
            norm("n1", (6,))
            self_attention(0)
            norm("n2")
            dve.wait_ge(S("ff_out"), 1)
            link(V.tensor_tensor(x[:, :, :], bank[:, 1, 0:256].rearrange("p (b d) -> p b d", b=B), x[:, :, :], ALU.add))
            norm("n3")
            query(1)
            cross(1)
            norm("n4")
            self_attention(1)
            norm("n5")
            dve.wait_ge(S("r_exp"), 1)
            link(V.tensor_scalar(r_e[:, :, :], r_e[:, :, :], 1.0, None, ALU.add))
            link(V.reciprocal(r_sc[:, :, :], r_e[:, :, :]))
            link(V.tensor_tensor(r_scb[:, :, :], r_sc[:, :, :],
                                 bank[:, 1, 64:64 + E].unsqueeze(1).to_broadcast([P, B, E]), ALU.add))
            g4 = r_scb[:, :, :].rearrange("p b (g k) -> p (b g) k", k=4)
            V.tensor_tensor(r_six[:, :, 0:3], g4[:, :, 0:3], g4[:, :, 1:4], ALU.add)
            V.tensor_tensor(r_six[:, :, 3:5], g4[:, :, 0:2], g4[:, :, 2:4], ALU.add)
            link(V.tensor_tensor(r_six[:, :, 5:6], g4[:, :, 0:1], g4[:, :, 3:4], ALU.add))
            link(V.tensor_reduce(r_gs[:, :, 0:4], r_six[:, :, :].rearrange("p (b g) s -> p b g s", b=B), AX.X, ALU.max))
            for b in range(B):
                last = V.max(r_v8[:, b, :], r_gs[:, b, :])
            link(last)
            link(V.tensor_copy(r_top[:, :, 0:2], r_v8[:, :, 0:2]))
            for b in range(B):
                last = V.match_replace(r_mr[:, b, :], r_top[:, b, :], r_gs[:, b, :], BIG)
            link(last)
            link(V.tensor_scalar(r_gm[:, :, :], r_mr[:, :, :], BIGHALF, None, ALU.is_ge))
            link(V.tensor_tensor(r_msk[:, :, :].rearrange("p b (g k) -> p b g k", k=4),
                                 r_scb[:, :, :].rearrange("p b (g k) -> p b g k", k=4),
                                 r_gm[:, :, 0:4].unsqueeze(3).to_broadcast([P, B, GROUPS, 4]), ALU.mult))
            link(V.tensor_scalar(r_msk[:, :, :], r_msk[:, :, :], 0.0, None, ALU.add))
            for b in range(B):
                last = V.max(r_v8[:, b, :], r_msk[:, b, :])
            link(last)
            link(V.tensor_copy(r_top4[:, :, 0:4], r_v8[:, :, 0:4]))
            for b in range(B):
                last = V.match_replace(r_mr2[:, b, :], r_top4[:, b, :], r_msk[:, b, :], BIG)
            link(last)
            link(V.tensor_scalar(r_mr2[:, :, :], r_mr2[:, :, :], BIGHALF, None, ALU.is_ge))
            link(V.tensor_tensor(r_mr2[:, :, :], r_mr2[:, :, :], r_sc[:, :, :], ALU.mult))
            link(V.tensor_reduce(r_sum[:, :], r_mr2[:, :, :], AX.X, ALU.add))
            link(V.tensor_scalar(r_sum[:, :], r_sum[:, :], 1e-20, None, ALU.add))
            link(V.reciprocal(r_sum[:, :], r_sum[:, :]))
            link(V.tensor_scalar(r_sum[:, :], r_sum[:, :], ROUTED_SCALE, None, ALU.mult))
            V.tensor_tensor(comb[:, :, :], r_mr2[:, :, :], r_sum[:, :].unsqueeze(2).to_broadcast([P, B, E]),
                            ALU.mult).then_inc(S("comb"), 1)
            for f in range(FB1 + 1):
                if f < FB1:
                    dve.wait_ge(S("f_tanh"), f + 1)
                    if f >= 2:
                        dve.wait_ge(S("f_inner"), f - 1)
                    V.scalar_tensor_tensor(f_a[:, f % 2, :], f_t[:, f, :], 1.0, bank[:, 3 + f % 4, 0:256],
                                           ALU.add, ALU.mult).then_inc(S("f_silu"), 1)
                if f:
                    dve.wait_ge(S("f_silu"), f)
                    V.scalar_tensor_tensor(f_h[:, f - 1, :], f_a[:, (f - 1) % 2, :], 0.5,
                                           bank[:, 3 + (f - 1) % 4, 256:512], ALU.mult, ALU.mult) \
                        .then_inc(S("f_inner"), 1)
            for b in range(B):
                dve.wait_ge(S("down_done"), 1)
                V.tensor_tensor(x[:, b, :], bank[:, b, 0:P], x[:, b, :], ALU.add).then_inc(S("y_ready"), 1)

        @block.tensor
        def _(pe):
            T = nc.tensor

            def mm(out_, lhsT, rhs, start=True, stop=True, **kw):
                return T.matmul(out_, lhsT=lhsT, rhs=rhs, start=start, stop=stop, **kw)

            def prep_k(l, c):
                k = 8 * l + c
                if l == 0:
                    pe.wait_ge(S(f"in_ctx{c // 2}"), 16)
                if c >= 2:
                    pe.wait_ge(S("k_rest1"), k - 1)
                mm(bank[:, k_bank(l, c), :], WK[l], ctxT_s[:, c * 512:(c + 1) * 512]).then_inc(S("k_proj"), 1)

            def prep_v(l, c):
                k = 8 * l + c
                if l or c >= 2:
                    pe.wait_ge(S("v_copied"), k if l else k - 1)
                for i in range(4):
                    last = mm(bank[:, v_bank(l, c), i * P:(i + 1) * P],
                              ctxT_s[:, c * 512 + i * P:c * 512 + (i + 1) * P], WV[l])
                last.then_inc(S("v_proj"), 1)

            def norm(ph):
                for b in range(B):
                    pe.wait_ge(S(f"{ph}_xn"), b + 1)
                    last = T.transpose(bank[:, 0, b * P:(b + 1) * P], xn[:, b, :], ident)
                last.then_inc(S(f"{ph}_xnTp"), 1)
                pe.wait_ge(S(f"{ph}_xnT"), 1)

            def query(l):
                mm(bank[:, 1, 0:256], WQ[l], xnT[:, :]).then_inc(S("q_proj"), 1)

            def cross(l, masked):
                g0 = NN * l

                def put(p_off, b, done, extra=None):
                    for s in range(PARTS):
                        last = mm(bank[:, 6, 0:P], selq[:, bass.ds(p_off + s * NP * P, P)],
                                  q_parts[:, s, b * P:(b + 1) * P], start=(s == 0),
                                  stop=(s == PARTS - 1 and extra is None))
                    if extra is not None:
                        last = mm(bank[:, 6, 0:P], extra, ident_b[:, :], start=False, stop=True)
                    last.then_inc(S(done), 1)

                def put_max(n, p_off, b):
                    put(p_off, b, "qm_rows")

                def put_exp(n, p_off, u):
                    pe.wait_ge(S("m_rows"), n + (g0 + 1))
                    put(p_off, u % 2, "qe_rows", m_rows[u % 2][:, :])

                def a_unit(n, u, w):
                    if w == 0:
                        pe.wait_ge(S("qm_put"), n + (g0 + 1))
                        pe.wait_ge(S(f"k_loaded{u % U}"), (n - u % U) * 24 + 96 * (g0 // U + 1))
                    if not (isinstance(n, int) and 4 * (n + g0) + w - 1 <= 0):
                        pe.wait_ge(S("max_done"), n * 4 + (4 * g0 + w - 1))
                    for h in range(2):
                        keys = slice((w % 2) * 1024 + h * 512, (w % 2) * 1024 + (h + 1) * 512)
                        o = bank[:, 2 * (w % 2) + h, :]
                        a = w // 2
                        last = mm(o, q_max[u % 2][:, a * P:(a + 1) * P], kpair[u % U][:, keys], stop=not masked)
                        if masked:
                            last = mm(o, ident, mask_s[:, u % 2, keys], start=False)
                    last.then_inc(S("a_done"), 1)

                def b_unit(n, u, j):
                    if j == 0:
                        pe.wait_ge(S("qe_put"), n + (g0 + 1))
                    pe.wait_ge(S("exp_done"), n * 8 + (C_EXP + 8 * g0 + j - 1))
                    for i in range(2):
                        c = 2 * j + i
                        o = bank[:, 4 + j % 2, i * 256:(i + 1) * 256]
                        last = mm(o, kpair[u % U][:, c * P:(c + 1) * P], q_exp[u % 2][:, :], stop=not masked)
                        if masked:
                            last = mm(o, mask_s[:, u % 2, c * P:(c + 1) * P],
                                      two_ident[:, :, :].rearrange("p a q -> p (a q)"), start=False)
                    last.then_inc(S("b_done"), 1)

                def pv_group(n, u, k):
                    if k == 0:
                        pe.wait_ge(S("v_pair"), n + (g0 + 1))
                        if not (isinstance(n, int) and n + l == 0):
                            pe.wait_ge(S("o_taken"), n + 16 * l)
                    pe.wait_ge(S("exp_done"), n * 8 + (C_EXP + 8 * g0 + 2 * k + 2))
                    for t in range(4):
                        c = 4 * k + t
                        last = mm(bank[t * 32:(t + 1) * 32, 7, 0:256], vpair[u % 2][:, c, :],
                                  probs[:, (c // 2) % 4, (c % 2) * 256:(c % 2 + 1) * 256],
                                  start=(k == 0), stop=(k == KB // 4 - 1))
                    last.then_inc(S("pv_done"), 1)

                def heads(n, u):
                    pe.wait_ge(S("o_taken"), n + 16 * l)
                    pe.wait_ge(S("o_div"), n + (16 * l + C_DIV - 1))
                    for a in range(2):
                        last = mm(bank[:, 6, 256 + 9 * a:256 + 9 * (a + 1)], o_sb[(u + 1) % 2][:, a * P:(a + 1) * P],
                                  sel_o[:, a, :])
                    last.then_inc(S("o_heads"), 1)

                def p_of(i, k):
                    return i * (2 * P) + (k // 2) * P

                def body(n, v, i, ahead, qm, qe, n_tail=None):
                    for k in range(4):
                        b_unit(n, v, 2 * k)
                        b_unit(n, v, 2 * k + 1)
                        if l == 0 and n_tail is not None and k % 2 == 0:
                            if n_tail == k == 0:
                                pe.wait_ge(S("max_done"), 4 * NN)
                            prep_k(1, 2 * n_tail + k // 2)
                        if ahead:
                            a_unit(n + 2, v + 2, k)
                        if k == 0:
                            if qm:
                                pe.wait_ge(S("o_div"), n + (16 * l + C_DIV - 1))
                                put_max(n + 3, p_of(i, v + 3), (v + 3) % 2)
                            pv_group(n - 1, v - 1, 3)
                        else:
                            pv_group(n, v, k - 1)
                        if k == 1 and qe:
                            pe.wait_ge(S("qm_put"), (n + (g0 + 4)) if qm else g0 + NN)
                            pe.wait_ge(S("o_div"), n + (16 * l + C_DIV - 1))
                            put_exp(n + 1, p_of(i, v + 1), v + 1)
                        if k == 2:
                            pe.wait_ge(S("qe_put"), (n + (g0 + 2)) if qe else g0 + NN)
                            heads(n, v)

                put_max(0, p_of(0, 0), 0)
                pe.wait_ge(S("qm_put"), g0 + 1)
                put_max(1, p_of(0, 1), 1)
                for w in range(4):
                    a_unit(0, 0, w)
                pe.wait_ge(S("qm_put"), g0 + 2)
                put_max(2, p_of(0, 2), 0)
                a_unit(1, 1, 0)
                pe.wait_ge(S("qm_put"), g0 + 3)
                put_exp(0, p_of(0, 0), 0)
                ahead = [(1, 1), (1, 2), (1, 3), (2, 0), (2, 1), (2, 2), (2, 3)]
                for k in range(4):
                    b_unit(0, 0, 2 * k)
                    b_unit(0, 0, 2 * k + 1)
                    m, w = ahead[2 * k]
                    a_unit(m, m, w)
                    if k:
                        pv_group(0, 0, k - 1)
                    if k == 2:
                        pe.wait_ge(S("qe_put"), g0 + 1)
                        put_max(3, p_of(0, 3), 1)
                    if k < 3:
                        m, w = ahead[2 * k + 1]
                        a_unit(m, m, w)
                pe.wait_ge(S("qm_put"), g0 + 4)
                put_exp(1, p_of(0, 1), 1)
                with pe.Fori(0, 3) as i:
                    for v in range(1, U + 1):
                        body(i * U + v, v, i, True, True, True)
                for v in range(1, U):
                    n = 12 + v
                    body(n, v, 3, n + 2 < NN, n + 3 < NN, n + 1 < NN, n - 14 if n >= 14 else None)
                pv_group(NN - 1, 1, 3)
                heads(NN, 0)

            def cross_out(l):
                pe.wait_ge(S("o_div"), 16 * (l + 1) + C_DIV)
                pe.wait_ge(S("max_done"), 4 * NN * (l + 1))
                if l == 0:
                    pe.wait_ge(S("k_rest1"), 8 + 3)
                for b in range(B):
                    last = T.transpose(bank[:, 0, b * P:(b + 1) * P], onorm[:, b, :], ident)
                last.then_inc(S("oT_p"), 1)
                if l == 0:
                    for c in range(4, 6):
                        prep_k(1, c)
                pe.wait_ge(S("oT"), l + 1)
                for b in range(B):
                    last = mm(bank[:, 1 + b, 0:P], oT[:, b * P:(b + 1) * P], WO[l], stop=(l == 0))
                    if l:
                        last = mm(bank[:, 1 + b, 0:P], ones_row, R_("bo1"), start=False)
                    last.then_inc(S("o_out"), 1)

            def self_attention(l):
                wq, wk, wv = (B_("aq"), B_("ak"), B_("av")) if l else (w_g[:, :], wk_eff[:, :], wv_eff[:, :])
                mm(bank[:, 2, 0:256], wk, xnT[:, :]).then_inc(S("k_self"), 1)
                mm(bank[:, 1, 0:256], wq, xnT[:, :]).then_inc(S("q_self"), 1)
                if l == 0:
                    pe.wait_ge(S("k_rest1"), 8 + 7)
                for b in range(B):
                    last = mm(bank[:, 3, b * P:(b + 1) * P], xnT[:, b * P:(b + 1) * P], wv, stop=(l == 0))
                    if l:
                        last = mm(bank[:, 3, b * P:(b + 1) * P], ones_row, R_("bv"), start=False)
                last.then_inc(S("v_self"), 1)
                pe.wait_ge(S("qT"), l + 1)

                def scores(w):
                    b, g = w // 4, w % 4
                    rows = slice(g * 32, (g + 1) * 32)
                    pe.wait_ge(S("kexp"), 2 * l + b + 1)
                    if w >= 4:
                        pe.wait_ge(S("s_copied"), 8 * l + w - 3)
                    mm(bank[:, 4 + g, :], qT[rows, b * P:(b + 1) * P],
                       kexp[rows, b, :, :].rearrange("p j k -> p (j k)")).then_inc(S("s_done"), 1)

                def transposes(w):
                    pe.wait_ge(S("s_exp"), 8 * l + w + 1)
                    if w >= 2:
                        pe.wait_ge(S(f"p_copied{w % 2}"), 4 * l + w // 2)
                    for h in range(4):
                        last = T.transpose(bank[:, w % 2, h * P:(h + 1) * P], s_sb[:, w, h * P:(h + 1) * P], ident)
                    last.then_inc(S("p_trans"), 1)

                def values(w):
                    b, g = w // 4, w % 4
                    pe.wait_ge(S(f"p_copied{w % 2}"), 4 * l + w // 2 + 1)
                    for t in range(4):
                        last = mm(bank[t * 32:(t + 1) * 32, 2 + 2 * b, g * P:(g + 1) * P], v32[:, b, 4 * g + t, :],
                                  pT[:, w, t * P:(t + 1) * P])
                    last.then_inc(S("pv_self"), 1)

                def back(b):
                    pe.wait_ge(S("o_flat"), 2 * l + b + 1)
                    for g in range(4):
                        last = T.transpose(bank[:, 5 + b, g * P:(g + 1) * P], o_flat[:, b, g * P:(g + 1) * P], ident)
                    last.then_inc(S("o_back"), 1)

                for w in range(8 + 4):
                    if w < 2:
                        for g in range(4):
                            scores(4 * w + g)
                    if l == 0 and w == 0:
                        pe.wait_ge(S("v32"), 1)
                        prep_k(1, 7)
                    if w >= 4:
                        if w == 4:
                            pe.wait_ge(S("v32"), l + 1)
                        transposes(w - 4)
                        if w >= 5:
                            values(w - 5)
                values(7)
                back(0)
                back(1)
                if l:
                    pe.wait_ge(S("att"), 4)
                    for b in range(B):
                        last = T.transpose(bank[:, 3, b * P:(b + 1) * P], att[:, b, :], ident)
                    last.then_inc(S("attT_p"), 1)
                    pe.wait_ge(S("attT"), 1)
                    for b in range(B):
                        mm(bank[:, 4, b * P:(b + 1) * P], attT[:, b * P:(b + 1) * P], B_("aoT"), stop=False)
                        last = mm(bank[:, 4, b * P:(b + 1) * P], ones_row, R_("bout"), start=False)
                    last.then_inc(S("att_out"), 1)

            pe.wait_ge(S("in_A"), 16)
            for c in range(2):
                prep_k(0, c)
            norm("n0")
            query(0)
            for c in range(2, 8):
                prep_k(0, c)
            for c in range(8):
                prep_v(0, c)
            pe.wait_ge(S("in_B"), 16)
            pe.wait_ge(S("in_C"), 16)
            mm(bank[:, 2, 0:P], C_("w_dq"), C_("w_uqT"))
            mm(bank[:, 2, P:2 * P], C_("w_uqT"), C_("w_dq"))
            mm(bank[0:64, 2, 2 * P:3 * P], B_("w_uv", 64), B_("w_oT")).then_inc(S("fold1"), 1)
            pe.wait_ge(S("fold1_c"), 1)
            mm(bank[:, 3, 0:P], C_("w_dkv"), v_eff[:, :])
            mm(bank[0:64, 3, P:2 * P], B_("w_uk", 64), w_gT[:, :]).then_inc(S("fold2"), 1)
            pe.wait_ge(S("fold2_c"), 1)
            mm(bank[:, 2, 0:P], C_("w_dkv"), k_effT[:, :]).then_inc(S("fold3"), 1)
            pe.wait_ge(S("fold3_c"), 1)
            pe.wait_ge(S("flag_rows"), 1)
            mm(bank[0:1, 3, 0:1], flag_f[:, 0:1], ones_col[:, :]).then_inc(S("flag_sum"), 1)
            pe.wait_ge(S("flag"), 1)
            pe.wait_ge(S("q_split"), 1)
            pe.wait_ge(S("in_selq"), 16)
            pe.wait_ge(S("m_zero"), 2)
            pe.wait_ge(S("v_copied"), 8)
            pe.wait_ge(S("idents"), 1)
            entries = pe.value_load(flag_i[0:1, 0:1], min_val=0, max_val=P * B * SK)
            with pe.If(entries > 0):
                cross(0, True)
            with pe.Else():
                cross(0, False)
            cross_out(0)
            prep_k(1, 6)
            norm("n1")
            self_attention(0)
            for c in range(3):
                prep_v(1, c)
            norm("n2")
            pe.wait_ge(S("in_sel"), 32)
            for b in range(B):
                mm(bank[:, 1, b * P:(b + 1) * P], xnT[:, b * P:(b + 1) * P], wsel[:, :], stop=False)
                last = mm(bank[:, 1, b * P:(b + 1) * P], ones_row, bsel[:, :], start=False)
            last.then_inc(S("ff_out"), 1)
            for c in range(3, 6):
                prep_v(1, c)
            norm("n3")
            for c in range(6, 8):
                prep_v(1, c)
            query(1)
            pe.wait_ge(S("q_split"), 2)
            pe.wait_ge(S("v_copied"), 16)
            cross(1, False)
            cross_out(1)
            norm("n4")
            self_attention(1)
            norm("n5")
            for b in range(B):
                mm(bank[:, 1, b * E:(b + 1) * E], xnT[:, b * P:(b + 1) * P], B_("router", E))
            mm(bank[:, 1, 64:64 + E], ones_row, R_("ebias", E)).then_inc(S("r_logits"), 1)
            pe.wait_ge(S("in_M"), 32)

            def inner(f):
                if f >= 4:
                    pe.wait_ge(S("f_inner"), f - 3)
                o = bank[:, 3 + f % 4, :]
                for k, c in (("gate", 0), ("up", 256)):
                    w = wM[:, PK_M[k] + f * P:PK_M[k] + (f + 1) * P]
                    last = mm(o[:, c:c + 256], w, xnT[:, :])
                last.then_inc(S("f_done"), 1)

            def weights(k):
                if k >= 2:
                    pe.wait_ge(S("f_weight"), k - 1)
                for i in range(2):
                    last = mm(bank[:, r_bank(k), i * 256:(i + 1) * 256],
                              rep[:, (2 * k + i) * P:(2 * k + i + 1) * P], combT[:, :])
                last.then_inc(S("rep_done"), 1)

            def down(f, first, final):
                pe.wait_ge(S("f_scaled"), f + 1) if f < FB else pe.wait_ge(S("f_inner"), FB1)
                for b in range(B):
                    last = mm(bank[:, b, 0:P], f_h[:, f, b * P:(b + 1) * P],
                              wM[:, PK_M["down"] + f * P:PK_M["down"] + (f + 1) * P], start=first, stop=final)
                return last

            for f in range(4):
                inner(f)
            pe.wait_ge(S("comb"), 1)
            for b in range(B):
                last = T.transpose(bank[0:E, 2, b * P:(b + 1) * P], comb[:, b, :], ident)
            last.then_inc(S("combT_p"), 1)
            pe.wait_ge(S("combT"), 1)
            for f in range(4, FB1):
                inner(f)
                if f - 4 < FB // 2:
                    weights(f - 4)
                if f >= 6:
                    down(f - 6, f == 6, False)
            for f in range(3, FB):
                down(f, False, False)
            last = down(FB, False, True)
            last.then_inc(S("down_done"), 1)


def v_scratch(t):
    return t[:, :, :].rearrange("p w n -> p (w n)")


def constants():
    one = np.uint16(0x3F80)
    selq = np.zeros((P, PARTS, NP, P), np.uint16)
    for h in range(H):
        for s, (_, qp) in enumerate(SLOTS):
            for d in range(HD):
                selq[h * HD + d, qp, h // 2, (h % 2) * HOFF + s * HD + d] = one
    sel_o = np.zeros((P, 2, 9), np.float32)
    for t in range(4):
        for a in range(2):
            for d in range(HD):
                sel_o[t * 32 + a * HD + d, a, d] = 1.0
            sel_o[t * 32 + 2 * HD, a, HD] = 1.0
    hsel = np.zeros((P, 4), np.float32)
    for h in range(H):
        hsel[h * HD:(h + 1) * HD, h % 4] = 1.0
    rep = np.zeros((E, FB * P), np.float32)
    for e in range(E):
        rep[e, e * 64:(e + 1) * 64] = 1.0
    return selq.reshape(P, PARTS * NP * P), sel_o.reshape(P, 18), hsel, rep


def kernel(**inp):
    import concourse.bacc as bacc
    from concourse.bass_utils import run_bass_kernel_spmd

    f = {k: np.ascontiguousarray(v) for k, v in inp.items()}
    selq, sel_o, hsel, rep = constants()
    x = f["x"]
    ident = np.eye(P, dtype=np.float32)
    packA = np.concatenate([x[0], x[1], f["L0_xattn_wq"].reshape(P, P), f["L0_xattn_wk"].reshape(P, P),
                            f["L0_xattn_wv"].reshape(P, P), f["L0_xattn_wo"].reshape(P, P), ident], axis=1)
    aw = f["L1_attn_attn_w"].reshape(H, 3, HD, P)
    ab = f["L1_attn_attn_b"].reshape(H, 3, HD)
    aq, ak, av = (aw[:, i].reshape(P, P).T for i in range(3))
    bq, bk, bv = (ab[:, i].reshape(P) for i in range(3))
    packB = np.concatenate([f["L1_xattn_Wk"].T, f["L1_xattn_Wv"].T, f["L1_xattn_Wq"].T, f["L1_xattn_Wo"].T,
                            f["L0_attn_W_o"].T, f["L0_attn_W_uv"], f["L0_attn_W_uk"], aq, ak, av,
                            f["L1_attn_out_w"].T, f["L1_ffn_router_weight"].T, hsel, sel_o,
                            bq[:, None], bk[:, None]], axis=1)
    packC = np.concatenate([f["L0_attn_W_dq"], f["L0_attn_W_uq"].T, f["L0_attn_W_dkv"]], axis=1)
    packR = np.concatenate([f["L0_ffn_u"], f["L0_ffn_logits"], f["L1_xattn_bo"], bv, f["L1_attn_out_b"],
                            f["L1_ffn_e_bias"], np.ones(P, np.float32)])[None, :]
    down = np.concatenate([f["L1_ffn_down_w"].transpose(0, 2, 1).reshape(E * 64, P), f["L1_ffn_sh_down_w"].T], axis=0)
    packM = np.concatenate([f["L1_ffn_gate_w"].reshape(E * 64, P).T, f["L1_ffn_sh_gate_w"].T,
                            f["L1_ffn_up_w"].reshape(E * 64, P).T, f["L1_ffn_sh_up_w"].T,
                            down.reshape(FB1, P, P).transpose(1, 0, 2).reshape(P, FB1 * P)], axis=1)
    ctxT = f["ctx_1024"].reshape(B * SK, P).T
    ins = dict(packA=packA, packB=packB, packC=packC, packR=packR, packM=packM, ffnW=f["L0_ffn_W"], ffnb=f["L0_ffn_b"],
               mask=f["mask_Bx1xSxS2_ff0"], ctxT=ctxT, selq_d=selq, rep_d=rep)
    nc = bacc.Bacc("TRN2", target_bir_lowering=False, num_devices=1)
    arrays, args = {}, []
    for name, a in ins.items():
        a = np.ascontiguousarray(a)
        arrays["in_" + name] = a
        args.append(nc.dram_tensor("in_" + name, a.shape, mybir.dt.from_np(a.dtype), kind="ExternalInput").ap())
    out = nc.dram_tensor("out_0", (B, P, P), F32, kind="ExternalOutput").ap()
    perceiver_kernel(nc, *args, out)
    r = run_bass_kernel_spmd(nc, [arrays], core_ids=[0])
    return r.results[0]["out_0"]
```

```python
from contextlib import ExitStack

import numpy as np

import concourse.bass as bass
from concourse import mybir

F32 = mybir.dt.float32
BF16 = mybir.dt.bfloat16
U16 = mybir.dt.uint16
U32 = mybir.dt.uint32
I32 = mybir.dt.int32
ALU = mybir.AluOpType
ACT = mybir.ActivationFunctionType
AX = mybir.AxisListType

P = 128
B = 2
H = 16
HD = P // H
SK = 2048
NP = H // 2
NN = NP * B
KB = SK // P
PARTS = 3
SLOTS = [(0, 0), (0, 1), (0, 2), (1, 0), (1, 1), (2, 0)]
K_TIMES = [sum(kp == part for kp, _ in SLOTS) for part in range(PARTS)]
HR = len(SLOTS) * HD
HOFF = 64
VW = 17
VP = 32
U = 4
E = 16
FB = E * 64 // P
FB1 = FB + 1
GROUPS = 4
SCALE = float(HD) ** -0.5
BIG = 3.0e38
BIGHALF = 2.0e38
EPS = 1e-5
ROUTED_SCALE = 2.5

PK_A = dict(x=0, wq0=256, wk0=384, wv0=512, wo0=640, ident=768)
PK_A_W = 896
PK_B = dict(wk1=0, wv1=128, wq1=256, wo1=384, w_oT=512, w_uv=640, w_uk=704, aq=768, ak=896, av=1024,
            aoT=1152, router=1280, hsel=1296, qsel=1300, sel_o=1304, bq=1322, bk=1323)
PK_B_W = 1324
PK_C = dict(w_dq=0, w_uqT=128, w_dkv=256)
PK_C_W = 384
PK_R = dict(u=0, logits=8, bo1=16, bv=144, bout=272, ebias=400, ones=416)
PK_R_W = 544
PK_M = dict(gate=0, up=1152, down=2304)
PK_M_W = 3456

K1_BANK = (0, 1, 2, 3, 2, 3, 2, 3)
SUB_POOL = (1, 3, 5)

C_EXP = 4
C_PV = 16
C_DIV = 2


def perceiver_kernel(nc, packA, packB, packC, packR, packM, ffnW, ffnb, mask, ctxT, selq_d, rep_d, out):
    with ExitStack() as ctx:
        def sb(name, shape, dt=F32):
            return ctx.enter_context(nc.sbuf_tensor(name, shape, dt))

        sems = {}

        def S(name):
            if name not in sems:
                sems[name] = ctx.enter_context(nc.semaphore(name))
            return sems[name]

        bank = ctx.enter_context(nc.psum_tensor("bank", [P, 8, 512], F32))
        kscr = nc.dram_tensor("k_scratch", (2, B, PARTS, H, HD, SK), BF16, kind="Internal").ap()

        wA = sb("wA", [P, PK_A_W])
        wB = sb("wB", [P, PK_B_W])
        wC = sb("wC", [64, PK_C_W])
        wR = sb("wR", [1, PK_R_W])
        wM = sb("wM", [P, PK_M_W])
        ctxT_s = sb("ctxT_s", [P, B * SK])
        mask_s = sb("mask_s", [P, B, SK])
        selq = sb("selq", [P, PARTS * NP * P], BF16)
        rep = sb("rep", [E, FB * P])
        ident_b = sb("ident_b", [P, P], BF16)
        two_ident = sb("two_ident", [P, 2, P])

        kparts = sb("kparts", [P, PARTS, B * SK], BF16)
        k_rest = [sb(f"k_rest{i}", [P, 512]) for i in range(2)]
        v_all = [sb(f"v_all{l}", [P, NP, B, KB, VW]) for l in range(2)]

        kpair = [sb(f"kpair{i}", [P, SK], BF16) for i in range(U)]
        vpair = [sb(f"vpair{i}", [P, KB, VP]) for i in range(2)]
        q_f = sb("q_f", [P, B * P])
        q_rest = sb("q_rest", [P, B * P])
        q_parts = sb("q_parts", [P, PARTS, B * P], BF16)
        q_max = [sb(f"q_max{i}", [P, 2 * P], BF16) for i in range(2)]
        q_exp = [sb(f"q_exp{i}", [P, 2 * P], BF16) for i in range(2)]
        mx = [sb(f"mx{i}", [P, 2, 2]) for i in range(2)]
        negm = sb("negm", [P, 2])
        m_rows = [sb(f"m_rows{i}", [P, P], BF16) for i in range(2)]
        probs = sb("probs", [P, 4, 512])
        o_sb = [sb(f"o_sb{i}", [P, 2 * P]) for i in range(2)]
        o_rec = sb("o_rec", [P, 2])
        onorm = sb("onorm", [P, B, P])
        oT = sb("oT", [P, B * P])

        x = wA[:, 0:B * P].rearrange("p (b d) -> p b d", b=B)
        st = sb("st", [P, B, 6])
        mv = sb("mv", [P, B, 2])
        ve = sb("ve", [P, B])
        mhalf = sb("mhalf", [P, B])
        y0 = sb("y0", [P, B])
        yt = sb("yt", [P, B])
        rstd = sb("rstd", [P, B])
        xn = sb("xn", [P, B, P])
        xnT = sb("xnT", [P, B * P])

        dead_v = v_all[0][:, :, :, :, :].rearrange("p a b k w -> p (a b k w)")
        kexp = dead_v[:, 0:B * 4 * P].rearrange("p (b j k) -> p b j k", b=B, j=4)
        qexp = dead_v[:, B * 4 * P + B * H * VP:2 * B * 4 * P + B * H * VP].rearrange("p (b g q) -> p b g q", b=B, g=4)
        v32 = dead_v[:, B * 4 * P:B * 4 * P + B * H * VP].rearrange("p (b h w) -> p b h w", b=B, h=H)
        s_sb = sb("s_sb", [P, 2 * 4, 512])
        pT = mask_s[:, :, :].rearrange("p b (w n) -> p (b w) n", n=512)
        o_flat = sb("o_flat", [P, B, 512])
        s_mx = sb("s_mx", [P, 8, 4])
        s_rec = sb("s_rec", [P, B, H])
        att = sb("att", [P, B, P])
        attT = sb("attT", [P, B * P])
        w_g = sb("w_g", [P, P])
        w_gT = sb("w_gT", [P, P])
        k_effT = sb("k_effT", [64, P])
        v_eff = sb("v_eff", [64, P])
        wk_eff = sb("wk_eff", [P, P])
        wv_eff = sb("wv_eff", [P, P])

        gum = sb("gum", [1, 64])
        gidx = sb("gidx", [1, 8], U32)
        wsel = sb("wsel", [P, P])
        bsel = sb("bsel", [1, P])
        flag_f = sb("flag_f", [P, 2])
        flag_i = sb("flag_i", [1, 1], I32)
        ones_col = sb("ones_col", [P, 1])

        r_e = sb("r_e", [P, B, E])
        r_sc = sb("r_sc", [P, B, E])
        r_scb = sb("r_scb", [P, B, E])
        r_six = sb("r_six", [P, B * GROUPS, 6])
        r_gs = sb("r_gs", [P, B, 8])
        r_v8 = sb("r_v8", [P, B, 8])
        r_top = sb("r_top", [P, B, 8])
        r_top4 = sb("r_top4", [P, B, 8])
        r_mr = sb("r_mr", [P, B, 8])
        r_gm = sb("r_gm", [P, B, 8])
        r_msk = sb("r_msk", [P, B, E])
        r_mr2 = sb("r_mr2", [P, B, E])
        r_sum = sb("r_sum", [P, B])
        comb = sb("comb", [P, B, E])
        combT = sb("combT", [E, B * P])
        f_t = s_sb[:, :, :].rearrange("p w n -> p (w n)")[:, 0:FB1 * 256].rearrange("p (f t) -> p f t", t=256)
        f_h = dead_v[:, 0:FB1 * 256].rearrange("p (f t) -> p f t", t=256)
        f_a = kpair[0][:, :].bitcast(F32)[:, 0:512].rearrange("p (i t) -> p i t", i=2)
        f_c = pT[:, 0:4, :].rearrange("p w (i t) -> p (w i) t", t=256)

        def A_(k, w=P):
            return wA[:, PK_A[k]:PK_A[k] + w]

        def B_(k, w=P):
            return wB[:, PK_B[k]:PK_B[k] + w]

        def C_(k):
            return wC[:, PK_C[k]:PK_C[k] + P]

        def R_(k, w=P):
            return wR[0:1, PK_R[k]:PK_R[k] + w]

        ident = A_("ident")
        ones_row = R_("ones")
        sel_o = B_("sel_o", 18).rearrange("p (a c) -> p a c", a=2)
        WK = [A_("wk0"), B_("wk1")]
        WV = [A_("wv0"), B_("wv1")]
        WQ = [A_("wq0"), B_("wq1")]
        WO = [A_("wo0"), B_("wo1")]

        def r_bank(k):
            return 2 if k % 2 else 7

        def k_bank(l, c):
            return K1_BANK[c] if l else 4 + c % 4

        def v_bank(l, c):
            return 7 - c % 2 if l else 2 + c % 2

        block = ctx.enter_context(nc.Block())

        @block.sync
        def _(sp):
            sp.dma_start(wA[:, :], packA).then_inc(S("in_A"), 16)
            for c in range(4):
                sp.dma_start(ctxT_s[:, c * 1024:(c + 1) * 1024], ctxT[:, c * 1024:(c + 1) * 1024]) \
                    .then_inc(S(f"in_ctx{c}"), 16)
            for b in range(B):
                sp.dma_start(mask_s[:, b, :], mask[b, 0, :, :]).then_inc(S("in_mask"), 16)

            def store_k(l, b):
                sp.wait_ge(S("k_low"), 8 * l + 4 * b + 4)
                for kp in range(PARTS):
                    sp.dma_start(kscr[l, b, kp, :, :, :],
                                 kparts[:, kp, b * SK:(b + 1) * SK]).then_inc(S(f"k_stored{b}"), 16)

            def load_k(l, p, b, u):
                for a in range(2):
                    row = a * HOFF
                    for kp in range(PARTS):
                        times = K_TIMES[kp]
                        src = kscr[l, b, kp, bass.ds(p * 2 + a, 1), :, :].rearrange("h d t -> (h d) t")
                        src = src.unsqueeze(0).to_broadcast([times, HD, SK])
                        sp.dma_start(kpair[u][row:row + times * HD, :], src).then_inc(S(f"k_loaded{u}"), 16)
                        row += times * HD

            def first_k(l, n):
                sp.wait_ge(S(f"k_stored{n % B}"), 16 * PARTS * (l + 1))
                if l:
                    sp.wait_ge(S("b_done"), 8 * (NN * l + n - 3))
                else:
                    sp.wait_ge(S("k_ones"), U)
                load_k(l, n // B, n % B, n)

            def cross_k(l):
                with sp.Fori(0, 3) as i:
                    for u in range(U):
                        sp.wait_ge(S("b_done"), i * 32 + (8 * (NN * l + u) + 1))
                        load_k(l, i * 2 + (u + 3) // 2, (u + 3) % B, (u + 3) % U)
                sp.wait_ge(S("b_done"), 8 * (NN * l + 12))
                load_k(l, NP - 1, 1, 3)

            store_k(0, 0)
            sp.dma_start(selq[:, :].bitcast(U16), selq_d).then_inc(S("in_selq"), 16)
            store_k(0, 1)
            for n in range(2):
                first_k(0, n)
            sp.dma_start(wB[:, :], packB).then_inc(S("in_B"), 16)
            first_k(0, 2)
            sp.dma_start(wC[:, :], packC).then_inc(S("in_C"), 16)
            cross_k(0)
            sp.dma_start(wM[:, :], packM).then_inc(S("in_M"), 16)
            sp.dma_start(rep[:, :], rep_d).then_inc(S("in_M"), 16)
            sp.wait_ge(S("idx"), 1)
            idx = sp.value_load(gidx[0:1, 0:1], min_val=0, max_val=7)
            sp.dma_start(wsel[:, :], ffnW[bass.ds(idx, 1), :, :]).then_inc(S("in_sel"), 16)
            sp.dma_start(bsel[:, :], ffnb[bass.ds(idx, 1), :]).then_inc(S("in_sel"), 16)
            store_k(1, 0)
            for n in (0, 2):
                first_k(1, n)
            store_k(1, 1)
            first_k(1, 1)
            cross_k(1)
            sp.wait_ge(S("y_ready"), 2)
            sp.dma_start(out.rearrange("b t d -> t b d"), x).then_inc(S("out_done"), 16)
            sp.wait_ge(S("out_done"), 16)

        @block.gpsimd
        def _(pool):
            pool.memset(mhalf[:, :], -0.5).then_inc(S("mhalf"), 1)
            two_ones = float(np.array([0x3F80, 0x3F80], np.uint16).view(np.float32)[0])
            for i in range(U):
                pool.memset(kpair[i][:, :].bitcast(F32), two_ones).then_inc(S("k_ones"), 1)
            for i in range(2):
                pool.memset(vpair[i][:, :, :], 0.0).then_inc(S("v_zero"), 1)

            def norm(ph):
                pool.wait_ge(S(f"{ph}_var"), 1)
                pool.tensor_tensor(y0[:, :], ve[:, :], mhalf[:, :], ALU.pow).then_inc(S(f"{ph}_y0"), 1)

            def prep_k(l, c):
                pool.wait_ge(S("k_mid"), 8 * l + c + 1)
                cols = slice(c * 512, (c + 1) * 512)
                pool.tensor_tensor(kparts[:, 2, cols], k_rest[c % 2][:, :], kparts[:, 1, cols], ALU.subtract) \
                    .then_inc(S("k_low"), 1)

            def cross_v(l):
                pool.wait_ge(S("v_copied"), 8 * (l + 1))
                if l == 0:
                    pool.wait_ge(S("v_zero"), 4)

                def one(n, pp, u):
                    pool.wait_ge(S("pv_done"), n * 4 + (C_PV + 4 * NN * l - 4))
                    pool.tensor_copy(vpair[u % 2][:, :, 0:VW], pp).then_inc(S("v_pair"), 1)

                vl = v_all[l][:, :, :, :, :].rearrange("p a b k w -> p (a b k w)")
                with pool.Fori(0, 4) as i:
                    for u in range(U):
                        W = KB * VW
                        src = vl[:, bass.ds(i * (U * W) + u * W, W)].rearrange("p (k w) -> p k w", w=VW)
                        one(i * U + u, src, u)

            def causal(l):
                for w in range(8):
                    pool.wait_ge(S("s_copied"), 8 * l + w + 1)
                    v = s_sb[:, w, :].rearrange("p (h k) -> p h k", h=4)
                    pool.affine_select(out=v, in_=v, compare_op=ALU.is_ge, fill=(-BIG if l == 0 else -10000.0),
                                       base=0, pattern=[[0, 4], [-1, P]], channel_multiplier=1) \
                        .then_inc(S("s_masked"), 1)
                    if w - 1 in SUB_POOL:
                        pool.wait_ge(S("s_max"), 8 * l + w)
                        v = s_sb[:, w - 1, :].rearrange("p (h k) -> p h k", h=4)
                        pool.tensor_tensor(v, v, s_mx[:, w - 1, :].unsqueeze(2).to_broadcast([P, 4, P]),
                                           ALU.subtract).then_inc(S("s_sub_pool"), 1)

            pool.wait_ge(S("mhalf"), 1)
            norm("n0")
            for c in range(8):
                prep_k(0, c)
            pool.wait_ge(S("in_A"), 16)
            pool.tensor_copy(ident_b[:, :], ident)
            for a in range(2):
                last = pool.tensor_copy(two_ident[:, a, :], ident)
            last.then_inc(S("idents"), 1)
            cross_v(0)
            for c in range(4):
                prep_k(1, c)
            pool.wait_ge(S("v_pair"), NN)
            pool.memset(v32, 0.0).then_inc(S("v32_zero"), 1)
            pool.wait_ge(S("v32_zero"), 1)
            pool.memset(v32[:, :, :, HD:HD + 1], 1.0).then_inc(S("v32_ones"), 1)
            norm("n1")
            causal(0)
            norm("n2")
            for c in range(4, 6):
                prep_k(1, c)
            norm("n3")
            for c in range(6, 8):
                prep_k(1, c)
            cross_v(1)
            norm("n4")
            causal(1)
            norm("n5")
            for f in range(FB):
                pool.wait_ge(S("f_inner"), f + 1)
                pool.wait_ge(S("f_weight"), f // 2 + 1)
                pool.tensor_tensor(f_h[:, f, :], f_h[:, f, :], f_c[:, f, :], ALU.mult).then_inc(S("f_scaled"), 1)

        @block.scalar
        def _(act):
            act.dma_start(wR[:, :], packR).then_inc(S("in_R"), 16)
            chain = [0]

            def link(ins):
                chain[0] += 1
                ins.then_inc(S("act_link"), 1)
                act.wait_ge(S("act_link"), chain[0])

            def copy(dst, src, scale=1.0):
                return act.activation(dst, src, ACT.Copy, scale=scale)

            def prep_k(l, c):
                k = 8 * l + c
                act.wait_ge(S("k_proj"), k + 1)
                if l and c % 4 == 0:
                    act.wait_ge(S(f"k_stored{c // 4}"), 16 * PARTS)
                copy(kparts[:, 0, c * 512:(c + 1) * 512], bank[:, k_bank(l, c), :]).then_inc(S("k_high"), 1)

            def prep_v(l, c):
                act.wait_ge(S("v_proj"), 8 * l + c + 1)
                b, kb = c // 4, (c % 4) * 4
                copy(v_all[l][:, :, b, kb:kb + 4, 0:16].rearrange("p a k w -> p k a w"),
                     bank[:, v_bank(l, c), :].rearrange("p (k a w) -> p k a w", k=4, a=NP)).then_inc(S("v_copied"), 1)

            def norm(ph):
                act.wait_ge(S(f"{ph}_xnTp"), 1)
                copy(xnT[:, :], bank[:, 0, 0:256]).then_inc(S(f"{ph}_xnT"), 1)

            def query(l):
                act.wait_ge(S("q_proj"), l + 1)
                copy(q_f[:, :], bank[:, 1, 0:256], SCALE).then_inc(S("q_f"), 1)
                act.wait_ge(S("q_f"), l + 1)
                copy(q_parts[:, 0, :], q_f[:, :]).then_inc(S("q_high"), 1)

            def cross(l):
                g0 = NN * l

                def put_q(dst):
                    copy(dst[0:64, 0:P], bank[0:64, 6, 0:P])
                    return copy(dst[64:P, P:2 * P], bank[64:P, 6, 0:P])

                def put_qm(n, u):
                    act.wait_ge(S("qm_rows"), n + (g0 + 1))
                    put_q(q_max[u % 2]).then_inc(S("qm_put"), 1)

                def put_qe(n, u):
                    act.wait_ge(S("qe_rows"), n + (g0 + 1))
                    put_q(q_exp[u % 2]).then_inc(S("qe_put"), 1)

                def take_o(n, u):
                    act.wait_ge(S("pv_done"), n * 4 + (C_PV + 4 * g0))
                    copy(o_sb[(u + 1) % 2][:, :], bank[:, 7, 0:256]).then_inc(S("o_taken"), 1)

                def exp_unit(n, j):
                    act.wait_ge(S("b_done"), n * 8 + (8 * g0 + j + 1))
                    if j % 2 == 0:
                        act.wait_ge(S("pv_done"), n * 4 + (C_PV + 4 * g0 + j // 2 - 1))
                    act.activation(probs[:, j % 4, :], bank[:, 4 + j % 2, :], ACT.Exp).then_inc(S("exp_done"), 1)

                def body(n, v, qm=True, qe=True):
                    for j in range(8):
                        exp_unit(n, j)
                        if j == 1:
                            if qm:
                                put_qm(n + 2, v + 2)
                            if v:
                                take_o(n, v)
                        if j == 6 and qe:
                            put_qe(n + 1, v + 1)
                        if l == 0 and isinstance(n, int) and (n, j) in k1_after:
                            prep_k(1, k1_after[n, j])

                k1_after = {(14, 7): 0, (15, 2): 1, (15, 4): 2, (15, 6): 3}
                act.wait_ge(S("q_zero"), 4)
                for n in range(2):
                    put_qm(n, n)
                put_qe(0, 0)
                body(0, 0)
                with act.Fori(0, 3) as i:
                    for v in range(1, U + 1):
                        body(i * U + v, v)
                for n in range(NN - 3, NN):
                    body(n, n - 12, n + 2 < NN, n + 1 < NN)
                take_o(NN, 0)
                act.wait_ge(S("oT_p"), l + 1)
                copy(oT[:, :], bank[:, 0, 0:256]).then_inc(S("oT"), 1)

            def self_attention(l):
                def s_copy(w):
                    act.wait_ge(S("s_done"), 8 * l + w + 1)
                    copy(s_sb[:, w, :], bank[:, 4 + w % 4, :]).then_inc(S("s_copied"), 1)

                def s_exp(w):
                    done = sum(k in SUB_POOL for k in range(w + 1))
                    if w in SUB_POOL:
                        act.wait_ge(S("s_sub_pool"), len(SUB_POOL) * l + done)
                    else:
                        act.wait_ge(S("s_sub"), (8 - len(SUB_POOL)) * l + w + 1 - done)
                    act.activation(s_sb[:, w, :], s_sb[:, w, :], ACT.Exp).then_inc(S("s_exp"), 1)

                def p_copy(w):
                    act.wait_ge(S("p_trans"), 8 * l + w + 1)
                    copy(pT[:, w, :], bank[:, w % 2, :]).then_inc(S("p_copied1"), 1)

                for w in range(8 + 6):
                    if w < 8:
                        s_copy(w)
                    if w == 2:
                        act.wait_ge(S("v_self"), l + 1)
                        act.wait_ge(S("v32_ones"), 1)
                        copy(v32[:, :, :, 0:HD], bank[:, 3, 0:256].rearrange("p (b h d) -> p b h d", b=B, d=HD)) \
                            .then_inc(S("v32"), 1)
                    if 3 <= w < 11:
                        s_exp(w - 3)
                    if w >= 6 and w % 2 == 0:
                        p_copy(w - 5)
                    if w in (10, 13):
                        b = w // 13
                        act.wait_ge(S("pv_self"), 8 * l + 4 * b + 4)
                        copy(o_flat[:, b, :], bank[:, 2 + b, :]).then_inc(S("o_flat"), 1)
                if l:
                    act.wait_ge(S("attT_p"), 1)
                    copy(attT[:, :], bank[:, 3, 0:256]).then_inc(S("attT"), 1)

            act.wait_ge(S("in_R"), 16)
            link(act.activation(gum[:, 0:8], R_("u", 8), ACT.Ln))
            act.activation(gum[:, 8:16], gum[:, 0:8], ACT.Ln, scale=-1.0).then_inc(S("gum_ln"), 1)
            act.wait_ge(S("gum_shift"), 1)
            act.activation(gum[:, 24:32], gum[:, 16:24], ACT.Exp).then_inc(S("gum_exp"), 1)
            act.wait_ge(S("gum_sum"), 1)
            act.activation(gum[:, 33:34], gum[:, 32:33], ACT.Ln).then_inc(S("gum_lse"), 1)
            prep_k(0, 0)
            norm("n0")
            for c in range(1, 4):
                prep_k(0, c)
            query(0)
            for c in range(4, 8):
                prep_k(0, c)
            for c in range(8):
                prep_v(0, c)
            cross(0)
            for c in range(2):
                prep_v(1, c)
            norm("n1")
            self_attention(0)
            for c in range(4, 6):
                prep_k(1, c)
            for c in range(2, 4):
                prep_v(1, c)
            norm("n2")
            for c in range(6, 8):
                prep_k(1, c)
            for c in range(4, 6):
                prep_v(1, c)
            norm("n3")
            query(1)
            for c in range(6, 8):
                prep_v(1, c)
            cross(1)
            norm("n4")
            self_attention(1)
            norm("n5")
            act.wait_ge(S("r_logits"), 1)
            act.activation(r_e[:, :, :], bank[:, 1, 0:2 * E].rearrange("p (b e) -> p b e", b=B),
                           ACT.Exp, scale=-1.0).then_inc(S("r_exp"), 1)
            def tanh(f):
                act.wait_ge(S("f_done"), f + 1)
                act.activation(f_t[:, f, :], bank[:, 3 + f % 4, 0:256], ACT.Tanh, scale=0.5) \
                    .then_inc(S("f_tanh"), 1)

            for f in range(4):
                tanh(f)
            act.wait_ge(S("combT_p"), 1)
            copy(combT[:, :], bank[0:E, 2, 0:256]).then_inc(S("combT"), 1)
            for f in range(4, FB1):
                tanh(f)
                if f - 4 < FB // 2:
                    act.wait_ge(S("rep_done"), f - 3)
                    copy(f_c[:, 2 * f - 8:2 * f - 6, :], bank[:, r_bank(f - 4), :].rearrange("p (i t) -> p i t", i=2)) \
                        .then_inc(S("f_weight"), 1)

        @block.vector
        def _(dve):
            chain = [0]

            def link(ins):
                chain[0] += 1
                ins.then_inc(S("dve_link"), 1)
                dve.wait_ge(S("dve_link"), chain[0])

            V = nc.vector
            for i in range(2):
                V.memset(q_max[i][:, :], 0.0).then_inc(S("q_zero"), 1)
                V.memset(q_exp[i][:, :], 0.0).then_inc(S("q_zero"), 1)
                V.memset(m_rows[i][:, :], 0.0).then_inc(S("m_zero"), 1)
                V.memset(v_all[i][:, :, :, :, VW - 1:VW], 1.0).then_inc(S("v_zero"), 1)
            V.memset(ones_col[:, :], 1.0).then_inc(S("exp_done"), C_EXP)
            V.memset(r_gs[:, :, :], -BIG).then_inc(S("o_div"), C_DIV)
            V.memset(r_top[:, :, :], BIG)
            V.memset(r_top4[:, :, :], BIG).then_inc(S("pv_done"), C_PV)
            dve.wait_ge(S("pv_done"), C_PV)

            def fold(step):
                dve.wait_ge(S(f"fold{step}"), 1)
                if step == 1:
                    V.tensor_copy(w_g[:, :], bank[:, 4, 0:P])
                    V.tensor_copy(w_gT[:, :], bank[:, 4, P:2 * P])
                    V.tensor_copy(v_eff[:, :], bank[0:64, 4, 2 * P:3 * P]).then_inc(S("fold1_c"), 1)
                elif step == 2:
                    V.tensor_copy(wv_eff[:, :], bank[:, 5, 0:P])
                    V.tensor_copy(k_effT[:, :], bank[0:64, 5, P:2 * P]).then_inc(S("fold2_c"), 1)
                else:
                    V.tensor_copy(wk_eff[:, :], bank[:, 4, 0:P]).then_inc(S("fold3_c"), 1)

            def norm(ph, before=None, after=None):
                for b in range(B):
                    last = V.bn_stats(st[:, b, :], x[:, b, :])
                link(last)
                for b in range(B):
                    last = V.bn_aggr(mv[:, b, :], st[:, b, :])
                link(last)
                V.tensor_scalar(ve[:, :], mv[:, :, 1], EPS, None, ALU.add).then_inc(S(f"{ph}_var"), 1)
                if before:
                    before()
                dve.wait_ge(S(f"{ph}_y0"), 1)
                link(V.tensor_tensor(yt[:, :], y0[:, :], y0[:, :], ALU.mult))
                link(V.tensor_tensor(yt[:, :], yt[:, :], ve[:, :], ALU.mult))
                link(V.tensor_scalar(yt[:, :], yt[:, :], -0.5, 1.5, ALU.mult, ALU.add))
                link(V.tensor_tensor(rstd[:, :], yt[:, :], y0[:, :], ALU.mult))
                for b in range(B):
                    V.tensor_scalar(xn[:, b, :], x[:, b, :], mv[:, b, 0:1], rstd[:, b:b + 1],
                                    ALU.subtract, ALU.mult).then_inc(S(f"{ph}_xn"), 1)
                if after:
                    after()

            def prep_k(l, c):
                k = 8 * l + c
                cols = slice(c * 512, (c + 1) * 512)
                dve.wait_ge(S("k_high"), k + 1)
                if k >= 2:
                    dve.wait_ge(S("k_low"), k - 1)
                V.tensor_tensor(k_rest[c % 2][:, :], bank[:, k_bank(l, c), :], kparts[:, 0, cols], ALU.subtract) \
                    .then_inc(S("k_rest1"), 1)
                dve.wait_ge(S("k_rest1"), k + 1)
                V.tensor_copy(kparts[:, 1, cols], k_rest[c % 2][:, :]).then_inc(S("k_mid"), 1)

            def query(l):
                dve.wait_ge(S("q_high"), l + 1)
                link(V.tensor_tensor(q_rest[:, :], q_f[:, :], q_parts[:, 0, :], ALU.subtract))
                link(V.tensor_copy(q_parts[:, 1, :], q_rest[:, :]))
                V.tensor_tensor(q_parts[:, 2, :], q_rest[:, :], q_parts[:, 1, :], ALU.subtract) \
                    .then_inc(S("q_split"), 1)

            def cross(l):
                g0 = NN * l

                def maxima(n, u, w):
                    dve.wait_ge(S("a_done"), n * 4 + (4 * g0 + w + 1))
                    V.tensor_reduce(mx[u % 2][:, w // 2, w % 2:w % 2 + 1],
                                    bank[:, 2 * (w % 2):2 * (w % 2) + 2, :], AX.XY, ALU.max) \
                        .then_inc(S("max_done"), 1)

                def rows(n, u):
                    m3 = m_rows[u % 2][:, :].rearrange("q (a r) -> q a r", a=2)
                    dve.wait_ge(S("max_done"), n * 4 + (4 * g0 + 4))
                    V.tensor_reduce(negm[:, :], mx[u % 2][:, :, :], AX.X, ALU.max, negate=True) \
                        .then_inc(S("neg_done"), 1)
                    dve.wait_ge(S("neg_done"), n + (g0 + 1))
                    V.tensor_copy(m3[:, :, HR], negm[:, :]).then_inc(S("m_high"), 1)
                    dve.wait_ge(S("m_high"), n + (g0 + 1))
                    V.tensor_tensor(m3[:, :, HR + 1], negm[:, :], m3[:, :, HR], ALU.subtract) \
                        .then_inc(S("m_rows"), 1)

                def divide(n, off, b):
                    ps = bank[:, 6, 256:256 + 18].rearrange("p (a c) -> p a c", a=2)
                    dve.wait_ge(S("o_heads"), n + 16 * l)
                    V.reciprocal(o_rec[:, :], ps[:, :, HD]).then_inc(S("o_rec"), 1)
                    dve.wait_ge(S("o_rec"), n + 16 * l)
                    dst = onorm[:, b, bass.ds(off, 16)].rearrange("p (a d) -> p a d", a=2)
                    V.tensor_tensor(dst, ps[:, :, 0:HD], o_rec[:, :].unsqueeze(2).to_broadcast([P, 2, HD]), ALU.mult) \
                        .then_inc(S("o_div"), 1)

                def body(n, v, i):
                    static = isinstance(n, int)
                    if not static or n + 1 < NN:
                        maxima(n + 1, v + 1, 2)
                        maxima(n + 1, v + 1, 3)
                    elif l == 0:
                        prep_k(1, 1)
                        prep_k(1, 2)
                    if v:
                        divide(n, i * 32 + 16 * ((v - 1) // 2), (v - 1) % 2)
                    if not static or n + 1 < NN:
                        rows(n + 1, v + 1)
                    if not static or n + 2 < NN:
                        maxima(n + 2, v, 0)
                        maxima(n + 2, v, 1)
                    elif l == 0:
                        prep_k(1, 0 if n + 1 < NN else 3)

                for w in range(4):
                    maxima(0, 0, w)
                rows(0, 0)
                for w in range(2):
                    maxima(1, 1, w)
                body(0, 0, 0)
                with dve.Fori(0, 3) as i:
                    for v in range(1, U + 1):
                        body(i * U + v, v, i)
                for n in range(NN - 3, NN):
                    body(n, n - 12, 3)
                divide(NN, 16 * (NP - 1), 1)
                if l == 0:
                    fold(1)
                for b in range(B):
                    dve.wait_ge(S("o_out"), 2 * l + b + 1)
                    last = V.tensor_tensor(x[:, b, :], bank[:, 1 + b, 0:P], x[:, b, :], ALU.add)
                link(last)

            def self_attention(l):
                bk, bq = (B_("bk", 1), B_("bq", 1)) if l else (0.0, 0.0)
                for b in range(B):
                    dve.wait_ge(S("q_self"), l + 1)
                    q = bank[:, 1, b * P:(b + 1) * P].unsqueeze(1).to_broadcast([P, 4, P])
                    V.scalar_tensor_tensor(qexp[:, b, :, :], q, bq,
                                           B_("qsel", 4).unsqueeze(2).to_broadcast([P, 4, P]), ALU.add, ALU.mult) \
                        .then_inc(S("qexp"), 1)
                    dve.wait_ge(S("k_self"), l + 1)
                    k = bank[:, 2, b * P:(b + 1) * P].unsqueeze(1).to_broadcast([P, 4, P])
                    V.scalar_tensor_tensor(kexp[:, b, :, :], k, bk,
                                           B_("hsel", 4).unsqueeze(2).to_broadcast([P, 4, P]), ALU.add, ALU.mult) \
                        .then_inc(S("kexp"), 1)

                def s_max(w):
                    dve.wait_ge(S("s_masked"), 8 * l + w + 1)
                    V.tensor_reduce(s_mx[:, w, :], s_sb[:, w, :].rearrange("p (h k) -> p h k", h=4), AX.X, ALU.max) \
                        .then_inc(S("s_max"), 1)

                def s_sub(w):
                    dve.wait_ge(S("s_max"), 8 * l + w + 1)
                    v = s_sb[:, w, :].rearrange("p (h k) -> p h k", h=4)
                    V.tensor_tensor(v, v, s_mx[:, w, :].unsqueeze(2).to_broadcast([P, 4, P]), ALU.subtract) \
                        .then_inc(S("s_sub"), 1)

                def p_copy(w):
                    dve.wait_ge(S("p_trans"), 8 * l + w + 1)
                    V.tensor_copy(pT[:, w, :], bank[:, w % 2, :]).then_inc(S("p_copied0"), 1)

                for w in range(8 + 4):
                    if w < 8:
                        s_max(w)
                        if w not in SUB_POOL:
                            s_sub(w)
                    if w >= 4 and w % 2 == 0:
                        p_copy(w - 4)
                for b in range(B):
                    dve.wait_ge(S("o_back"), 2 * l + b + 1)
                    o = bank[:, 5 + b, :].rearrange("p (h w) -> p h w", w=VP)
                    link(V.reciprocal(s_rec[:, b, :], o[:, :, HD]))
                    V.tensor_tensor(att[:, b, :].rearrange("p (h d) -> p h d", h=H), o[:, :, 0:HD],
                                    s_rec[:, b, :].unsqueeze(2).to_broadcast([P, H, HD]), ALU.mult) \
                        .then_inc(S("att"), 1)
                dve.wait_ge(S("att"), 2 * l + 2)
                if l == 0:
                    link(V.tensor_tensor(x[:, :, :], att[:, :, :], x[:, :, :], ALU.add))
                else:
                    dve.wait_ge(S("att_out"), 1)
                    link(V.tensor_tensor(x[:, :, :], bank[:, 4, 0:256].rearrange("p (b d) -> p b d", b=B), x[:, :, :],
                                         ALU.add))

            dve.wait_ge(S("in_R"), 16)
            link(V.tensor_reduce(gum[:, 34:35], R_("logits", 8), AX.X, ALU.max))
            V.tensor_scalar(gum[:, 16:24], R_("logits", 8), gum[:, 34:35], None, ALU.subtract) \
                .then_inc(S("gum_shift"), 1)
            def gum_sum():
                dve.wait_ge(S("gum_exp"), 1)
                V.tensor_reduce(gum[:, 32:33], gum[:, 24:32], AX.X, ALU.add).then_inc(S("gum_sum"), 1)

            dve.wait_ge(S("in_A"), 16)
            norm("n0", gum_sum)
            for c in range(4):
                prep_k(0, c)
            query(0)
            for c in range(4, 8):
                prep_k(0, c)
            dve.wait_ge(S("gum_lse"), 1)
            link(V.tensor_scalar(gum[:, 36:44], gum[:, 16:24], gum[:, 33:34], None, ALU.subtract))
            dve.wait_ge(S("gum_ln"), 1)
            link(V.tensor_tensor(gum[:, 44:52], gum[:, 36:44], gum[:, 8:16], ALU.subtract))
            link(V.max(gum[:, 52:60], gum[:, 44:52]))
            V.max_index(gidx[:, :], gum[:, 52:60], gum[:, 44:52]).then_inc(S("idx"), 1)
            dve.wait_ge(S("in_mask"), 32)
            mflat = mask_s[:, :, :].rearrange("p b t -> p (b t)")
            V.tensor_scalar(v_scratch(s_sb), mflat, 0.0, None, ALU.not_equal, ALU.add, accum_out=flag_f[:, 0:1]) \
                .then_inc(S("flag_rows"), 1)
            dve.wait_ge(S("flag_sum"), 1)
            V.tensor_copy(flag_i[:, :], bank[0:1, 1, 0:1]).then_inc(S("flag"), 1)
            cross(0)
            norm("n1", lambda: fold(2), lambda: fold(3))
            self_attention(0)
            norm("n2", lambda: prep_k(1, 4), lambda: prep_k(1, 5))
            dve.wait_ge(S("ff_out"), 1)
            link(V.tensor_tensor(x[:, :, :], bank[:, 1, 0:256].rearrange("p (b d) -> p b d", b=B), x[:, :, :], ALU.add))
            norm("n3", lambda: prep_k(1, 6), lambda: prep_k(1, 7))
            query(1)
            cross(1)
            norm("n4")
            self_attention(1)
            norm("n5")
            dve.wait_ge(S("r_exp"), 1)
            link(V.tensor_scalar(r_e[:, :, :], r_e[:, :, :], 1.0, None, ALU.add))
            link(V.reciprocal(r_sc[:, :, :], r_e[:, :, :]))
            link(V.tensor_tensor(r_scb[:, :, :], r_sc[:, :, :],
                                 bank[:, 1, 64:64 + E].unsqueeze(1).to_broadcast([P, B, E]), ALU.add))
            g4 = r_scb[:, :, :].rearrange("p b (g k) -> p (b g) k", k=4)
            V.tensor_tensor(r_six[:, :, 0:3], g4[:, :, 0:3], g4[:, :, 1:4], ALU.add)
            V.tensor_tensor(r_six[:, :, 3:5], g4[:, :, 0:2], g4[:, :, 2:4], ALU.add)
            link(V.tensor_tensor(r_six[:, :, 5:6], g4[:, :, 0:1], g4[:, :, 3:4], ALU.add))
            link(V.tensor_reduce(r_gs[:, :, 0:4], r_six[:, :, :].rearrange("p (b g) s -> p b g s", b=B), AX.X, ALU.max))
            for b in range(B):
                last = V.max(r_v8[:, b, :], r_gs[:, b, :])
            link(last)
            link(V.tensor_copy(r_top[:, :, 0:2], r_v8[:, :, 0:2]))
            for b in range(B):
                last = V.match_replace(r_mr[:, b, :], r_top[:, b, :], r_gs[:, b, :], BIG)
            link(last)
            link(V.tensor_scalar(r_gm[:, :, :], r_mr[:, :, :], BIGHALF, None, ALU.is_ge))
            link(V.tensor_tensor(r_msk[:, :, :].rearrange("p b (g k) -> p b g k", k=4),
                                 r_scb[:, :, :].rearrange("p b (g k) -> p b g k", k=4),
                                 r_gm[:, :, 0:4].unsqueeze(3).to_broadcast([P, B, GROUPS, 4]), ALU.mult))
            link(V.tensor_scalar(r_msk[:, :, :], r_msk[:, :, :], 0.0, None, ALU.add))
            for b in range(B):
                last = V.max(r_v8[:, b, :], r_msk[:, b, :])
            link(last)
            link(V.tensor_copy(r_top4[:, :, 0:4], r_v8[:, :, 0:4]))
            for b in range(B):
                last = V.match_replace(r_mr2[:, b, :], r_top4[:, b, :], r_msk[:, b, :], BIG)
            link(last)
            link(V.tensor_scalar(r_mr2[:, :, :], r_mr2[:, :, :], BIGHALF, None, ALU.is_ge))
            link(V.tensor_tensor(r_mr2[:, :, :], r_mr2[:, :, :], r_sc[:, :, :], ALU.mult))
            link(V.tensor_reduce(r_sum[:, :], r_mr2[:, :, :], AX.X, ALU.add))
            link(V.tensor_scalar(r_sum[:, :], r_sum[:, :], 1e-20, None, ALU.add))
            link(V.reciprocal(r_sum[:, :], r_sum[:, :]))
            link(V.tensor_scalar(r_sum[:, :], r_sum[:, :], ROUTED_SCALE, None, ALU.mult))
            V.tensor_tensor(comb[:, :, :], r_mr2[:, :, :], r_sum[:, :].unsqueeze(2).to_broadcast([P, B, E]),
                            ALU.mult).then_inc(S("comb"), 1)
            for f in range(FB1 + 1):
                if f < FB1:
                    dve.wait_ge(S("f_tanh"), f + 1)
                    if f >= 2:
                        dve.wait_ge(S("f_inner"), f - 1)
                    V.scalar_tensor_tensor(f_a[:, f % 2, :], f_t[:, f, :], 1.0, bank[:, 3 + f % 4, 0:256],
                                           ALU.add, ALU.mult).then_inc(S("f_silu"), 1)
                if f:
                    dve.wait_ge(S("f_silu"), f)
                    V.scalar_tensor_tensor(f_h[:, f - 1, :], f_a[:, (f - 1) % 2, :], 0.5,
                                           bank[:, 3 + (f - 1) % 4, 256:512], ALU.mult, ALU.mult) \
                        .then_inc(S("f_inner"), 1)
            for b in range(B):
                dve.wait_ge(S("down_done"), 1)
                V.tensor_tensor(x[:, b, :], bank[:, b, 0:P], x[:, b, :], ALU.add).then_inc(S("y_ready"), 1)

        @block.tensor
        def _(pe):
            T = nc.tensor

            def mm(out_, lhsT, rhs, start=True, stop=True, **kw):
                return T.matmul(out_, lhsT=lhsT, rhs=rhs, start=start, stop=stop, **kw)

            def prep_k(l, c):
                k = 8 * l + c
                if l == 0:
                    pe.wait_ge(S(f"in_ctx{c // 2}"), 16)
                free = k - 1 if l else k - 3
                if free > 0 and c >= (2 if l else 4):
                    pe.wait_ge(S("k_rest1"), free)
                mm(bank[:, k_bank(l, c), :], WK[l], ctxT_s[:, c * 512:(c + 1) * 512]).then_inc(S("k_proj"), 1)

            def prep_v(l, c):
                k = 8 * l + c
                if c >= 2:
                    pe.wait_ge(S("v_copied"), k - 1)
                for i in range(4):
                    last = mm(bank[:, v_bank(l, c), i * P:(i + 1) * P],
                              ctxT_s[:, c * 512 + i * P:c * 512 + (i + 1) * P], WV[l])
                last.then_inc(S("v_proj"), 1)

            def norm(ph):
                for b in range(B):
                    pe.wait_ge(S(f"{ph}_xn"), b + 1)
                    last = T.transpose(bank[:, 0, b * P:(b + 1) * P], xn[:, b, :], ident)
                last.then_inc(S(f"{ph}_xnTp"), 1)
                pe.wait_ge(S(f"{ph}_xnT"), 1)

            def query(l):
                mm(bank[:, 1, 0:256], WQ[l], xnT[:, :]).then_inc(S("q_proj"), 1)

            def cross(l, masked):
                g0 = NN * l

                def put(p_off, b, done, extra=None):
                    for s in range(PARTS):
                        last = mm(bank[:, 6, 0:P], selq[:, bass.ds(p_off + s * NP * P, P)],
                                  q_parts[:, s, b * P:(b + 1) * P], start=(s == 0),
                                  stop=(s == PARTS - 1 and extra is None))
                    if extra is not None:
                        last = mm(bank[:, 6, 0:P], extra, ident_b[:, :], start=False, stop=True)
                    last.then_inc(S(done), 1)

                def put_max(n, p_off, b):
                    put(p_off, b, "qm_rows")

                def put_exp(n, p_off, u):
                    pe.wait_ge(S("m_rows"), n + (g0 + 1))
                    put(p_off, u % 2, "qe_rows", m_rows[u % 2][:, :])

                def a_unit(n, u, w):
                    if w == 0:
                        pe.wait_ge(S("qm_put"), n + (g0 + 1))
                        pe.wait_ge(S(f"k_loaded{u % U}"), (n - u % U) * 24 + 96 * (g0 // U + 1))
                    if not (isinstance(n, int) and 4 * (n + g0) + w - 1 <= 0):
                        pe.wait_ge(S("max_done"), n * 4 + (4 * g0 + w - 1))
                    for h in range(2):
                        keys = slice((w % 2) * 1024 + h * 512, (w % 2) * 1024 + (h + 1) * 512)
                        o = bank[:, 2 * (w % 2) + h, :]
                        a = w // 2
                        last = mm(o, q_max[u % 2][:, a * P:(a + 1) * P], kpair[u % U][:, keys], stop=not masked)
                        if masked:
                            last = mm(o, ident, mask_s[:, u % 2, keys], start=False)
                    last.then_inc(S("a_done"), 1)

                def b_unit(n, u, j):
                    if j == 0:
                        pe.wait_ge(S("qe_put"), n + (g0 + 1))
                    pe.wait_ge(S("exp_done"), n * 8 + (C_EXP + 8 * g0 + j - 1))
                    for i in range(2):
                        c = 2 * j + i
                        o = bank[:, 4 + j % 2, i * 256:(i + 1) * 256]
                        last = mm(o, kpair[u % U][:, c * P:(c + 1) * P], q_exp[u % 2][:, :], stop=not masked)
                        if masked:
                            last = mm(o, mask_s[:, u % 2, c * P:(c + 1) * P],
                                      two_ident[:, :, :].rearrange("p a q -> p (a q)"), start=False)
                    last.then_inc(S("b_done"), 1)

                def pv_group(n, u, k):
                    if k == 0:
                        pe.wait_ge(S("v_pair"), n + (g0 + 1))
                        if not (isinstance(n, int) and n + l == 0):
                            pe.wait_ge(S("o_taken"), n + 16 * l)
                    pe.wait_ge(S("exp_done"), n * 8 + (C_EXP + 8 * g0 + 2 * k + 2))
                    for t in range(4):
                        c = 4 * k + t
                        last = mm(bank[t * 32:(t + 1) * 32, 7, 0:256], vpair[u % 2][:, c, :],
                                  probs[:, (c // 2) % 4, (c % 2) * 256:(c % 2 + 1) * 256],
                                  start=(k == 0), stop=(k == KB // 4 - 1))
                    last.then_inc(S("pv_done"), 1)

                def heads(n, u):
                    pe.wait_ge(S("o_taken"), n + 16 * l)
                    pe.wait_ge(S("o_div"), n + (16 * l + C_DIV - 1))
                    for a in range(2):
                        last = mm(bank[:, 6, 256 + 9 * a:256 + 9 * (a + 1)], o_sb[(u + 1) % 2][:, a * P:(a + 1) * P],
                                  sel_o[:, a, :])
                    last.then_inc(S("o_heads"), 1)

                def p_of(i, k):
                    return i * (2 * P) + (k // 2) * P

                def body(n, v, i, a1=True, a2=True):
                    for k in range(4):
                        b_unit(n, v, 2 * k)
                        b_unit(n, v, 2 * k + 1)
                        if k == 3 and a1:
                            pe.wait_ge(S("o_div"), n + (16 * l + C_DIV))
                            put_exp(n + 1, p_of(i, v + 1), v + 1)
                        if k < 2 and a1:
                            a_unit(n + 1, v + 1, 2 + k)
                        if k >= 2 and a2:
                            a_unit(n + 2, v + 2, k - 2)
                        if l == 0 and (a1, a2, k) in k1_at:
                            if a1:
                                pe.wait_ge(S("max_done"), 4 * NN)
                            prep_k(1, k1_at[a1, a2, k])
                        if k == 0 and a2:
                            put_max(n + 2, p_of(i, v + 2), v % 2)
                        if k:
                            pv_group(n, v, k - 1)
                        elif v:
                            pv_group(n - 1, v - 1, 3)
                        if k == 1 and v:
                            heads(n, v)

                k1_at = {(True, False, 3): 0, (False, False, 0): 1, (False, False, 1): 2, (False, False, 2): 3}
                put_max(0, p_of(0, 0), 0)
                pe.wait_ge(S("qm_put"), g0 + 1)
                put_max(1, p_of(0, 1), 1)
                for w in range(4):
                    a_unit(0, 0, w)
                for w in range(2):
                    a_unit(1, 1, w)
                pe.wait_ge(S("qm_put"), g0 + 2)
                put_exp(0, p_of(0, 0), 0)
                body(0, 0, 0)
                if l == 0:
                    pe.wait_ge(S("in_B"), 16)
                with pe.Fori(0, 3) as i:
                    for v in range(1, U + 1):
                        body(i * U + v, v, i)
                for n in range(NN - 3, NN):
                    body(n, n - 12, 3, n + 1 < NN, n + 2 < NN)
                pv_group(NN - 1, 1, 3)
                heads(NN, 0)

            def cross_out(l):
                pe.wait_ge(S("o_div"), 16 * (l + 1) + C_DIV)
                pe.wait_ge(S("max_done"), 4 * NN * (l + 1))
                if l == 0:
                    pe.wait_ge(S("k_rest1"), 8 + 3)
                for b in range(B):
                    last = T.transpose(bank[:, 0, b * P:(b + 1) * P], onorm[:, b, :], ident)
                last.then_inc(S("oT_p"), 1)
                if l == 0:
                    pe.wait_ge(S("in_B"), 16)
                    pe.wait_ge(S("in_C"), 16)
                    mm(bank[:, 4, 0:P], C_("w_dq"), C_("w_uqT"))
                    mm(bank[:, 4, P:2 * P], C_("w_uqT"), C_("w_dq"))
                    mm(bank[0:64, 4, 2 * P:3 * P], B_("w_uv", 64), B_("w_oT")).then_inc(S("fold1"), 1)
                pe.wait_ge(S("oT"), l + 1)
                for b in range(B):
                    last = mm(bank[:, 1 + b, 0:P], oT[:, b * P:(b + 1) * P], WO[l], stop=(l == 0))
                    if l:
                        last = mm(bank[:, 1 + b, 0:P], ones_row, R_("bo1"), start=False)
                    last.then_inc(S("o_out"), 1)
                if l == 0:
                    pe.wait_ge(S("fold1_c"), 1)
                    mm(bank[:, 5, 0:P], C_("w_dkv"), v_eff[:, :])
                    mm(bank[0:64, 5, P:2 * P], B_("w_uk", 64), w_gT[:, :]).then_inc(S("fold2"), 1)

            def self_attention(l):
                wq, wk, wv = (B_("aq"), B_("ak"), B_("av")) if l else (w_g[:, :], wk_eff[:, :], wv_eff[:, :])
                mm(bank[:, 1, 0:256], wq, xnT[:, :]).then_inc(S("q_self"), 1)
                if l == 0:
                    pe.wait_ge(S("fold3_c"), 1)
                mm(bank[:, 2, 0:256], wk, xnT[:, :]).then_inc(S("k_self"), 1)
                if l == 0:
                    pe.wait_ge(S("v_copied"), 10)

                def scores(w):
                    b, g = w // 4, w % 4
                    pe.wait_ge(S("qexp"), 2 * l + b + 1)
                    pe.wait_ge(S("kexp"), 2 * l + b + 1)
                    if w >= 4:
                        pe.wait_ge(S("s_copied"), 8 * l + w - 3)
                    mm(bank[:, 4 + w % 4, :], qexp[:, b, g, :],
                       kexp[:, b, :, :].rearrange("p j k -> p (j k)")).then_inc(S("s_done"), 1)

                def transposes(w):
                    pe.wait_ge(S("s_exp"), 8 * l + w + 1)
                    if w >= 2:
                        pe.wait_ge(S(f"p_copied{w % 2}"), 4 * l + w // 2)
                    for h in range(4):
                        last = T.transpose(bank[:, w % 2, h * P:(h + 1) * P], s_sb[:, w, h * P:(h + 1) * P], ident)
                    last.then_inc(S("p_trans"), 1)

                def values(w):
                    b, g = w // 4, w % 4
                    pe.wait_ge(S(f"p_copied{w % 2}"), 4 * l + w // 2 + 1)
                    for t in range(4):
                        last = mm(bank[t * 32:(t + 1) * 32, 2 + b, g * P:(g + 1) * P], v32[:, b, 4 * g + t, :],
                                  pT[:, w, t * P:(t + 1) * P])
                    last.then_inc(S("pv_self"), 1)

                def back(b):
                    pe.wait_ge(S("o_flat"), 2 * l + b + 1)
                    for g in range(4):
                        last = T.transpose(bank[:, 5 + b, g * P:(g + 1) * P], o_flat[:, b, g * P:(g + 1) * P], ident)
                    last.then_inc(S("o_back"), 1)

                for w in range(8 + 6):
                    if w < 8:
                        scores(w)
                    if w == 2:
                        if l == 0:
                            pe.wait_ge(S("k_rest1"), 8 + 4)
                        for b in range(B):
                            last = mm(bank[:, 3, b * P:(b + 1) * P], xnT[:, b * P:(b + 1) * P], wv, stop=(l == 0))
                            if l:
                                last = mm(bank[:, 3, b * P:(b + 1) * P], ones_row, R_("bv"), start=False)
                        last.then_inc(S("v_self"), 1)
                    if 4 <= w < 12:
                        transposes(w - 4)
                    if w >= 6:
                        if w == 6:
                            pe.wait_ge(S("v32"), l + 1)
                        values(w - 6)
                back(0)
                back(1)
                if l:
                    pe.wait_ge(S("att"), 4)
                    for b in range(B):
                        last = T.transpose(bank[:, 3, b * P:(b + 1) * P], att[:, b, :], ident)
                    last.then_inc(S("attT_p"), 1)
                    pe.wait_ge(S("attT"), 1)
                    for b in range(B):
                        mm(bank[:, 4, b * P:(b + 1) * P], attT[:, b * P:(b + 1) * P], B_("aoT"), stop=False)
                        last = mm(bank[:, 4, b * P:(b + 1) * P], ones_row, R_("bout"), start=False)
                    last.then_inc(S("att_out"), 1)

            pe.wait_ge(S("in_A"), 16)
            for c in range(2):
                prep_k(0, c)
            norm("n0")
            for c in range(2, 4):
                prep_k(0, c)
            query(0)
            for c in range(4, 8):
                prep_k(0, c)
            for c in range(8):
                prep_v(0, c)
            pe.wait_ge(S("q_f"), 1)
            pe.wait_ge(S("flag_rows"), 1)
            mm(bank[0:1, 1, 0:1], flag_f[:, 0:1], ones_col[:, :]).then_inc(S("flag_sum"), 1)
            pe.wait_ge(S("flag"), 1)
            pe.wait_ge(S("q_split"), 1)
            pe.wait_ge(S("in_selq"), 16)
            pe.wait_ge(S("m_zero"), 2)
            pe.wait_ge(S("v_copied"), 8)
            pe.wait_ge(S("idents"), 1)
            entries = pe.value_load(flag_i[0:1, 0:1], min_val=0, max_val=P * B * SK)
            with pe.If(entries > 0):
                cross(0, True)
            with pe.Else():
                cross(0, False)
            cross_out(0)
            for c in range(2):
                prep_v(1, c)
            pe.wait_ge(S("fold2_c"), 1)
            mm(bank[:, 4, 0:P], C_("w_dkv"), k_effT[:, :]).then_inc(S("fold3"), 1)
            norm("n1")
            self_attention(0)
            for c in range(4, 6):
                prep_k(1, c)
            prep_v(1, 2)
            pe.wait_ge(S("att"), 2)
            prep_v(1, 3)
            norm("n2")
            pe.wait_ge(S("in_sel"), 32)
            for b in range(B):
                mm(bank[:, 1, b * P:(b + 1) * P], xnT[:, b * P:(b + 1) * P], wsel[:, :], stop=False)
                last = mm(bank[:, 1, b * P:(b + 1) * P], ones_row, bsel[:, :], start=False)
            last.then_inc(S("ff_out"), 1)
            for c in range(6, 8):
                prep_k(1, c)
            for c in range(4, 6):
                prep_v(1, c)
            norm("n3")
            query(1)
            for c in range(6, 8):
                prep_v(1, c)
            pe.wait_ge(S("q_split"), 2)
            pe.wait_ge(S("v_copied"), 16)
            cross(1, False)
            cross_out(1)
            norm("n4")
            self_attention(1)
            norm("n5")
            for b in range(B):
                mm(bank[:, 1, b * E:(b + 1) * E], xnT[:, b * P:(b + 1) * P], B_("router", E))
            mm(bank[:, 1, 64:64 + E], ones_row, R_("ebias", E)).then_inc(S("r_logits"), 1)
            pe.wait_ge(S("in_M"), 32)

            def inner(f):
                if f >= 4:
                    pe.wait_ge(S("f_inner"), f - 3)
                o = bank[:, 3 + f % 4, :]
                for k, c in (("gate", 0), ("up", 256)):
                    w = wM[:, PK_M[k] + f * P:PK_M[k] + (f + 1) * P]
                    last = mm(o[:, c:c + 256], w, xnT[:, :])
                last.then_inc(S("f_done"), 1)

            def weights(k):
                if k >= 2:
                    pe.wait_ge(S("f_weight"), k - 1)
                for i in range(2):
                    last = mm(bank[:, r_bank(k), i * 256:(i + 1) * 256],
                              rep[:, (2 * k + i) * P:(2 * k + i + 1) * P], combT[:, :])
                last.then_inc(S("rep_done"), 1)

            def down(f, first, final):
                pe.wait_ge(S("f_scaled"), f + 1) if f < FB else pe.wait_ge(S("f_inner"), FB1)
                for b in range(B):
                    last = mm(bank[:, b, 0:P], f_h[:, f, b * P:(b + 1) * P],
                              wM[:, PK_M["down"] + f * P:PK_M["down"] + (f + 1) * P], start=first, stop=final)
                return last

            for f in range(4):
                inner(f)
            pe.wait_ge(S("comb"), 1)
            for b in range(B):
                last = T.transpose(bank[0:E, 2, b * P:(b + 1) * P], comb[:, b, :], ident)
            last.then_inc(S("combT_p"), 1)
            pe.wait_ge(S("combT"), 1)
            for f in range(4, FB1):
                inner(f)
                if f - 4 < FB // 2:
                    weights(f - 4)
                if f >= 6:
                    down(f - 6, f == 6, False)
            for f in range(3, FB):
                down(f, False, False)
            last = down(FB, False, True)
            last.then_inc(S("down_done"), 1)


def v_scratch(t):
    return t[:, :, :].rearrange("p w n -> p (w n)")


def constants():
    one = np.uint16(0x3F80)
    selq = np.zeros((P, PARTS, NP, P), np.uint16)
    for h in range(H):
        for s, (_, qp) in enumerate(SLOTS):
            for d in range(HD):
                selq[h * HD + d, qp, h // 2, (h % 2) * HOFF + s * HD + d] = one
    sel_o = np.zeros((P, 2, 9), np.float32)
    for t in range(4):
        for a in range(2):
            for d in range(HD):
                sel_o[t * 32 + a * HD + d, a, d] = 1.0
            sel_o[t * 32 + 2 * HD, a, HD] = 1.0
    hsel = np.zeros((P, 4), np.float32)
    qsel = np.zeros((P, 4), np.float32)
    for h in range(H):
        hsel[h * HD:(h + 1) * HD, h % 4] = 1.0
        qsel[h * HD:(h + 1) * HD, h // 4] = SCALE
    rep = np.zeros((E, FB * P), np.float32)
    for e in range(E):
        rep[e, e * 64:(e + 1) * 64] = 1.0
    return selq.reshape(P, PARTS * NP * P), sel_o.reshape(P, 18), hsel, qsel, rep


def kernel(**inp):
    import concourse.bacc as bacc
    from concourse.bass_utils import run_bass_kernel_spmd

    f = {k: np.ascontiguousarray(v) for k, v in inp.items()}
    selq, sel_o, hsel, qsel, rep = constants()
    x = f["x"]
    ident = np.eye(P, dtype=np.float32)
    packA = np.concatenate([x[0], x[1], f["L0_xattn_wq"].reshape(P, P), f["L0_xattn_wk"].reshape(P, P),
                            f["L0_xattn_wv"].reshape(P, P), f["L0_xattn_wo"].reshape(P, P), ident], axis=1)
    aw = f["L1_attn_attn_w"].reshape(H, 3, HD, P)
    ab = f["L1_attn_attn_b"].reshape(H, 3, HD)
    aq, ak, av = (aw[:, i].reshape(P, P).T for i in range(3))
    bq, bk, bv = (ab[:, i].reshape(P) for i in range(3))
    packB = np.concatenate([f["L1_xattn_Wk"].T, f["L1_xattn_Wv"].T, f["L1_xattn_Wq"].T, f["L1_xattn_Wo"].T,
                            f["L0_attn_W_o"].T, f["L0_attn_W_uv"], f["L0_attn_W_uk"], aq, ak, av,
                            f["L1_attn_out_w"].T, f["L1_ffn_router_weight"].T, hsel, qsel, sel_o,
                            bq[:, None], bk[:, None]], axis=1)
    packC = np.concatenate([f["L0_attn_W_dq"], f["L0_attn_W_uq"].T, f["L0_attn_W_dkv"]], axis=1)
    packR = np.concatenate([f["L0_ffn_u"], f["L0_ffn_logits"], f["L1_xattn_bo"], bv, f["L1_attn_out_b"],
                            f["L1_ffn_e_bias"], np.ones(P, np.float32)])[None, :]
    down = np.concatenate([f["L1_ffn_down_w"].transpose(0, 2, 1).reshape(E * 64, P), f["L1_ffn_sh_down_w"].T], axis=0)
    packM = np.concatenate([f["L1_ffn_gate_w"].reshape(E * 64, P).T, f["L1_ffn_sh_gate_w"].T,
                            f["L1_ffn_up_w"].reshape(E * 64, P).T, f["L1_ffn_sh_up_w"].T,
                            down.reshape(FB1, P, P).transpose(1, 0, 2).reshape(P, FB1 * P)], axis=1)
    ctxT = f["ctx_1024"].reshape(B * SK, P).T
    ins = dict(packA=packA, packB=packB, packC=packC, packR=packR, packM=packM, ffnW=f["L0_ffn_W"], ffnb=f["L0_ffn_b"],
               mask=f["mask_Bx1xSxS2_ff0"], ctxT=ctxT, selq_d=selq, rep_d=rep)
    nc = bacc.Bacc("TRN2", target_bir_lowering=False, num_devices=1)
    arrays, args = {}, []
    for name, a in ins.items():
        a = np.ascontiguousarray(a)
        arrays["in_" + name] = a
        args.append(nc.dram_tensor("in_" + name, a.shape, mybir.dt.from_np(a.dtype), kind="ExternalInput").ap())
    out = nc.dram_tensor("out_0", (B, P, P), F32, kind="ExternalOutput").ap()
    perceiver_kernel(nc, *args, out)
    r = run_bass_kernel_spmd(nc, [arrays], core_ids=[0])
    return r.results[0]["out_0"]
```
